# Optimizing a Trainium2 kernel written in Bass

```python
import numpy as np
import jax
import jax.numpy as jnp

def _softmax(x, axis=-1):
    return jax.nn.softmax(x, axis=axis)

def _gelu(x):
    return jax.nn.gelu(x, approximate=True)

def _silu(x):
    return jax.nn.silu(x)

def _sigmoid(x):
    return jax.nn.sigmoid(x)

def _layernorm(x, axis=-1, eps=1e-05):
    m = jnp.mean(x, axis=axis, keepdims=True)
    v = jnp.var(x, axis=axis, keepdims=True)
    return (x - m) / jnp.sqrt(v + eps)

def _scatter_add(tgt, idx, src, axis=0):
    return tgt.at[idx].add(src)

def _segment_sum(src, seg, n):
    return jax.ops.segment_sum(src, seg, n)
kernel_name = 'mk_decoder_postln_d2_seqx_r4_e63bc5'

def setup_inputs(seed: int=0):
    np.random.seed(seed)
    _w = jnp.asarray

    def _rec_inputs():
        import jax
        import jax.numpy as jnp
        _rk = jax.random.key(seed)
        x = -0.000125 + 0.9999 * jax.random.normal(jax.random.fold_in(_rk, 1), (16, 128, 512), jnp.float32)
        _lenS = 128 - jax.random.randint(jax.random.fold_in(_rk, 7), (16,), 0, max(1, 128 // 4) + 1, jnp.int32)
        _lenS2 = 128 - jax.random.randint(jax.random.fold_in(_rk, 8), (16,), 0, max(1, 128 // 4) + 1, jnp.int32)
        _ctx_2048P = jax.random.normal(jax.random.fold_in(_rk, 11), (16, 16, 512), jnp.float32)
        _ctx_2048c = jax.random.dirichlet(jax.random.fold_in(_rk, 511), 0.3 * jnp.ones((16,), jnp.float32), (16, 128))
        _ctx_2048t = jnp.einsum('bsk,bkd->bsd', _ctx_2048c, _ctx_2048P)
        _ctx_2048t = _ctx_2048t * jax.lax.rsqrt(jnp.mean(jnp.square(_ctx_2048t)) + 1e-12) * 0.953939
        ctx_2048 = -1.52775e-05 + 0.999936 * (_ctx_2048t + 0.3 * jax.random.normal(jax.random.fold_in(_rk, 611), (16, 128, 512), jnp.float32))
        return (x, ctx_2048)
    x, ctx_2048 = _rec_inputs()

    def _L0_attn_setup():
        import jax, jax.numpy as jnp
        import numpy as np
        DIM = 512
        HEAD_DIM = 128
        NUM_HEADS = 16
        BATCH = 2
        SEQ = 512
        key = jax.random.key(seed)
        k1, k2, k3 = jax.random.split(key, 3)
        qkv_out = (NUM_HEADS + 2 * NUM_HEADS) * HEAD_DIM
        x = jax.random.normal(k1, (BATCH, SEQ, DIM), dtype=jnp.float32)
        w_qkv = jax.random.normal(k2, (qkv_out, DIM), dtype=jnp.float32) * (1.0 / np.sqrt(DIM))
        w_out = jax.random.normal(k3, (DIM, NUM_HEADS * HEAD_DIM), dtype=jnp.float32) * (1.0 / np.sqrt(NUM_HEADS * HEAD_DIM))
        return {'x': x, 'w_qkv': w_qkv, 'w_out': w_out}
    _L0_attn_all = _L0_attn_setup()
    _L0_attn_in = {k: v for k, v in _L0_attn_all.items() if k in ('w_qkv', 'w_out')}
    del _L0_attn_all

    def _L0_xattn_setup():
        import jax, jax.numpy as jnp
        import numpy as np
        EPS = 1e-06
        NUM_HEADS = 16

        def _feature_map(x):
            return jnp.where(x > 0, x + 1.0, jnp.exp(x))
        key = jax.random.key(seed)
        ks = jax.random.split(key, 7)
        B, L, S, D = (4, 1024, 1024, 512)
        sc = 1.0 / np.sqrt(D)
        return {'query': jax.random.normal(ks[0], (B, L, D), jnp.float32), 'kv': jax.random.normal(ks[1], (B, S, D), jnp.float32), 'Wq': jax.random.normal(ks[2], (D, D), jnp.float32) * sc, 'Wg': jax.random.normal(ks[3], (D, D), jnp.float32) * sc, 'bg': jnp.ones((D,), jnp.float32), 'Wkv': jax.random.normal(ks[4], (2 * D, D), jnp.float32) * sc, 'Wo': jax.random.normal(ks[5], (D, D), jnp.float32) * sc}
    _L0_xattn_all = _L0_xattn_setup()
    _L0_xattn_in = {k: v for k, v in _L0_xattn_all.items() if k in ('Wq', 'Wg', 'bg', 'Wkv', 'Wo')}
    del _L0_xattn_all

    def _L0_ffn_setup():
        import jax, jax.numpy as jnp
        import numpy as np
        N_BLOCKS = 16
        BLOCK_SIZE = 128
        TOP_K = N_BLOCKS // 4
        key = jax.random.key(seed)
        k1, k2, k3, k4, k5 = jax.random.split(key, 5)
        in_f, out_f = (512, 2048)
        x = jax.random.normal(k1, (2, 1024, in_f), dtype=jnp.float32)
        Wr = jax.random.normal(k2, (N_BLOCKS, in_f), dtype=jnp.float32) * in_f ** (-0.5)
        br = jnp.zeros((N_BLOCKS,), dtype=jnp.float32)
        W1 = jax.random.normal(k3, (out_f, in_f), dtype=jnp.float32) * in_f ** (-0.5)
        W2 = jax.random.normal(k4, (in_f, out_f), dtype=jnp.float32) * out_f ** (-0.5)
        return {'x': x, 'Wr': Wr, 'br': br, 'W1': W1, 'W2': W2}
    _L0_ffn_all = _L0_ffn_setup()
    _L0_ffn_in = {k: v for k, v in _L0_ffn_all.items() if k in ('Wr', 'br', 'W1', 'W2')}
    del _L0_ffn_all

    def _L1_attn_setup():
        import jax, jax.numpy as jnp
        import numpy as np
        B, T, HID = (1, 512, 512)
        H = 16
        D = HID // H
        EPS = 1e-05

        def _layer_norm(x, eps=1e-05):
            mu = jnp.mean(x, axis=-1, keepdims=True)
            var = jnp.mean((x - mu) ** 2, axis=-1, keepdims=True)
            return (x - mu) * jax.lax.rsqrt(var + eps)

        def _feature_map(x, gamma, beta):
            return _layer_norm(x * gamma + beta)
        key = jax.random.key(seed)
        ks = jax.random.split(key, 8)
        s = HID ** (-0.5)
        return {'hidden_states': jax.random.normal(ks[0], (B, T, HID), jnp.float32), 'Wq': jax.random.normal(ks[1], (HID, HID), jnp.float32) * s, 'Wk': jax.random.normal(ks[2], (HID, HID), jnp.float32) * s, 'Wv': jax.random.normal(ks[3], (HID, HID), jnp.float32) * s, 'Wo': jax.random.normal(ks[4], (HID, HID), jnp.float32) * s, 'gamma': 1.0 + 0.1 * jax.random.normal(ks[5], (D,), jnp.float32), 'beta': 0.1 * jax.random.normal(ks[6], (D,), jnp.float32)}
    _L1_attn_all = _L1_attn_setup()
    _L1_attn_in = {k: v for k, v in _L1_attn_all.items() if k in ('Wq', 'Wk', 'Wv', 'Wo', 'gamma', 'beta')}
    del _L1_attn_all

    def _L1_xattn_setup():
        import jax, jax.numpy as jnp
        import numpy as np
        B_DIM, T_DIM, C_DIM = (16, 256, 512)

        def _wkv(w, u, k, v):
            Bn, Tn, Cn = k.shape
            NEG_INF = jnp.float32(-1e+38)

            def step(carry, kv_t):
                p, q, o = carry
                kt, vt = kv_t
                no = jnp.maximum(o, u + kt)
                A = jnp.exp(o - no)
                E = jnp.exp(u + kt - no)
                y = (A * p + E * vt) / (A * q + E)
                no2 = jnp.maximum(w + o, kt)
                A2 = jnp.exp(w + o - no2)
                E2 = jnp.exp(kt - no2)
                return ((A2 * p + E2 * vt, A2 * q + E2, no2), y)
            init = (jnp.zeros((Bn, Cn), k.dtype), jnp.zeros((Bn, Cn), k.dtype), jnp.full((Bn, Cn), NEG_INF, k.dtype))
            kT = jnp.moveaxis(k, 1, 0)
            vT = jnp.moveaxis(v, 1, 0)
            _, yT = jax.lax.scan(step, init, (kT, vT))
            return jnp.moveaxis(yT, 0, 1)
        key = jax.random.key(seed)
        k1, k2, k3, k4 = jax.random.split(key, 4)
        w = -jnp.exp(jax.random.normal(k1, (C_DIM,), jnp.float32))
        u = jax.random.normal(k2, (C_DIM,), jnp.float32)
        k = jax.random.normal(k3, (B_DIM, T_DIM, C_DIM), jnp.float32)
        v = jax.random.normal(k4, (B_DIM, T_DIM, C_DIM), jnp.float32)
        return {'B': B_DIM, 'T': T_DIM, 'C': C_DIM, 'w': w, 'u': u, 'k': k, 'v': v}
    _L1_xattn_all = _L1_xattn_setup()
    _L1_xattn_in = {k: v for k, v in _L1_xattn_all.items() if k in ('w', 'u')}
    del _L1_xattn_all

    def _L1_ffn_setup():
        import jax, jax.numpy as jnp
        import numpy as np
        EPS = 1e-08

        def rms_norm(x, eps=EPS):
            mean = jnp.mean(x, axis=-1, keepdims=True)
            var = jnp.var(x, axis=-1, keepdims=True)
            return (x - mean) / jnp.sqrt(var + eps)

        def activation_quant(x):
            s = 127.0 / jnp.max(jnp.abs(x), axis=-1, keepdims=True)
            return jnp.clip(jnp.round(s * x), -128, 127) / s

        def ternary_matmul(x, w):
            return jnp.matmul(x, jnp.sign(w).T)
        key = jax.random.key(seed)
        k0, k1, k2, k3 = jax.random.split(key, 4)
        B, S, D, H = (4, 512, 512, 2048)
        x = jax.random.normal(k0, (B, S, D), dtype=jnp.float32)
        W_g = jax.random.normal(k1, (H, D), dtype=jnp.float32) * 0.01
        W_u = jax.random.normal(k2, (H, D), dtype=jnp.float32) * 0.01
        W_d = jax.random.normal(k3, (D, H), dtype=jnp.float32) * 0.01
        return {'x': x, 'W_g': W_g, 'W_u': W_u, 'W_d': W_d}
    _L1_ffn_all = _L1_ffn_setup()
    _L1_ffn_in = {k: v for k, v in _L1_ffn_all.items() if k in ('W_g', 'W_u', 'W_d')}
    del _L1_ffn_all
    return {'x': x, 'ctx_2048': ctx_2048, 'L0_attn_w_qkv': _L0_attn_in['w_qkv'], 'L0_attn_w_out': _L0_attn_in['w_out'], 'L0_xattn_Wq': _L0_xattn_in['Wq'], 'L0_xattn_Wg': _L0_xattn_in['Wg'], 'L0_xattn_bg': _L0_xattn_in['bg'], 'L0_xattn_Wkv': _L0_xattn_in['Wkv'], 'L0_xattn_Wo': _L0_xattn_in['Wo'], 'L0_ffn_Wr': _L0_ffn_in['Wr'], 'L0_ffn_br': _L0_ffn_in['br'], 'L0_ffn_W1': _L0_ffn_in['W1'], 'L0_ffn_W2': _L0_ffn_in['W2'], 'L1_attn_Wq': _L1_attn_in['Wq'], 'L1_attn_Wk': _L1_attn_in['Wk'], 'L1_attn_Wv': _L1_attn_in['Wv'], 'L1_attn_Wo': _L1_attn_in['Wo'], 'L1_attn_gamma': _L1_attn_in['gamma'], 'L1_attn_beta': _L1_attn_in['beta'], 'L1_xattn_w': _L1_xattn_in['w'], 'L1_xattn_u': _L1_xattn_in['u'], 'L1_ffn_W_g': _L1_ffn_in['W_g'], 'L1_ffn_W_u': _L1_ffn_in['W_u'], 'L1_ffn_W_d': _L1_ffn_in['W_d']}

def reference(x, ctx_2048, L0_attn_w_qkv, L0_attn_w_out, L0_xattn_Wq, L0_xattn_Wg, L0_xattn_bg, L0_xattn_Wkv, L0_xattn_Wo, L0_ffn_Wr, L0_ffn_br, L0_ffn_W1, L0_ffn_W2, L1_attn_Wq, L1_attn_Wk, L1_attn_Wv, L1_attn_Wo, L1_attn_gamma, L1_attn_beta, L1_xattn_w, L1_xattn_u, L1_ffn_W_g, L1_ffn_W_u, L1_ffn_W_d):
    import jax
    import jax.numpy as jnp

    def _L0_attn_ref(x, w_qkv, w_out):
        import jax, jax.numpy as jnp
        import numpy as np
        DIM = 512
        HEAD_DIM = 128
        NUM_HEADS = 16
        BATCH = 2
        SEQ = 512
        B, S, _ = x.shape
        H, D = (NUM_HEADS, HEAD_DIM)
        qkv = (x @ w_qkv.T).reshape(B, S, 3 * H, D)
        q = qkv[:, :, :H]
        k = qkv[:, :, H:2 * H]
        v = qkv[:, :, 2 * H:]
        scale = 1.0 / jnp.sqrt(jnp.asarray(D, dtype=x.dtype))
        logits = jnp.einsum('bqhd,bkhd->bhqk', q, k) * scale
        weights = jax.nn.softmax(logits.astype(jnp.float32), axis=-1).astype(logits.dtype)
        combined = jnp.einsum('bhqk,bkhd->bqhd', weights, v).reshape(B, S, H * D)
        return combined @ w_out.T

    def _L0_xattn_ref(query, kv, Wq, Wg, bg, Wkv, Wo):
        import jax, jax.numpy as jnp
        import numpy as np
        EPS = 1e-06
        NUM_HEADS = 16

        def _feature_map(x):
            return jnp.where(x > 0, x + 1.0, jnp.exp(x))
        B, L, D = query.shape
        S = kv.shape[1]
        H = NUM_HEADS
        hd = D // H
        q = query @ Wq.T
        gate = jax.nn.sigmoid(query @ Wg.T + bg)
        kvp = kv @ Wkv.T
        k, v = jnp.split(kvp, 2, axis=-1)
        q = _feature_map(q.reshape(B, L, H, hd).transpose(0, 2, 1, 3))
        k = _feature_map(k.reshape(B, S, H, hd).transpose(0, 2, 1, 3))
        v = v.reshape(B, S, H, hd).transpose(0, 2, 1, 3)
        kv_summary = jnp.einsum('bhsd,bhse->bhde', k, v)
        k_sum = k.sum(axis=-2)
        z = 1.0 / (jnp.einsum('bhld,bhd->bhl', q, k_sum)[..., None] + EPS)
        attn = jnp.einsum('bhld,bhde->bhle', q, kv_summary) * z
        attn = attn.transpose(0, 2, 1, 3).reshape(B, L, D)
        out = attn * gate @ Wo.T
        return out

    def _L0_ffn_ref(x, Wr, br, W1, W2):
        import jax, jax.numpy as jnp
        import numpy as np
        N_BLOCKS = 16
        BLOCK_SIZE = 128
        TOP_K = N_BLOCKS // 4
        x_shape = x.shape
        in_f = x_shape[-1]
        xf = x.reshape(-1, in_f)
        n = xf.shape[0]
        prob = jax.nn.softmax(xf @ Wr.T + br, axis=-1)
        _, idx = jax.lax.top_k(prob, TOP_K)
        mask = jnp.zeros((n, N_BLOCKS), dtype=xf.dtype)
        mask = mask.at[jnp.arange(n)[:, None], idx].set(1.0)
        W1b = W1.reshape(N_BLOCKS, BLOCK_SIZE, in_f)
        h = jnp.einsum('nf,ibf->nib', xf, W1b)
        h = jax.nn.gelu(h, approximate=False) * mask[:, :, None]
        W2b = W2.reshape(in_f, N_BLOCKS, BLOCK_SIZE)
        y = jnp.einsum('nib,fib->nf', h, W2b)
        return y.reshape(x_shape)

    def _L1_attn_ref(hidden_states, Wq, Wk, Wv, Wo, gamma, beta):
        import jax, jax.numpy as jnp
        import numpy as np
        B, T, HID = (1, 512, 512)
        H = 16
        D = HID // H
        EPS = 1e-05

        def _layer_norm(x, eps=1e-05):
            mu = jnp.mean(x, axis=-1, keepdims=True)
            var = jnp.mean((x - mu) ** 2, axis=-1, keepdims=True)
            return (x - mu) * jax.lax.rsqrt(var + eps)

        def _feature_map(x, gamma, beta):
            return _layer_norm(x * gamma + beta)
        b, t, _ = hidden_states.shape
        q = (hidden_states @ Wq.T).reshape(b, t, H, D)
        k = (hidden_states @ Wk.T).reshape(b, t, H, D)
        v = (hidden_states @ Wv.T).reshape(b, t, H, D)
        q = _feature_map(q, gamma, beta)
        k = _feature_map(k, gamma, beta)
        q = q * D ** (-0.5)
        attn = jnp.einsum('bqhd,bkhd->bhqk', q, k) ** 2
        mask = jnp.tril(jnp.ones((t, t), dtype=bool))
        attn = jnp.where(mask, attn, 0.0)
        o = jnp.einsum('bhqk,bkhd->bqhd', attn, v)
        z = jnp.sum(attn, axis=-1)
        o = o / (jnp.swapaxes(z, 1, 2)[..., None] + EPS)
        o = o.reshape(b, t, H * D)
        return o @ Wo.T

    def _L1_xattn_ref(B, T, C, w, u, k, v):
        import jax, jax.numpy as jnp
        import numpy as np
        B_DIM, T_DIM, C_DIM = (16, 256, 512)

        def _wkv(w, u, k, v):
            Bn, Tn, Cn = k.shape
            NEG_INF = jnp.float32(-1e+38)

            def step(carry, kv_t):
                p, q, o = carry
                kt, vt = kv_t
                no = jnp.maximum(o, u + kt)
                A = jnp.exp(o - no)
                E = jnp.exp(u + kt - no)
                y = (A * p + E * vt) / (A * q + E)
                no2 = jnp.maximum(w + o, kt)
                A2 = jnp.exp(w + o - no2)
                E2 = jnp.exp(kt - no2)
                return ((A2 * p + E2 * vt, A2 * q + E2, no2), y)
            init = (jnp.zeros((Bn, Cn), k.dtype), jnp.zeros((Bn, Cn), k.dtype), jnp.full((Bn, Cn), NEG_INF, k.dtype))
            kT = jnp.moveaxis(k, 1, 0)
            vT = jnp.moveaxis(v, 1, 0)
            _, yT = jax.lax.scan(step, init, (kT, vT))
            return jnp.moveaxis(yT, 0, 1)
        return _wkv(w, u, k, v)

    def _L1_ffn_ref(x, W_g, W_u, W_d):
        import jax, jax.numpy as jnp
        import numpy as np
        EPS = 1e-08

        def rms_norm(x, eps=EPS):
            mean = jnp.mean(x, axis=-1, keepdims=True)
            var = jnp.var(x, axis=-1, keepdims=True)
            return (x - mean) / jnp.sqrt(var + eps)

        def activation_quant(x):
            s = 127.0 / jnp.max(jnp.abs(x), axis=-1, keepdims=True)
            return jnp.clip(jnp.round(s * x), -128, 127) / s

        def ternary_matmul(x, w):
            return jnp.matmul(x, jnp.sign(w).T)
        xq = activation_quant(rms_norm(x))
        g = jax.nn.silu(ternary_matmul(xq, W_g))
        u = ternary_matmul(xq, W_u)
        p = g * u
        return ternary_matmul(p, W_d)
    x = _layernorm(x + _L0_attn_ref(x, L0_attn_w_qkv, L0_attn_w_out), axis=-1)
    x = _layernorm(x + _L0_xattn_ref(x, ctx_2048, L0_xattn_Wq, L0_xattn_Wg, L0_xattn_bg, L0_xattn_Wkv, L0_xattn_Wo), axis=-1)
    x = _layernorm(x + _L0_ffn_ref(x, L0_ffn_Wr, L0_ffn_br, L0_ffn_W1, L0_ffn_W2), axis=-1)
    x = _layernorm(x + _L1_attn_ref(x, L1_attn_Wq, L1_attn_Wk, L1_attn_Wv, L1_attn_Wo, L1_attn_gamma, L1_attn_beta), axis=-1)
    x = _layernorm(x + _L1_xattn_ref(16, 128, 512, L1_xattn_w, L1_xattn_u, x, ctx_2048), axis=-1)
    x = _layernorm(x + _L1_ffn_ref(x, L1_ffn_W_g, L1_ffn_W_u, L1_ffn_W_d), axis=-1)
    return x

_drawn_inputs = setup_inputs


def setup_inputs(seed=0):
    import zlib

    import numpy as np

    out = dict(_drawn_inputs(seed))
    spreads = {'L0_xattn_bg': (1.0, 0.2), 'L0_ffn_br': (0.0, 0.1)}
    factors = {}
    for name, (base, spread) in spreads.items():
        noise = np.random.default_rng([zlib.crc32(name.encode()), seed]).standard_normal(out[name].shape)
        drawn = base * np.exp(spread * noise) if base else spread * noise
        out[name] = jnp.asarray(drawn.astype(out[name].dtype))
    for name, factor in factors.items():
        out[name] = (out[name] * factor).astype(out[name].dtype)
    return out
```

```python
from contextlib import ExitStack
import concourse.bass as bass
from concourse import mybir
P = 128
F32 = mybir.dt.float32
F32R = mybir.dt.float32r
BF16 = mybir.dt.bfloat16
ALU = mybir.AluOpType
ACT = mybir.ActivationFunctionType
AX = mybir.AxisListType.X
D = 512
KT = D // P
HG = 4
GROUPS = 4
TB = 4
TG = 4
TOK = TB * P


def stage_memory(nc, ctx):
    used = []

    def clear():
        with nc.Block() as block:
            @block.gpsimd
            def _(gps):
                for semaphore in used:
                    gps.sem_clear(semaphore)

    def sb(name, shape, dt=F32):
        return ctx.enter_context(nc.sbuf_tensor(name, shape, dt))

    def sem(name):
        used.append(ctx.enter_context(nc.semaphore(name)))
        return used[-1]

    return sb, sem, clear


def split3(nc, out, st_h, st_l, mv_h, mv_l, first, last):
    nc.tensor.matmul(out, st_h, mv_h, start=first, stop=False)
    nc.tensor.matmul(out, st_h, mv_l, start=False, stop=False)
    return nc.tensor.matmul(out, st_l, mv_h, start=False, stop=last)


def make_identity(nc, gps, ident, ready):
    gps.memset(ident[:], 0.0).then_inc(ready, 1)
    gps.wait_ge(ready, 1)
    gps.affine_select(out=ident[:], in_=ident[:], compare_op=ALU.not_equal, fill=1.0, base=0,
                      pattern=[[-1, P]], channel_multiplier=1).then_inc(ready, 1)


def self_attention(nc, x_dram, xT_dram, w_dram, acc):
    with ExitStack() as ctx:
        sb, sem, clear_semaphores = stage_memory(nc, ctx)
        w_raw = sb("a_w_raw", [P, 4, KT * D])
        w_h = sb("a_w_h", [P, 4, KT, D], F32R)
        w_l = sb("a_w_l", [P, 4, KT, D], F32R)
        xT_raw = sb("a_xT_raw", [P, KT, TOK])
        xT_h = sb("a_xT_h", [P, KT, TOK], F32R)
        xT_l = sb("a_xT_l", [P, KT, TOK], F32R)
        qT = sb("a_qT", [P, 2, TOK])
        kT = sb("a_kT", [P, 2, TOK])
        v = sb("a_v", [P, TB, D])
        probs = sb("a_probs", [P, 2, TB, P])
        probsT = sb("a_probsT", [P, TOK])
        oT_h = sb("a_oT_h", [P, HG, TOK], F32R)
        oT_l = sb("a_oT_l", [P, HG, TOK], F32R)
        ident = sb("a_ident", [P, P])
        rowmax = sb("a_rowmax", [P, 2, TB])
        negmax = sb("a_negmax", [P, 2, TB])
        rowsum = sb("a_rowsum", [P, 2, TB])
        rowinv = sb("a_rowinv", [P, 2, TB])
        ring = [ctx.enter_context(nc.psum_tensor(f"a_ring{i}", [P, D], F32)) for i in range(4)]
        ps_s = [ctx.enter_context(nc.psum_tensor(f"a_ps_s{i}", [P, TOK], F32)) for i in range(2)]
        ps_t = ctx.enter_context(nc.psum_tensor("a_ps_t", [P, TOK], F32))
        ps_o = ctx.enter_context(nc.psum_tensor("a_ps_o", [P, TOK], F32))
        x_loaded, w_loaded, xT_loaded = sem("a_x_loaded"), [sem(f"a_w_loaded{c}") for c in range(4)], sem("a_xT_loaded")
        ident_ready = sem("a_ident_ready")
        w_high, w_split, sp_waited = sem("a_w_high"), sem("a_w_split"), sem("a_sp_waited")
        xT_high, xT_split = sem("a_xT_high"), sem("a_xT_split")
        v_done, q_done, k_done, s_done = sem("a_v_done"), sem("a_q_done"), sem("a_k_done"), sem("a_s_done")
        t_done, o_done, out_done = sem("a_t_done"), sem("a_o_done"), sem("a_out_done")
        v_ready, q_ready, k_ready = sem("a_v_ready"), sem("a_q_ready"), sem("a_k_ready")
        max_ready, negmax_ready, exp_ready, inv_ready, probs_ready = (
            sem("a_max_ready"), sem("a_negmax_ready"), sem("a_exp_ready"), sem("a_inv_ready"), sem("a_probs_ready"))
        probsT_ready, o_high, o_split, added = sem("a_probsT_ready"), sem("a_o_high"), sem("a_o_split"), sem("a_added")
        V, Q, K, O = range(4)
        SCALE = float(P) ** -0.5
        ctx.callback(clear_semaphores)
        block = ctx.enter_context(nc.Block())

        @block.sync
        def _(sp):
            sp.dma_start(xT_raw[:], xT_dram[0]).then_inc(xT_loaded, 16)
            for c in range(4):
                sp.dma_start(w_raw[:, c], w_dram[0, c]).then_inc(w_loaded[c], 16)
            sp.dma_start(acc[:], x_dram).then_inc(x_loaded, 16)
            with sp.Fori(0, GROUPS) as g:
                with sp.Fori(0, TG) as t:
                    sp.wait_ge(xT_split, (g * TG + t) * KT + KT)
                    sp.sem_inc(sp_waited, 1)
                    sp.dma_start(xT_raw[:], xT_dram[(t + 1) % TG if isinstance(t, int) else (t + 1) & 3]).then_inc(xT_loaded, 16)
                for c in range(4):
                    sp.wait_ge(w_split, g * 4 * KT + (c + 1) * KT)
                    sp.sem_inc(sp_waited, 1)
                    sp.dma_start(w_raw[:, c], w_dram[(g + 1) & 3, c]).then_inc(w_loaded[c], 16)
            for c in range(4):
                sp.wait_ge(w_loaded[c], (GROUPS + 1) * 16)

        @block.gpsimd
        def _(gps):
            make_identity(nc, gps, ident, ident_ready)
            with gps.Fori(0, GROUPS) as g:
                for c in range(4):
                    for kt in range(KT):
                        gps.wait_ge(w_high, g * 4 * KT + c * KT + kt + 1)
                        gps.tensor_tensor(w_l[:, c, kt], w_raw[:, c, kt * D:(kt + 1) * D],
                                          w_h[:, c, kt].bitcast(F32), ALU.subtract).then_inc(w_split, 1)

        @block.scalar
        def _(act):
            act.wait_ge(xT_loaded, 16)
            for kt in range(KT):
                act.activation(xT_h[:, kt], xT_raw[:, kt], ACT.Copy).then_inc(xT_high, 1)
            with act.Fori(0, GROUPS) as g:
                for c, (freed, per) in enumerate(((v_done, 16), (q_done, 16), (k_done, 16), (out_done, 16))):
                    act.wait_ge(w_loaded[c], g * 16 + 16)
                    act.wait_ge(freed, g * per + 1)
                    for kt in range(KT):
                        act.activation(w_h[:, c, kt], w_raw[:, c, kt * D:(kt + 1) * D], ACT.Copy).then_inc(w_high, 1)
                with act.Fori(0, TG) as t:
                    s = g * TG + t

                    def q_evac(j):
                        act.wait_ge(q_done, s * HG + j + 2)
                        act.activation(qT[:, j % 2], ring[2 * (j % 2)][:], ACT.Copy).then_inc(q_ready, 1)

                    def exps(j):
                        act.wait_ge(negmax_ready, s * HG + j + 1)
                        for b in range(TB):
                            last = act.activation(probs[:, j % 2, b], ps_s[j % 2][:, b * P:(b + 1) * P], ACT.Exp,
                                                  bias=negmax[:, j % 2, b:b + 1], scale=SCALE,
                                                  accum_out=rowsum[:, j % 2, b:b + 1])
                        last.then_inc(exp_ready, 1)

                    def probsT_evac(j):
                        act.wait_ge(t_done, s * HG + j + 1)
                        act.activation(probsT[:], ps_t[:], ACT.Copy).then_inc(probsT_ready, 1)

                    def o_evac(j):
                        act.wait_ge(o_done, s * HG + j + 1)
                        act.activation(oT_h[:, j], ps_o[:], ACT.Copy).then_inc(o_high, 1)

                    for i in range(TB):
                        act.wait_ge(v_done, s * TB + i + 2)
                        act.activation(v[:, i], ring[i][:], ACT.Copy).then_inc(v_ready, 1)
                    q_evac(0)
                    exps(0)
                    for j in range(1, HG):
                        q_evac(j)
                        probsT_evac(j - 1)
                        o_evac(j - 1)
                        exps(j)
                    act.wait_ge(xT_loaded, s * 16 + 32)
                    act.wait_ge(k_done, s * HG + HG + 1)
                    for kt in range(KT):
                        act.activation(xT_h[:, kt], xT_raw[:, kt], ACT.Copy).then_inc(xT_high, 1)
                    probsT_evac(HG - 1)
                    o_evac(HG - 1)

        @block.vector
        def _(dve):
            def low_parts(s):
                for kt in range(KT):
                    dve.wait_ge(xT_high, s * KT + kt + 1)
                    dve.tensor_tensor(xT_l[:, kt], xT_raw[:, kt], xT_h[:, kt].bitcast(F32), ALU.subtract).then_inc(xT_split, 1)
            dve.sem_inc(added, TB)
            low_parts(0)
            dve.wait_ge(x_loaded, 16)
            with dve.Fori(0, GROUPS) as g:
                with dve.Fori(0, TG) as t:
                    s = g * TG + t

                    def k_evac(j):
                        dve.wait_ge(k_done, s * HG + j + 2)
                        dve.tensor_copy(kT[:, j % 2], ring[2 * (j % 2) + 1][:]).then_inc(k_ready, 1)

                    def softmax(j):
                        n = s * HG + j + 1
                        dve.wait_ge(s_done, n)
                        dve.tensor_reduce(rowmax[:, j % 2], ps_s[j % 2][:].rearrange("p (b k) -> p b k", b=TB), AX, ALU.max).then_inc(max_ready, 1)
                        dve.wait_ge(max_ready, n)
                        dve.tensor_scalar(negmax[:, j % 2], rowmax[:, j % 2], -SCALE, None, ALU.mult).then_inc(negmax_ready, 1)
                        dve.wait_ge(exp_ready, n)
                        dve.reciprocal(rowinv[:, j % 2], rowsum[:, j % 2]).then_inc(inv_ready, 1)
                        dve.wait_ge(inv_ready, n)
                        dve.tensor_tensor(probs[:, j % 2], probs[:, j % 2],
                                          rowinv[:, j % 2].unsqueeze(2).broadcast_to([P, TB, P]), ALU.mult).then_inc(probs_ready, 1)

                    def o_low(j):
                        dve.wait_ge(o_high, s * HG + j + 1)
                        dve.tensor_tensor(oT_l[:, j], ps_o[:], oT_h[:, j].bitcast(F32), ALU.subtract).then_inc(o_split, 1)

                    k_evac(0)
                    softmax(0)
                    for j in range(1, HG):
                        k_evac(j)
                        o_low(j - 1)
                        softmax(j)
                    low_parts(s + 1)
                    o_low(HG - 1)
                    for i in range(TB):
                        dve.wait_ge(out_done, s * TB + i + 2)
                        dve.tensor_tensor(acc[:, t * TB + i], acc[:, t * TB + i], ring[i][:], ALU.add).then_inc(added, 1)

        @block.tensor
        def _(pe):
            for freed in (v_done, q_done, k_done, out_done):
                pe.sem_inc(freed, 1)
            pe.wait_ge(ident_ready, 2)
            with pe.Fori(0, GROUPS) as g:
                with pe.Fori(0, TG) as t:
                    s = g * TG + t

                    def project(c, j, ks, bank, done):
                        for kt in ks:
                            cols = slice(j * P, (j + 1) * P)
                            last = split3(nc, bank[:], w_h[:, c, kt, cols], w_l[:, c, kt, cols],
                                          xT_h[:, kt], xT_l[:, kt], kt == 0, kt == KT - 1)
                        if ks[-1] == KT - 1:
                            last.then_inc(done, 1)

                    def scores(j):
                        pe.wait_ge(q_ready, s * HG + j + 1)
                        pe.wait_ge(k_ready, s * HG + j + 1)
                        for b in range(TB):
                            c = slice(b * P, (b + 1) * P)
                            last = nc.tensor.matmul(ps_s[j % 2][:, c], qT[:, j % 2, c], kT[:, j % 2, c], start=True, stop=True)
                        last.then_inc(s_done, 1)

                    def transposes(j):
                        pe.wait_ge(probs_ready, s * HG + j + 1)
                        for b in range(TB):
                            last = nc.tensor.transpose(ps_t[:, b * P:(b + 1) * P], probs[:, j % 2, b], ident[:])
                        last.then_inc(t_done, 1)

                    def weighted(j):
                        pe.wait_ge(probsT_ready, s * HG + j + 1)
                        if j:
                            pe.wait_ge(o_split, s * HG + j)
                        for b in range(TB):
                            c = slice(b * P, (b + 1) * P)
                            last = nc.tensor.matmul(ps_o[:, c], v[:, b, j * P:(j + 1) * P], probsT[:, c], start=True, stop=True)
                        last.then_inc(o_done, 1)

                    def out_proj(j, tiles):
                        pe.wait_ge(o_split, s * HG + j + 1)
                        if j == 0:
                            pe.wait_ge(w_split, g * 4 * KT + 4 * KT)
                        for i in tiles:
                            if j == 0:
                                pe.wait_ge((q_ready, k_ready)[i % 2], s * HG + 3 + i // 2)
                            c = slice(i * P, (i + 1) * P)
                            last = split3(nc, ring[i][:], oT_h[:, j, c], oT_l[:, j, c],
                                          w_h[:, O, j], w_l[:, O, j], j == 0, j == HG - 1)
                            if j == HG - 1:
                                last.then_inc(out_done, 1)

                    for i in range(TB):
                        for kt in range(KT):
                            if i == 0:
                                pe.wait_ge(xT_split, s * KT + kt + 1)
                                pe.wait_ge(w_split, g * 4 * KT + kt + 1)
                            if kt == 0:
                                pe.wait_ge(added, s * TB + i + 1)
                            c = slice(i * P, (i + 1) * P)
                            last = split3(nc, ring[i][:], xT_h[:, kt, c], xT_l[:, kt, c],
                                          w_h[:, V, kt], w_l[:, V, kt], kt == 0, kt == KT - 1)
                        last.then_inc(v_done, 1)
                    for j in range(HG):
                        if j == 0:
                            pe.wait_ge(w_split, g * 4 * KT + 2 * KT)
                        if j < 2:
                            pe.wait_ge(v_ready, s * TB + 2 * j + 1)
                        else:
                            pe.wait_ge(q_ready, s * HG + j - 1)
                        project(Q, j, range(KT), ring[2 * (j % 2)], q_done)
                        if j == 0:
                            pe.wait_ge(w_split, g * 4 * KT + 3 * KT)
                        if j < 2:
                            pe.wait_ge(v_ready, s * TB + 2 * j + 2)
                        else:
                            pe.wait_ge(k_ready, s * HG + j - 1)
                        project(K, j, range(KT // 2), ring[2 * (j % 2) + 1], k_done)
                        if j:
                            transposes(j - 1)
                        project(K, j, range(KT // 2, KT), ring[2 * (j % 2) + 1], k_done)
                        if j:
                            weighted(j - 1)
                        scores(j)
                    out_proj(0, range(TB))
                    out_proj(1, range(TB))
                    transposes(HG - 1)
                    out_proj(2, range(TB // 2))
                    weighted(HG - 1)
                    out_proj(2, range(TB // 2, TB))
                    out_proj(3, range(TB))


class LayerNorm:

    def __init__(self, nc, sb, sem, name, eps, count=TB):
        self.nc, self.eps, self.count = nc, eps, count
        self.stats, self.moments = sb(f"{name}_stats", [P, count, 6]), sb(f"{name}_moments", [P, count, 2])
        self.var_eps, self.rstd, self.power = sb(f"{name}_var_eps", [P, count]), sb(f"{name}_rstd", [P, count]), sb(f"{name}_power", [P, count])
        self.stats_ready, self.moments_ready = sem(f"{name}_stats_ready"), sem(f"{name}_moments_ready")
        self.var_ready, self.rstd_ready = sem(f"{name}_var_ready"), sem(f"{name}_rstd_ready")
        self.power_ready, self.waited = sem(f"{name}_power_ready"), sem(f"{name}_waited")

    def constants(self, gps):
        gps.memset(self.power[:], -0.5).then_inc(self.power_ready, 1)
        gps.wait_ge(self.power_ready, 1)

    def statistics(self, dve, rows, n):
        for i in range(self.count):
            dve.bn_stats(self.stats[:, i], rows(i)).then_inc(self.stats_ready, 1)
        dve.wait_ge(self.stats_ready, n * self.count + self.count)
        dve.sem_inc(self.waited, 1)
        for i in range(self.count):
            dve.bn_aggr(self.moments[:, i], self.stats[:, i]).then_inc(self.moments_ready, 1)
        dve.wait_ge(self.moments_ready, n * self.count + self.count)
        dve.tensor_scalar(self.var_eps[:], self.moments[:, :, 1], self.eps, None, ALU.add).then_inc(self.var_ready, 1)

    def power_step(self, gps, n):
        gps.wait_ge(self.var_ready, n + 1)
        gps.tensor_tensor(self.rstd[:], self.var_eps[:], self.power[:], ALU.pow).then_inc(self.rstd_ready, 1)

    def apply(self, dve, out, row, i):
        return dve.tensor_scalar(out, row, self.moments[:, i, 0:1], self.rstd[:, i:i + 1], ALU.subtract, ALU.mult)


def linear_cross_attention(nc, ctxT_dram, w_dram, bg_dram, acc, x1_dram):
    with ExitStack() as ctx:
        sb, sem, clear_semaphores = stage_memory(nc, ctx)
        K, V, Q, G, O = range(5)
        w_h, w_l = sb("b_w_h", [P, 5, KT, D], F32R), sb("b_w_l", [P, 5, KT, D], F32R)
        c_raw = sb("b_c_raw", [P, KT, TOK])
        xs = c_raw
        c_h, c_l = sb("b_c_h", [P, KT, TOK], F32R), sb("b_c_l", [P, KT, TOK], F32R)
        xT_h, xT_l = sb("b_xT_h", [P, KT, TOK], F32R), sb("b_xT_l", [P, KT, TOK], F32R)
        kf, vs = sb("b_kf", [P, 2, D]), sb("b_v", [P, 2, D])
        low = sb("b_low", [P, 2, D])
        kv_blocks, ks_blocks = sb("b_kv_blocks", [P, TB, KT, P]), sb("b_ks_blocks", [P, TB, KT, P])
        w_raw = kv_blocks
        qf, gate = sb("b_qf", [P, 2, TOK]), sb("b_gate", [P, 2, TOK])
        a_h, a_l = sb("b_a_h", [P, KT, TOK], F32R), sb("b_a_l", [P, KT, TOK], F32R)
        bg, nbg = sb("b_bg", [P, KT]), sb("b_nbg", [P, KT])
        ident, blocks, ones = sb("b_ident", [P, P]), sb("b_blocks", [P, P]), sb("b_ones", [P, 1])
        ln_in, ln_out = LayerNorm(nc, sb, sem, "b_ln_in", 1e-5), LayerNorm(nc, sb, sem, "b_ln_out", 1e-5)
        bank = [ctx.enter_context(nc.psum_tensor(f"b_bank{i}", [P, D], F32)) for i in range(8)]
        w_loaded, bg_loaded, c_loaded, x1_stored = sem("b_w_loaded"), sem("b_bg_loaded"), sem("b_c_loaded"), sem("b_x1_stored")
        ident_ready, blocks_ready, nbg_ready = sem("b_ident_ready"), sem("b_blocks_ready"), sem("b_nbg_ready")
        w_high, w_split, c_high, c_split = sem("b_w_high"), sem("b_w_split"), sem("b_c_high"), sem("b_c_split")
        xs_ready, x_kept, xT_done, xT_high, xT_split = (
            sem("b_xs_ready"), sem("b_x_kept"), sem("b_xT_done"), sem("b_xT_high"), sem("b_xT_split"))
        k_done, v_done, kv_done, q_done, g_done, nd_done, out_done = (
            sem("b_k_done"), sem("b_v_done"), sem("b_kv_done"), sem("b_q_done"), sem("b_g_done"), sem("b_nd_done"), sem("b_out_done"))
        k_min, k_exp, k_ready, v_ready, kv_ready = sem("b_k_min"), sem("b_k_exp"), sem("b_k_ready"), sem("b_v_ready"), sem("b_kv_ready")
        q_min, q_exp, q_ready, g_exp, g_ready = sem("b_q_min"), sem("b_q_exp"), sem("b_q_ready"), sem("b_g_exp"), sem("b_g_ready")
        den_ready, inv_ready, a_ready, a_high, a_split = (
            sem("b_den_ready"), sem("b_inv_ready"), sem("b_a_ready"), sem("b_a_high"), sem("b_a_split"))
        added, x1_ready = sem("b_added"), sem("b_x1_ready")
        waited, sp_waited = sem("b_waited"), sem("b_sp_waited")
        EPS = 1e-6
        ctx.callback(clear_semaphores)
        block = ctx.enter_context(nc.Block())

        def steps(eng, body):
            with eng.Fori(0, TG - 1) as t:
                body(t, True)
            body(TG - 1, False)

        @block.sync
        def _(sp):
            sp.dma_start(bg[:], bg_dram).then_inc(bg_loaded, 16)
            sp.dma_start(w_raw[:], w_dram[0]).then_inc(w_loaded, 16)
            sp.dma_start(c_raw[:], ctxT_dram[0]).then_inc(c_loaded, 16)
            for c in range(1, 5):
                sp.wait_ge(w_split, c * KT)
                sp.dma_start(w_raw[:], w_dram[c]).then_inc(w_loaded, 16)

            def body(t, more):
                if more:
                    sp.wait_ge(xT_done, t * KT + KT)
                    sp.sem_inc(sp_waited, 1)
                    sp.wait_ge(x_kept, t + 1)
                    sp.sem_inc(sp_waited, 1)
                    sp.dma_start(c_raw[:], ctxT_dram[t + 1]).then_inc(c_loaded, 16)
                sp.wait_ge(x1_ready, t * TB + TB)
                sp.sem_inc(sp_waited, 1)
                sp.dma_start(x1_dram[t], acc[:, bass.ds(t * TB, TB)] if not isinstance(t, int) else acc[:, t * TB:t * TB + TB]).then_inc(x1_stored, 16)
            steps(sp, body)
            sp.wait_ge(x1_stored, TG * 16)

        @block.gpsimd
        def _(gps):
            ln_in.constants(gps)
            ln_out.constants(gps)
            ln_in.power_step(gps, 0)
            make_identity(nc, gps, ident, ident_ready)
            gps.memset(ones[:], 1.0).then_inc(blocks_ready, 1)
            gps.memset(blocks[:], 0.0).then_inc(blocks_ready, 1)
            gps.wait_ge(blocks_ready, 2)
            for h in range(4):
                gps.memset(blocks[32 * h:32 * h + 32, 32 * h:32 * h + 32], 1.0).then_inc(blocks_ready, 1)
            gps.wait_ge(blocks_ready, 6)

            def context_low(t):
                for kt in range(KT):
                    gps.wait_ge(c_high, t * KT + kt + 1)
                    gps.tensor_tensor(c_l[:, kt], c_raw[:, kt], c_h[:, kt].bitcast(F32), ALU.subtract).then_inc(c_split, 1)

            context_low(0)

            def body(t, more):
                if more:
                    ln_in.power_step(gps, t + 1)
                    context_low(t + 1)
                for m in range(KT):
                    gps.wait_ge(a_high, t * KT + m + 1)
                    gps.tensor_tensor(a_l[:, m], gate[:, m % 2], a_h[:, m].bitcast(F32), ALU.subtract).then_inc(a_split, 1)
                ln_out.power_step(gps, t)
            steps(gps, body)

        @block.scalar
        def _(act):
            def w_chunk(c):
                act.wait_ge(w_loaded, (c + 1) * 16)
                for kt in range(KT):
                    act.activation(w_h[:, c, kt], w_raw[:, kt], ACT.Copy).then_inc(w_high, 1)

            def context_high(t):
                act.wait_ge(c_loaded, t * 16 + 16)
                for kt in range(KT):
                    act.activation(c_h[:, kt], c_raw[:, kt], ACT.Copy).then_inc(c_high, 1)

            def keep_x(t):
                act.wait_ge(xs_ready, t * TB + TB)
                act.activation(acc[:, bass.ds(t * TB, TB)], xs[:], ACT.Copy).then_inc(x_kept, 1)

            def xT_highs(t):
                for kt in range(KT):
                    act.wait_ge(xT_done, t * KT + kt + 1)
                    act.activation(xT_h[:, kt], bank[4 + kt % 2][:], ACT.Copy).then_inc(xT_high, 1)

            w_chunk(K)
            context_high(0)
            w_chunk(V)
            w_chunk(Q)
            keep_x(0)
            xT_highs(0)
            w_chunk(G)
            w_chunk(O)

            def body(t, more):
                def a_highs(m):
                    act.wait_ge(a_ready, t * KT + m + 1)
                    act.activation(a_h[:, m], gate[:, m % 2], ACT.Copy).then_inc(a_high, 1)

                for i in range(TB):
                    act.wait_ge(k_min, t * TB + i + 1)
                    act.activation(low[:, i % 2], low[:, i % 2], ACT.Exp).then_inc(k_exp, 1)
                    act.wait_ge(v_done, t * TB + i + 1)
                    act.activation(vs[:, i % 2], bank[2 + i % 2][:], ACT.Copy).then_inc(v_ready, 1)
                if more:
                    context_high(t + 1)
                    keep_x(t + 1)
                for m in range(KT):
                    act.wait_ge(q_min, t * KT + m + 1)
                    act.activation(low[:, m % 2], low[:, m % 2], ACT.Exp).then_inc(q_exp, 1)
                    act.wait_ge(g_done, t * KT + m + 1)
                    if m == 0:
                        act.wait_ge(nbg_ready, 1)
                    if m >= 2:
                        act.wait_ge(a_split, t * KT + m - 1)
                    act.activation(gate[:, m % 2], bank[2 + m % 2][:], ACT.Exp, bias=nbg[:, m:m + 1], scale=-1.0).then_inc(g_exp, 1)
                    if m:
                        a_highs(m - 1)
                if more:
                    xT_highs(t + 1)
                a_highs(KT - 1)
            steps(act, body)

        @block.vector
        def _(dve):
            dve.wait_ge(bg_loaded, 16)
            dve.tensor_scalar(nbg[:], bg[:], -1.0, None, ALU.mult).then_inc(nbg_ready, 1)

            def norm_in(t):
                ln_in.statistics(dve, lambda i: acc[:, t * TB + i], t)
                dve.wait_ge(ln_in.rstd_ready, t + 1)
                dve.wait_ge(c_split, t * KT + KT)
                for i in range(TB):
                    ln_in.apply(dve, xs[:, i], acc[:, t * TB + i], i).then_inc(xs_ready, 1)

            def w_lows(c):
                for kt in range(KT):
                    dve.wait_ge(w_high, c * KT + kt + 1)
                    dve.tensor_tensor(w_l[:, c, kt], w_raw[:, kt], w_h[:, c, kt].bitcast(F32), ALU.subtract).then_inc(w_split, 1)

            def xT_lows(t):
                for kt in range(KT):
                    dve.wait_ge(xT_high, t * KT + kt + 1)
                    dve.tensor_tensor(xT_l[:, kt], bank[4 + kt % 2][:], xT_h[:, kt].bitcast(F32), ALU.subtract).then_inc(xT_split, 1)

            norm_in(0)
            w_lows(K)
            w_lows(V)
            w_lows(Q)
            xT_lows(0)
            w_lows(G)
            w_lows(O)
            dve.sem_inc(added, TB)

            def body(t, more):
                def feature_min(i, done, mins):
                    dve.wait_ge(done, t * TB + i + 1)
                    dve.tensor_scalar(low[:, i % 2], bank[i % 2][:], 0.0, None, ALU.min).then_inc(mins, 1)

                def feature(i, exps, out, ready):
                    dve.wait_ge(exps, t * TB + i + 1)
                    dve.scalar_tensor_tensor(out, bank[i % 2][:], 0.0, low[:, i % 2], ALU.max, ALU.add).then_inc(ready, 1)

                def kv_masks(i):
                    dve.wait_ge(kv_done, t * TB + i + 1)
                    if i == 0:
                        dve.wait_ge(blocks_ready, 6)
                    each = blocks[:].unsqueeze(1).broadcast_to([P, KT, P])
                    dve.tensor_tensor(kv_blocks[:, i], bank[4][:].rearrange("p (m e) -> p m e", m=KT), each, ALU.mult)
                    dve.tensor_tensor(ks_blocks[:, i], bank[5][:, 0:KT].unsqueeze(2).broadcast_to([P, KT, P]), each,
                                      ALU.mult).then_inc(kv_ready, 1)

                def quotient(m):
                    n = t * KT + m + 1
                    dve.wait_ge(g_exp, n)
                    dve.tensor_scalar(gate[:, m % 2], gate[:, m % 2], 1.0, None, ALU.add).then_inc(g_ready, 1)
                    dve.wait_ge(g_ready, n)
                    dve.wait_ge(nd_done, n)
                    dve.scalar_tensor_tensor(gate[:, m % 2], bank[7][:], EPS, gate[:, m % 2], ALU.add, ALU.mult).then_inc(den_ready, 1)
                    dve.wait_ge(den_ready, n)
                    dve.reciprocal(gate[:, m % 2], gate[:, m % 2]).then_inc(inv_ready, 1)
                    dve.wait_ge(inv_ready, n)
                    dve.tensor_tensor(gate[:, m % 2], bank[6][:], gate[:, m % 2], ALU.mult).then_inc(a_ready, 1)

                for i in range(TB):
                    feature_min(i, k_done, k_min)
                    if i:
                        kv_masks(i - 1)
                    feature(i, k_exp, kf[:, i % 2], k_ready)
                kv_masks(TB - 1)
                if more:
                    norm_in(t + 1)
                for m in range(KT):
                    feature_min(m, q_done, q_min)
                    feature(m, q_exp, qf[:, m % 2], q_ready)
                    if m:
                        quotient(m - 1)
                if more:
                    xT_lows(t + 1)
                quotient(KT - 1)
                dve.wait_ge(x_kept, t + 1)
                for i in range(TB):
                    dve.wait_ge(out_done, t * TB + i + 1)
                    dve.tensor_tensor(acc[:, t * TB + i], acc[:, t * TB + i], bank[i][:], ALU.add).then_inc(added, 1)
                dve.wait_ge(added, t * TB + 2 * TB)
                dve.sem_inc(waited, 1)
                ln_out.statistics(dve, lambda i: acc[:, t * TB + i], t)
                dve.wait_ge(ln_out.rstd_ready, t + 1)
                for i in range(TB):
                    ln_out.apply(dve, acc[:, t * TB + i], acc[:, t * TB + i], i).then_inc(x1_ready, 1)
            steps(dve, body)

        @block.tensor
        def _(pe):
            def xT_transposes(t):
                for kt in range(KT):
                    if kt == 0:
                        pe.wait_ge(xs_ready, t * TB + TB)
                    if kt >= 2:
                        pe.wait_ge(xT_split, t * KT + kt - 1)
                    for i in range(TB):
                        last = nc.tensor.transpose(bank[4 + kt % 2][:, i * P:(i + 1) * P], xs[:, i, kt * P:(kt + 1) * P], ident[:])
                    last.then_inc(xT_done, 1)

            pe.wait_ge(ident_ready, 2)
            pe.wait_ge(blocks_ready, 6)
            xT_transposes(0)

            def body(t, more):
                def rows(c, i, out, done, first):
                    for kt in range(KT):
                        if first:
                            pe.wait_ge(c_split, t * KT + kt + 1)
                        part = slice(i * P, (i + 1) * P)
                        last = split3(nc, out[:], c_h[:, kt, part], c_l[:, kt, part], w_h[:, c, kt], w_l[:, c, kt], kt == 0, kt == KT - 1)
                    last.then_inc(done, 1)

                def columns(c, m, out, done):
                    for kt in range(KT):
                        if m == 0 and c == Q:
                            pe.wait_ge(xT_split, t * KT + kt + 1)
                        part = slice(m * P, (m + 1) * P)
                        last = split3(nc, out[:], w_h[:, c, kt, part], w_l[:, c, kt, part], xT_h[:, kt], xT_l[:, kt], kt == 0, kt == KT - 1)
                    last.then_inc(done, 1)

                def summary(i):
                    pe.wait_ge(k_ready, t * TB + i + 1)
                    pe.wait_ge(v_ready, t * TB + i + 1)
                    if i:
                        pe.wait_ge(kv_ready, t * TB + i)
                    for m in range(KT):
                        part = slice(m * P, (m + 1) * P)
                        nc.tensor.matmul(bank[5][:, m:m + 1], kf[:, i % 2, part], ones[:], start=True, stop=True)
                    for m in range(KT):
                        part = slice(m * P, (m + 1) * P)
                        last = nc.tensor.matmul(bank[4][:, part], kf[:, i % 2, part], vs[:, i % 2, part], start=True, stop=True)
                    last.then_inc(kv_done, 1)

                def apply_summary(m):
                    pe.wait_ge(q_ready, t * KT + m + 1)
                    if m:
                        pe.wait_ge(a_ready, t * KT + m)
                    else:
                        pe.wait_ge(kv_ready, t * TB + TB)
                    for b in range(TB):
                        part = slice(b * P, (b + 1) * P)
                        nc.tensor.matmul(bank[7][:, part], ks_blocks[:, b, m], qf[:, m % 2, part], start=True, stop=True)
                    for b in range(TB):
                        part = slice(b * P, (b + 1) * P)
                        last = nc.tensor.matmul(bank[6][:, part], kv_blocks[:, b, m], qf[:, m % 2, part], start=True, stop=True)
                    last.then_inc(nd_done, 1)

                for i in range(TB):
                    if i < 2:
                        pe.wait_ge(added, t * TB + TB)
                    else:
                        pe.wait_ge(k_ready, t * TB + i - 1)
                        pe.wait_ge(v_ready, t * TB + i - 1)
                    if i == 0:
                        pe.wait_ge(w_split, (K + 1) * KT)
                    rows(K, i, bank[i % 2], k_done, i == 0)
                    if i == 0:
                        pe.wait_ge(w_split, (V + 1) * KT)
                    rows(V, i, bank[2 + i % 2], v_done, False)
                    if i:
                        summary(i - 1)
                pe.wait_ge(w_split, (Q + 1) * KT)
                for m in range(KT):
                    if m < 2:
                        pe.wait_ge(k_ready, t * TB + 3 + m)
                    else:
                        pe.wait_ge(q_ready, t * KT + m - 1)
                    columns(Q, m, bank[m % 2], q_done)
                    if m == 0:
                        pe.wait_ge(w_split, (G + 1) * KT)
                        summary(TB - 1)
                    if m < 2:
                        pe.wait_ge(v_ready, t * TB + 3 + m)
                    else:
                        pe.wait_ge(g_exp, t * KT + m - 1)
                    columns(G, m, bank[2 + m % 2], g_done)
                    if m:
                        apply_summary(m - 1)
                if more:
                    pe.wait_ge(kv_ready, t * TB + TB)
                    xT_transposes(t + 1)
                apply_summary(KT - 1)
                pe.wait_ge(w_split, (O + 1) * KT)
                for m in range(KT):
                    pe.wait_ge(a_split, t * KT + m + 1)
                    for i in range(TB):
                        if m == 0:
                            pe.wait_ge((q_ready, g_exp)[i // 2], t * KT + 3 + i % 2)
                        part = slice(i * P, (i + 1) * P)
                        last = split3(nc, bank[i][:], a_h[:, m, part], a_l[:, m, part], w_h[:, O, m], w_l[:, O, m], m == 0, m == KT - 1)
                        if m == KT - 1:
                            last.then_inc(out_done, 1)
            steps(pe, body)


NB = 16
TOP = 4


def steps(eng, body):
    with eng.Fori(0, TG - 1) as t:
        body(t, True)
    body(TG - 1, False)


def blockwise_ffn(nc, w_dram, wr_dram, br_dram, x1_dram, x2_dram):
    with ExitStack() as ctx:
        sb, sem, clear_semaphores = stage_memory(nc, ctx)
        NC = 2 * NB // 4
        w_h, w_l = sb("c_w_h", [P, NC, 4, D], F32R), sb("c_w_l", [P, NC, 4, D], F32R)
        xT_h, xT_l = sb("c_xT_h", [P, 2, KT, TOK], F32R), sb("c_xT_l", [P, 2, KT, TOK], F32R)
        xs, res = sb("c_xs", [P, TB, D]), sb("c_res", [P, TB, D])
        w_raw = res
        act_f, act_m = sb("c_act_f", [P, 2, TOK]), sb("c_act_m", [P, 2, TOK])
        act_h, act_l = sb("c_act_h", [P, 2, TOK], F32R), sb("c_act_l", [P, 2, TOK], F32R)
        wr_raw = sb("c_wr_raw", [P, KT, NB])
        wr_h, wr_l = sb("c_wr_h", [P, KT, NB], F32R), sb("c_wr_l", [P, KT, NB], F32R)
        br = sb("c_br", [NB, 1])
        logitT = sb("c_logitT", [NB, TOK])
        ident, identb = sb("c_ident", [P, P]), sb("c_identb", [P, P], BF16)
        pick = sb("c_pick", [NB, NB, P], BF16)
        shifted, prob = sb("c_shifted", [P, TB, NB]), sb("c_prob", [P, TB, NB])
        rmax, rsum, rinv = sb("c_rmax", [P, TB]), sb("c_rsum", [P, TB]), sb("c_rinv", [P, TB])
        top8, above, n_above = sb("c_top8", [P, TB, 8]), sb("c_above", [P, TB, NB]), sb("c_n_above", [P, TB])
        equal, rank, ones = sb("c_equal", [P, TB, NB]), sb("c_rank", [P, TB, NB]), sb("c_ones", [P, NB])
        mask, maskT = sb("c_mask", [P, TB, NB], BF16), sb("c_maskT", [NB, 2, TOK], BF16)
        ln = LayerNorm(nc, sb, sem, "c_ln", 1e-5)
        bank = [ctx.enter_context(nc.psum_tensor(f"c_bank{i}", [P, D], F32)) for i in range(7)]
        small = ctx.enter_context(nc.psum_tensor("c_small", [P, D], F32))
        smallb = small[:].bitcast(BF16)
        w_loaded = [sem(f"c_w_loaded{i}") for i in range(4)]
        small_loaded, xs_loaded, res_loaded, x2_stored = sem("c_small_loaded"), sem("c_xs_loaded"), sem("c_res_loaded"), sem("c_x2_stored")
        ident_ready, identb_ready, pick_ready = sem("c_ident_ready"), sem("c_identb_ready"), sem("c_pick_ready")
        w_high, w_split, wr_high, wr_split = sem("c_w_high"), sem("c_w_split"), sem("c_wr_high"), sem("c_wr_split")
        xT_done, xT_high, xT_split = sem("c_xT_done"), sem("c_xT_high"), sem("c_xT_split")
        logits_done, logits_ready, back_done, shift_ready, exp_ready = (
            sem("c_logits_done"), sem("c_logits_ready"), sem("c_back_done"), sem("c_shift_ready"), sem("c_exp_ready"))
        chain = sem("c_chain")
        maskT_done, maskT_ready = sem("c_maskT_done"), sem("c_maskT_ready")
        h_done, b_done, y_done = sem("c_h_done"), sem("c_b_done"), sem("c_y_done")
        gelu_ready, masked_ready, act_high, act_split = (
            sem("c_gelu_ready"), sem("c_masked_ready"), sem("c_act_high"), sem("c_act_split"))
        added, x2_ready = sem("c_added"), sem("c_x2_ready")
        waited, pe_waited = sem("c_waited"), sem("c_pe_waited")
        CHAIN = 4 + 7 * TB
        ctx.callback(clear_semaphores)
        block = ctx.enter_context(nc.Block())

        @block.sync
        def _(sp):
            sp.dma_start(xs[:], x1_dram[0]).then_inc(xs_loaded, 16)
            sp.dma_start(wr_raw[:], wr_dram).then_inc(small_loaded, 16)
            sp.dma_start(br[:], br_dram).then_inc(small_loaded, 16)
            for n in range(NC * 4):
                if n >= 4:
                    sp.wait_ge(w_split, n - 3)
                sp.dma_start(w_raw[:, n % 4], w_dram[n // 4, :, n % 4]).then_inc(w_loaded[n % 4], 16)
            sp.wait_ge(w_split, NC * 4)
            sp.dma_start(res[:], x1_dram[0]).then_inc(res_loaded, 16)

            def body(t, more):
                if more:
                    sp.wait_ge(xT_done, t * KT + KT)
                    sp.dma_start(xs[:], x1_dram[t + 1]).then_inc(xs_loaded, 16)
                sp.wait_ge(x2_ready, t * TB + TB)
                sp.dma_start(x2_dram[t], res[:]).then_inc(x2_stored, 16)
                if more:
                    sp.wait_ge(x2_stored, t * 16 + 16)
                    sp.dma_start(res[:], x1_dram[t + 1]).then_inc(res_loaded, 16)
            steps(sp, body)
            sp.wait_ge(x2_stored, TG * 16)

        @block.gpsimd
        def _(gps):
            make_identity(nc, gps, ident, ident_ready)
            ln.constants(gps)
            gps.memset(pick[:], 0.0).then_inc(pick_ready, 1)
            gps.memset(ones[:], 1.0).then_inc(pick_ready, 1)
            gps.wait_ge(pick_ready, 2)
            gps.affine_select(out=pick[:], in_=pick[:], compare_op=ALU.not_equal, fill=1.0, base=0,
                              pattern=[[-1, NB], [0, P]], channel_multiplier=1).then_inc(pick_ready, 1)
            gps.wait_ge(pick_ready, 3)

            def body(t, more):
                for i in range(NB):
                    gps.wait_ge(act_high, t * NB + i + 1)
                    gps.tensor_tensor(act_l[:, i % 2], act_m[:, i % 2], act_h[:, i % 2].bitcast(F32), ALU.subtract).then_inc(act_split, 1)
                ln.power_step(gps, t)
            steps(gps, body)

        XT_AT, LOGITS_AT, BACK_AT, MASK_AT = (1, 3, 5, 7), 9, 10, 13

        @block.scalar
        def _(act):
            def xT_high_part(t, kt):
                act.wait_ge(xT_done, t * KT + kt + 1)
                act.activation(xT_h[:, t % 2 if isinstance(t, int) else t & 1, kt], small[:], ACT.Copy).then_inc(xT_high, 1)

            def logit_bias(t):
                act.wait_ge(logits_done, t + 1)
                act.activation(logitT[:], small[0:NB, :], ACT.Identity, bias=br[:, 0:1]).then_inc(logits_ready, 1)

            def exps(t):
                act.wait_ge(shift_ready, t + 1)
                act.activation(prob[:], shifted[:], ACT.Exp).then_inc(exp_ready, 1)

            act.wait_ge(small_loaded, 32)
            act.activation(wr_h[:], wr_raw[:], ACT.Copy).then_inc(wr_high, 1)
            for kt in range(KT):
                xT_high_part(0, kt)
            logit_bias(0)
            exps(0)
            for n in range(NC * 4):
                act.wait_ge(w_loaded[n % 4], (n // 4 + 1) * 16)
                act.activation(w_h[:, n // 4, n % 4], w_raw[:, n % 4], ACT.Copy).then_inc(w_high, 1)

            def body(t, more):
                for i in range(NB):
                    act.wait_ge(h_done, t * NB + i + 1)
                    act.activation(act_f[:, i % 2], bank[4 + i % 2][:], ACT.Gelu).then_inc(gelu_ready, 1)
                    act.wait_ge(masked_ready, t * NB + i + 1)
                    act.activation(act_h[:, i % 2], act_m[:, i % 2], ACT.Copy).then_inc(act_high, 1)
                    if more:
                        if i in XT_AT:
                            xT_high_part(t + 1, XT_AT.index(i))
                        if i == LOGITS_AT:
                            logit_bias(t + 1)
                        if i == BACK_AT:
                            exps(t + 1)
            steps(act, body)

        @block.vector
        def _(dve):
            def xT_low_part(t, kt):
                dve.wait_ge(xT_high, t * KT + kt + 1)
                par = t % 2 if isinstance(t, int) else t & 1
                dve.tensor_tensor(xT_l[:, par, kt], small[:], xT_h[:, par, kt].bitcast(F32), ALU.subtract).then_inc(xT_split, 1)

            def shift(t):
                dve.wait_ge(back_done, t + 1)
                logits = small[:, 0:TB * NB].rearrange("p (b e) -> p b e", b=TB)
                dve.tensor_reduce(rmax[:], logits, AX, ALU.max).then_inc(chain, 1)
                dve.wait_ge(chain, t * CHAIN + 1)
                dve.tensor_tensor(shifted[:], logits, rmax[:].unsqueeze(2).broadcast_to([P, TB, NB]), ALU.subtract).then_inc(shift_ready, 1)

            def choose(t):
                at = [1]

                def link(instruction):
                    at[0] += 1
                    instruction.then_inc(chain, 1)
                    dve.wait_ge(chain, t * CHAIN + at[0])

                dve.wait_ge(exp_ready, t + 1)
                link(dve.tensor_reduce(rsum[:], prob[:], AX, ALU.add))
                link(dve.reciprocal(rinv[:], rsum[:]))
                link(dve.tensor_tensor(prob[:], prob[:], rinv[:].unsqueeze(2).broadcast_to([P, TB, NB]), ALU.mult))
                for b in range(TB):
                    dve.sem_inc(waited, 1)
                    least = top8[:, b, TOP - 1:TOP]
                    link(dve.max(top8[:, b], prob[:, b]))
                    link(dve.tensor_scalar(above[:, b], prob[:, b], least, None, ALU.is_gt, ALU.add, accum_out=n_above[:, b:b + 1]))
                    link(dve.tensor_scalar(equal[:, b], prob[:, b], least, None, ALU.is_equal))
                    link(dve.tensor_tensor_scan(rank[:, b], ones[:], equal[:, b], 0.0, ALU.mult, ALU.add))
                    link(dve.tensor_scalar(rank[:, b], rank[:, b], n_above[:, b:b + 1], float(TOP), ALU.add, ALU.is_le))
                    link(dve.tensor_tensor(rank[:, b], rank[:, b], equal[:, b], ALU.mult))
                    link(dve.tensor_tensor(mask[:, b], rank[:, b], above[:, b], ALU.add))
                assert at[0] == CHAIN

            def mask_columns(t):
                dve.wait_ge(maskT_done, t + 1)
                par = t % 2 if isinstance(t, int) else t & 1
                dve.tensor_copy(maskT[:, par], smallb[0:NB, 0:TOK]).then_inc(maskT_ready, 1)

            dve.wait_ge(ident_ready, 2)
            dve.tensor_copy(identb[:], ident[:]).then_inc(identb_ready, 1)
            dve.wait_ge(wr_high, 1)
            dve.tensor_tensor(wr_l[:], wr_raw[:], wr_h[:].bitcast(F32), ALU.subtract).then_inc(wr_split, 1)
            dve.wait_ge(pick_ready, 3)
            for kt in range(KT):
                xT_low_part(0, kt)
            shift(0)
            choose(0)
            mask_columns(0)
            for n in range(NC * 4):
                dve.wait_ge(w_high, n + 1)
                dve.tensor_tensor(w_l[:, n // 4, n % 4], w_raw[:, n % 4], w_h[:, n // 4, n % 4].bitcast(F32), ALU.subtract).then_inc(w_split, 1)
            dve.sem_inc(added, TB)

            def body(t, more):
                for i in range(NB):
                    dve.wait_ge(gelu_ready, t * NB + i + 1)
                    dve.wait_ge(b_done, t * NB + i + 1)
                    if i >= 2:
                        dve.wait_ge(act_split, t * NB + i - 1)
                    dve.tensor_tensor(act_m[:, i % 2], act_f[:, i % 2], bank[6][:], ALU.mult).then_inc(masked_ready, 1)
                    if more:
                        if i in XT_AT:
                            xT_low_part(t + 1, XT_AT.index(i))
                        if i == BACK_AT:
                            shift(t + 1)
                            choose(t + 1)
                        if i == MASK_AT:
                            mask_columns(t + 1)
                dve.wait_ge(res_loaded, t * 16 + 16)
                for i in range(TB):
                    dve.wait_ge(y_done, t * TB + i + 1)
                    dve.tensor_tensor(res[:, i], res[:, i], bank[i][:], ALU.add).then_inc(added, 1)
                dve.wait_ge(added, t * TB + 2 * TB)
                ln.statistics(dve, lambda i: res[:, i], t)
                dve.wait_ge(ln.rstd_ready, t + 1)
                for i in range(TB):
                    ln.apply(dve, res[:, i], res[:, i], i).then_inc(x2_ready, 1)
            steps(dve, body)

        @block.tensor
        def _(pe):
            def xT_transposes(t, kt):
                if kt == 0:
                    pe.wait_ge(xs_loaded, t * 16 + 16)
                else:
                    pe.wait_ge(xT_split, t * KT + kt)
                for i in range(TB):
                    last = nc.tensor.transpose(small[:, i * P:(i + 1) * P], xs[:, i, kt * P:(kt + 1) * P], ident[:])
                last.then_inc(xT_done, 1)

            def logits(t):
                par = t % 2 if isinstance(t, int) else t & 1
                pe.wait_ge(xT_split, t * KT + KT)
                for kt in range(KT):
                    last = split3(nc, small[0:NB, :], wr_h[:, kt], wr_l[:, kt], xT_h[:, par, kt], xT_l[:, par, kt], kt == 0, kt == KT - 1)
                last.then_inc(logits_done, 1)

            def logits_back(t):
                pe.wait_ge(logits_ready, t + 1)
                pe.sem_inc(pe_waited, 1)
                for b in range(TB):
                    last = nc.tensor.transpose(small[:, b * NB:(b + 1) * NB], logitT[:, b * P:(b + 1) * P], ident[0:NB, 0:NB])
                last.then_inc(back_done, 1)

            def mask_transposes(t):
                pe.wait_ge(chain, t * CHAIN + CHAIN)
                for b in range(TB):
                    last = nc.tensor.transpose(smallb[0:NB, b * P:(b + 1) * P], mask[:, b], identb[:])
                last.then_inc(maskT_done, 1)

            pe.wait_ge(ident_ready, 2)
            pe.wait_ge(pick_ready, 3)
            pe.wait_ge(identb_ready, 1)
            pe.wait_ge(wr_split, 1)
            for kt in range(KT):
                xT_transposes(0, kt)
            logits(0)
            logits_back(0)
            mask_transposes(0)

            def body(t, more):
                par = t % 2 if isinstance(t, int) else t & 1

                def hidden(i):
                    if i >= 2:
                        pe.wait_ge(gelu_ready, t * NB + i - 1)
                    for kt in range(KT):
                        pe.wait_ge(w_split, 8 * (i // 4) + kt + 1)
                        part = slice((i % 4) * P, (i % 4 + 1) * P)
                        last = split3(nc, bank[4 + i % 2][:], w_h[:, 2 * (i // 4), kt, part], w_l[:, 2 * (i // 4), kt, part],
                                      xT_h[:, par, kt], xT_l[:, par, kt], kt == 0, kt == KT - 1)
                    last.then_inc(h_done, 1)
                    if i == 0:
                        pe.wait_ge(maskT_ready, t + 1)
                    else:
                        pe.wait_ge(masked_ready, t * NB + i)
                    pe.sem_inc(pe_waited, 1)
                    nc.tensor.matmul(bank[6][:], pick[:, i], maskT[:, par], start=True, stop=True).then_inc(b_done, 1)

                def back(i):
                    pe.wait_ge(act_split, t * NB + i + 1)
                    pe.wait_ge(w_split, 8 * (i // 4) + 4 + i % 4 + 1)
                    for b in range(TB):
                        if i == 0:
                            pe.wait_ge(added, t * TB + b + 1)
                        part = slice(b * P, (b + 1) * P)
                        last = split3(nc, bank[b][:], act_h[:, i % 2, part], act_l[:, i % 2, part],
                                      w_h[:, 2 * (i // 4) + 1, i % 4], w_l[:, 2 * (i // 4) + 1, i % 4], i == 0, i == NB - 1)
                        if i == NB - 1:
                            last.then_inc(y_done, 1)

                for i in range(NB):
                    hidden(i)
                    if more:
                        if i in XT_AT:
                            xT_transposes(t + 1, XT_AT.index(i))
                        if i == LOGITS_AT:
                            logits(t + 1)
                        if i == BACK_AT:
                            logits_back(t + 1)
                        if i == MASK_AT:
                            mask_transposes(t + 1)
                    if i:
                        back(i - 1)
                back(NB - 1)
            steps(pe, body)


HD = 32
NH = D // HD
NEG = -1e38
EXT = P + 1


def powered_attention_and_wkv(nc, x2_dram, ctxT_dram, w_dram, gamma_dram, beta_dram, wu_dram, x4_dram):
    with ExitStack() as ctx:
        sb, sem, clear_semaphores = stage_memory(nc, ctx)
        Q, K, V, O = range(4)
        w_h, w_l = sb("d_w_h", [P, 4, KT, D], F32R), sb("d_w_l", [P, 4, KT, D], F32R)
        xs, res = sb("d_xs", [P, TB, D]), sb("d_res", [P, TB, D])
        x3 = res
        x4 = xs
        zT = sb("d_zT", [P, KT, TB, P])
        w_raw = [res[:], zT[:].rearrange("p c b e -> p c (b e)")]
        w_mean = sb("d_w_mean", [P, KT * NH])
        xT_h, xT_l = sb("d_xT_h", [P, KT, TOK], F32R), sb("d_xT_l", [P, KT, TOK], F32R)
        gamma, beta_row, beta_mean = sb("d_gamma", [P, HD]), sb("d_beta_row", [P, HD]), sb("d_beta_mean", [P, 1])
        beta = sb("d_beta", [P, 1])
        qT, kT = sb("d_qT", [P, 2, TOK]), sb("d_kT", [P, 1, TOK])
        squares = sb("d_squares", [P, 2, 2, TOK])
        v = sb("d_v", [P, TB, NH, HD + 1])
        norms, factor = sb("d_norms", [P, TB, 2, 4]), sb("d_factor", [P, TB * 4])
        scaled_q = sb("d_scaled_q", [P, TB, 4])
        weights = sb("d_weights", [P, 4, TOK])
        o_nat = sb("d_o_nat", [P, 2, TB, P])
        oT_h, oT_l = sb("d_oT_h", [P, KT, TOK], F32R), sb("d_oT_l", [P, KT, TOK], F32R)
        ident, causal, heads = sb("d_ident", [P, P]), sb("d_causal", [P, P]), sb("d_heads", [P, 4])
        ln3, ln4 = LayerNorm(nc, sb, sem, "d_ln3", 1e-5), LayerNorm(nc, sb, sem, "d_ln4", 1e-5)
        ext = lambda name, n=2: sb(name, [P, n, TB, EXT])
        k_ext, w_ext = ext("d_k_ext", KT), ext("d_w_ext", KT)
        wu = sb("d_wu", [P, 2, KT])
        vT = sb("d_vT", [P, KT, TB, P])
        o_ext, decay, entry, entry_v = ext("d_o_ext", 1), ext("d_decay"), ext("d_entry"), ext("d_entry_v", 1)
        p_ext, q_ext = ext("d_p_ext", 1), ext("d_q_ext", 1)
        old, new = sb("d_old", [P, 2, TB, P]), sb("d_new", [P, 2, TB, P])
        num, den = p_ext[:, 0, :, 0:P], q_ext[:, 0, :, 0:P]
        part = sb("d_part", [P, TB, P])
        inv = part
        ps_s = [ctx.enter_context(nc.psum_tensor(f"d_ps_s{i}", [P, TOK], F32)) for i in range(4)]
        ps_o = ctx.enter_context(nc.psum_tensor("d_ps_o", [P, 2, TOK], F32))
        ring = [ctx.enter_context(nc.psum_tensor(f"d_ring{i}", [P, TOK], F32)) for i in range(2)]
        names = """sp_waited small_loaded xs_loaded res_loaded v_loaded x4_stored ident_ready const_ready beta_ready
            w_fold w_high w_split xT_high xT_split
            v_ready q_ready k_ready sums_ready norms_ready vs_ready
            s_done square_ready dve_mask gps_mask av_done factor_ready o_ready oT_high oT_split out_done added x3_ready
            kx_ready o_scan a_ready d_ready e_ready decay_ready entry_ready old_ready new_ready ev_ready
            p_ready num_ready q_scan pool_parts den_ready ln_ready inv_ready newton z_parts z_ready zn_ready x4_ready""".split()
        S = {n: sem("d_" + n) for n in names}
        w_loaded = [sem("d_w_loaded0"), sem("d_w_loaded1")]
        ring_full = [sem("d_full0"), sem("d_full1")]
        FL = NH * HD
        ctx.callback(clear_semaphores)
        block = ctx.enter_context(nc.Block())

        def ring_order(attend, recur, more):
            names = []
            if attend:
                names += ["v0", "v1", "v2", "v3", "q0", "k0"]
            if recur:
                names += [f"kx{c}" for c in range(4)]
            if attend:
                for m in range(4):
                    if m < 3:
                        names += [f"q{m + 1}", f"k{m + 1}"]
                    names += [f"su{m}"]
                    if m:
                        names += [f"ot{m - 1}"]
                if more:
                    names += [f"xt{c}" for c in range(4)]
                names += ["ot3"]
            if recur:
                names += [f"zn{i}" for i in range(4)]
            return names

        class Ring:

            def __init__(self, t, attend, recur, more):
                self.t, self.order = t, ring_order(attend, recur, more)
                if isinstance(t, int):
                    self.base = (2, 2 + 12, 2 + 12 + 16, 2 + 12 + 32, 2 + 12 + 32 + 14)[t]
                else:
                    self.base = (t - 1) * 16 + 2 + 12

            def bank(self, name):
                return ring[self.order.index(name) % 2]

            def claim(self, pe, name):
                n, t = self.order.index(name), self.t
                if n < 2:
                    if not (isinstance(t, int) and t == 0):
                        pe.wait_ge(S["zn_ready"], (t - 1) * TB + 1)
                    return
                kind, k = self.order[n - 2][:-1], int(self.order[n - 2][-1])
                pe.wait_ge(*{
                    "v": (S["v_ready"], t * TB + k + 1), "q": (S["q_ready"], t * KT + k + 1),
                    "k": (S["k_ready"], t * KT + k + 1), "kx": (S["kx_ready"], (t - 1) * KT + k + 1),
                    "su": (S["sums_ready"], (t * KT + k) * 2 + 1), "ot": (S["oT_split"], t * KT + k + 1),
                    "xt": (S["xT_split"], (t + 1) * KT + k + 1), "zn": (S["zn_ready"], (t - 1) * TB + k + 2),
                }[kind])

            def filled(self, instruction, name):
                instruction.then_inc(ring_full[self.order.index(name) % 2], 1)

            def await_full(self, eng, name):
                n = self.order.index(name)
                eng.wait_ge(ring_full[n % 2], self.base + n // 2 + 1)

        def rounds(eng, body):
            body(0, True, False, True, Ring(0, True, False, True))
            with eng.Fori(1, TG - 1) as t:
                body(t, True, True, True, Ring(t, True, True, True))
            body(TG - 1, True, True, False, Ring(TG - 1, True, True, False))
            body(TG, False, True, False, Ring(TG, False, True, False))


        @block.sync
        def _(sp):
            sp.sem_inc(S["x4_stored"], 16)
            sp.dma_start(xs[:], x2_dram[0]).then_inc(S["xs_loaded"], 16)
            sp.dma_start(w_raw[0], w_dram[Q]).then_inc(w_loaded[0], 16)
            sp.dma_start(gamma[:], gamma_dram.rearrange("(a n) -> a n", a=1).broadcast_to([P, HD])).then_inc(S["small_loaded"], 16)
            sp.dma_start(beta_row[:], beta_dram.rearrange("(a n) -> a n", a=1).broadcast_to([P, HD])).then_inc(S["small_loaded"], 16)
            for j in range(4):
                sp.dma_start(beta[j * HD:(j + 1) * HD], beta_dram.rearrange("(n a) -> n a", a=1)).then_inc(S["small_loaded"], 16)
            sp.dma_start(wu[:], wu_dram).then_inc(S["small_loaded"], 16)
            sp.dma_start(w_raw[1], w_dram[K]).then_inc(w_loaded[1], 16)
            for c in (V, O):
                sp.wait_ge(S["w_split"], (c - 1) * KT)
                sp.dma_start(w_raw[c % 2], w_dram[c]).then_inc(w_loaded[c % 2], 16)
            sp.wait_ge(S["w_split"], 4 * KT)
            sp.dma_start(res[:], x2_dram[0]).then_inc(S["res_loaded"], 16)

            def body(t, attend, recur, more, ring_uses):
                if attend and more:
                    sp.wait_ge(S["xT_high"], (t + 1) * KT)
                    sp.sem_inc(S["sp_waited"], 1)
                    if recur:
                        sp.wait_ge(S["x4_stored"], t * 16)
                    sp.dma_start(xs[:], x2_dram[t + 1]).then_inc(S["xs_loaded"], 16)
                if recur:
                    sp.wait_ge(S["pool_parts"], (t - 1) * KT * 3 + 1)
                    sp.dma_start(vT[:], ctxT_dram[t - 1]).then_inc(S["v_loaded"], 16)
                if attend and recur:
                    sp.wait_ge(S["kx_ready"], t * KT)
                    sp.dma_start(res[:], x2_dram[t]).then_inc(S["res_loaded"], 16)
                if recur:
                    sp.wait_ge(S["x4_ready"], (t - 1) * TB + TB)
                    sp.dma_start(x4_dram[t - 1], x4[:]).then_inc(S["x4_stored"], 16)
            rounds(sp, body)
            sp.wait_ge(S["x4_stored"], TG * 16 + 16)

        @block.gpsimd
        def _(gps):
            for counted in ("pool_parts", "e_ready", "z_ready"):
                gps.sem_inc(S[counted], 1)
            ln3.constants(gps)
            ln4.constants(gps)
            make_identity(nc, gps, ident, S["ident_ready"])
            const = S["const_ready"]
            gps.memset(causal[:], 1.0).then_inc(const, 1)
            gps.memset(heads[:], 0.0).then_inc(const, 1)
            gps.memset(k_ext[:], NEG).then_inc(const, 1)
            gps.memset(w_ext[:], 0.0).then_inc(const, 1)
            for buffer in (decay, entry, entry_v):
                gps.memset(buffer[:], 0.0).then_inc(const, 1)
            gps.wait_ge(const, 7)
            gps.affine_select(out=causal[:], in_=causal[:], compare_op=ALU.is_ge, fill=0.0, base=0,
                              pattern=[[1, P]], channel_multiplier=-1).then_inc(const, 1)
            gps.memset(w_ext[:, :, :, 0:1], NEG).then_inc(const, 1)
            gps.wait_ge(const, 9)
            for j in range(4):
                gps.memset(heads[j * HD:(j + 1) * HD, j:j + 1], 1.0).then_inc(const, 1)
            gps.wait_ge(const, 13)

            def body(t, attend, recur, more, uses):
                c0 = (t - 1) * KT

                def restart_part(c):
                    gps.wait_ge(S["o_scan"], c0 + c + 1)
                    gps.tensor_tensor(entry[:, c % 2, :, 1:], k_ext[:, c, :, 1:], o_ext[:, 0, :, 1:], ALU.subtract).then_inc(S["e_ready"], 1)

                def entry_values(c):
                    gps.wait_ge(S["entry_ready"], c0 + c + 1)
                    if c == 0:
                        gps.wait_ge(S["v_loaded"], (t - 1) * 16 + 16)
                    gps.tensor_tensor(entry_v[:, 0, :, 1:], entry[:, c % 2, :, 1:], vT[:, c], ALU.mult).then_inc(S["ev_ready"], 1)

                def parts(c):
                    gps.wait_ge(S["q_scan"], c0 + c + 1)
                    gps.wait_ge(S["new_ready"], c0 + c + 1)
                    gps.tensor_tensor(num, old[:, c % 2], p_ext[:, 0, :, 0:P], ALU.mult).then_inc(S["pool_parts"], 1)
                    gps.tensor_tensor(den, old[:, c % 2], q_ext[:, 0, :, 0:P], ALU.mult).then_inc(S["pool_parts"], 1)
                    gps.tensor_tensor(part[:], new[:, c % 2], vT[:, c], ALU.mult).then_inc(S["pool_parts"], 1)

                def masks(m):
                    for j in (1, 3):
                        gps.wait_ge(S["square_ready"], t * 16 + m * 4 + j + 1)
                        gps.tensor_tensor(weights[:, j].rearrange("p (b q) -> p b q", b=TB), weights[:, j].rearrange("p (b q) -> p b q", b=TB),
                                          causal[:].unsqueeze(1).broadcast_to([P, TB, P]), ALU.mult).then_inc(S["gps_mask"], 1)

                def add_keys(c):
                    gps.wait_ge(S["z_parts"], c0 + c + 1)
                    gps.tensor_tensor(zT[:, c], zT[:, c], k_ext[:, c, :, 1:], ALU.add).then_inc(S["z_ready"], 1)

                for s in range(6):
                    if recur:
                        if s >= 2:
                            add_keys(s - 2)
                        if s < 4:
                            restart_part(s)
                        if 1 <= s <= 4:
                            parts(s - 1)
                    if attend and s < 4:
                        masks(s)
                    if recur and s < 4:
                        entry_values(s)
                if attend:
                    ln3.power_step(gps, t)
                if recur:
                    ln4.power_step(gps, t - 1)
            rounds(gps, body)

        @block.scalar
        def _(act):
            act.sem_inc(S["zn_ready"], 1)
            for kt in range(KT):
                act.wait_ge(ring_full[kt % 2], kt // 2 + 1)
                act.activation(xT_h[:, kt], ring[kt % 2][:], ACT.Copy).then_inc(S["xT_high"], 1)
            for c in range(4):
                if c < V:
                    act.wait_ge(S["w_fold"], 2 + 4 * (c + 1))
                else:
                    act.wait_ge(w_loaded[c % 2], 32)
                for kt in range(KT):
                    act.activation(w_h[:, c, kt], w_raw[c % 2][:, kt], ACT.Copy).then_inc(S["w_high"], 1)

            def body(t, attend, recur, more, uses):
                c0 = (t - 1) * KT

                def v_evac(i):
                    uses.await_full(act, f"v{i}")
                    if i == 0 and not (isinstance(t, int) and t == 0):
                        act.wait_ge(S["av_done"], t * KT)
                    ins = act.activation(v[:, i, :, 0:HD], uses.bank(f"v{i}")[:].rearrange("p (h d) -> p h d", h=NH), ACT.Copy)
                    ins.then_inc(S["v_ready"], 1)

                def qk_evac(name, m, out, which, ready):
                    uses.await_full(act, f"{name}{m}")
                    if m == 0:
                        act.wait_ge(S["beta_ready"], 1)
                    bank = uses.bank(f"{name}{m}")
                    act.activation(out, bank[:], ACT.Identity, bias=beta[:, 0:1])
                    ins = act.activation(squares[:, m % 2, which], bank[:], ACT.Square, bias=beta[:, 0:1])
                    ins.then_inc(ready, 1)

                def score_squares(m):
                    for j in range(4):
                        if j == 0:
                            act.wait_ge(S["s_done"], t * KT + m + 1)
                        act.activation(weights[:, j], ps_s[j][:], ACT.Square).then_inc(S["square_ready"], 1)

                def kx_evac(c):
                    uses.await_full(act, f"kx{c}")
                    act.wait_ge(S["z_ready"], c0 + 1)
                    if isinstance(t, int) and t == 1 and c == 0:
                        act.wait_ge(S["const_ready"], 13)
                    ins = act.activation(k_ext[:, c, :, 1:], uses.bank(f"kx{c}")[:].rearrange("p (b q) -> p b q", b=TB), ACT.Copy)
                    ins.then_inc(S["kx_ready"], 1)

                def exponentials(c):
                    act.wait_ge(S["a_ready"], c0 + c + 1)
                    act.activation(decay[:, c % 2, :, 1:], decay[:, c % 2, :, 1:], ACT.Exp).then_inc(S["decay_ready"], 1)
                    act.wait_ge(S["e_ready"], c0 + c + 2)
                    act.activation(entry[:, c % 2, :, 1:], entry[:, c % 2, :, 1:], ACT.Exp).then_inc(S["entry_ready"], 1)
                    act.wait_ge(S["d_ready"], c0 + c + 1)
                    act.activation(old[:, c % 2], new[:, c % 2], ACT.Relu).then_inc(S["old_ready"], 1)
                    act.activation(new[:, c % 2], new[:, c % 2], ACT.Relu, scale=-1.0).then_inc(S["old_ready"], 1)
                    act.wait_ge(S["old_ready"], (c0 + c) * 2 + 2)
                    act.activation(old[:, c % 2], old[:, c % 2], ACT.Exp, scale=-1.0)
                    act.activation(new[:, c % 2], new[:, c % 2], ACT.Exp, scale=-1.0).then_inc(S["new_ready"], 1)

                def inverse_start(c):
                    act.wait_ge(S["den_ready"], c0 + c + 1)
                    act.activation(inv[:], den, ACT.Ln).then_inc(S["ln_ready"], 1)
                    act.wait_ge(S["ln_ready"], c0 + c + 1)
                    act.activation(inv[:], inv[:], ACT.Exp, scale=-1.0).then_inc(S["inv_ready"], 1)

                def oT_highs(m):
                    uses.await_full(act, f"ot{m}")
                    act.activation(oT_h[:, m], uses.bank(f"ot{m}")[:], ACT.Copy).then_inc(S["oT_high"], 1)

                if attend:
                    for i in range(TB):
                        v_evac(i)
                    qk_evac("q", 0, qT[:, 0], 0, S["q_ready"])
                    qk_evac("k", 0, kT[:, 0], 1, S["k_ready"])
                if recur:
                    for c in range(4):
                        kx_evac(c)
                for s in range(6):
                    if attend and s < 4:
                        if s < 3:
                            qk_evac("q", s + 1, qT[:, (s + 1) % 2], 0, S["q_ready"])
                        score_squares(s)
                        if s < 3:
                            qk_evac("k", s + 1, kT[:, 0], 1, S["k_ready"])
                    if recur and s < 4:
                        exponentials(s)
                    if attend and 1 <= s < 4:
                        oT_highs(s - 1)
                    if recur and 1 <= s <= 4:
                        inverse_start(s - 1)
                    if attend and s == 3:
                        if more:
                            for kt in range(KT):
                                uses.await_full(act, f"xt{kt}")
                                act.activation(xT_h[:, kt], uses.bank(f"xt{kt}")[:], ACT.Copy).then_inc(S["xT_high"], 1)
                        oT_highs(3)
                if recur:
                    act.wait_ge(S["x4_stored"], t * 16)
                    for i in range(TB):
                        uses.await_full(act, f"zn{i}")
                        ins = act.activation(x4[:, i], uses.bank(f"zn{i}")[:], ACT.Copy)
                        ins.then_inc(S["zn_ready"], 1)
            rounds(act, body)

        @block.vector
        def _(dve):
            dve.wait_ge(S["small_loaded"], 7 * 16)
            dve.tensor_reduce(beta_mean[:], beta_row[:], AX, ALU.add).then_inc(S["w_fold"], 1)
            dve.wait_ge(S["w_fold"], 1)
            dve.tensor_scalar(beta_mean[:], beta_mean[:], -1.0 / HD, None, ALU.mult).then_inc(S["w_fold"], 1)
            dve.wait_ge(S["w_fold"], 2)
            dve.tensor_tensor(beta[:], beta[:], beta_mean[:], ALU.add).then_inc(S["beta_ready"], 1)
            for c in (Q, K):
                wv = w_raw[c].rearrange("p k (h d) -> p (k h) d", d=HD)
                dve.wait_ge(w_loaded[c], 16)
                base = 2 + 4 * c
                dve.tensor_tensor(wv, wv, gamma[:].unsqueeze(1).broadcast_to([P, KT * NH, HD]), ALU.mult).then_inc(S["w_fold"], 1)
                dve.wait_ge(S["w_fold"], base + 1)
                dve.tensor_reduce(w_mean[:], wv, AX, ALU.add).then_inc(S["w_fold"], 1)
                dve.wait_ge(S["w_fold"], base + 2)
                dve.tensor_scalar(w_mean[:], w_mean[:], 1.0 / HD, None, ALU.mult).then_inc(S["w_fold"], 1)
                dve.wait_ge(S["w_fold"], base + 3)
                dve.tensor_tensor(wv, wv, w_mean[:].unsqueeze(2).broadcast_to([P, KT * NH, HD]), ALU.subtract).then_inc(S["w_fold"], 1)

            def w_lows(c):
                for kt in range(KT):
                    dve.wait_ge(S["w_high"], c * KT + kt + 1)
                    dve.tensor_tensor(w_l[:, c, kt], w_raw[c % 2][:, kt], w_h[:, c, kt].bitcast(F32), ALU.subtract).then_inc(S["w_split"], 1)

            for kt in range(KT):
                dve.wait_ge(S["xT_high"], kt + 1)
                ins = dve.tensor_tensor(xT_l[:, kt], ring[kt % 2][:], xT_h[:, kt].bitcast(F32), ALU.subtract)
                ins.then_inc(S["xT_split"], 1)
            for c in range(4):
                w_lows(c)
            dve.wait_ge(S["const_ready"], 13)
            for c in range(KT):
                dve.tensor_scalar(w_ext[:, c, :, 1:], w_ext[:, c, :, 1:], wu[:, 0, c:c + 1], None, ALU.add).then_inc(S["newton"], 1)
            dve.wait_ge(S["newton"], 4)
            dve.sem_inc(S["added"], TB)

            def body(t, attend, recur, more, uses):
                c0 = (t - 1) * KT
                flat = lambda x: x.rearrange("p b e -> p (b e)")

                def start(c):
                    dve.wait_ge(S["kx_ready"], c0 + c + 1)
                    dve.wait_ge(S["e_ready"], c0 + c + 1)
                    if c or not (isinstance(t, int) and t == 1):
                        dve.wait_ge(S["d_ready"], c0 + c)
                        dve.wait_ge(S["a_ready"], c0 + c)
                    dve.tensor_tensor_scan(flat(o_ext[:, 0]), flat(w_ext[:, c]), flat(k_ext[:, c]), NEG, ALU.add, ALU.max).then_inc(S["o_scan"], 1)
                    dve.wait_ge(S["o_scan"], c0 + c + 1)
                    before, after = o_ext[:, 0, :, 0:P], o_ext[:, 0, :, 1:]
                    dve.scalar_tensor_tensor(decay[:, c % 2, :, 1:], before, wu[:, 0, c:c + 1], after, ALU.add, ALU.subtract).then_inc(S["a_ready"], 1)
                    dve.scalar_tensor_tensor(new[:, c % 2], k_ext[:, c, :, 1:], wu[:, 1, c:c + 1], before, ALU.add, ALU.subtract).then_inc(S["d_ready"], 1)

                def scans(c):
                    dve.wait_ge(S["ev_ready"], c0 + c + 1)
                    dve.wait_ge(S["decay_ready"], c0 + c + 1)
                    if c:
                        dve.wait_ge(S["z_parts"], c0 + c)
                    dve.tensor_tensor_scan(flat(p_ext[:, 0]), flat(decay[:, c % 2]), flat(entry_v[:, 0]), 0.0, ALU.mult, ALU.add).then_inc(S["p_ready"], 1)
                    dve.tensor_tensor_scan(flat(q_ext[:, 0]), flat(decay[:, c % 2]), flat(entry[:, c % 2]), 0.0, ALU.mult, ALU.add).then_inc(S["q_scan"], 1)

                def fraction(c):
                    dve.wait_ge(S["pool_parts"], (c0 + c) * 3 + 4)
                    dve.tensor_tensor(num, num, part[:], ALU.add).then_inc(S["num_ready"], 1)
                    dve.tensor_tensor(den, den, new[:, c % 2], ALU.add).then_inc(S["den_ready"], 1)

                def divide(c):
                    n = 4 + 2 * (c0 + c)
                    dve.wait_ge(S["inv_ready"], c0 + c + 1)
                    dve.tensor_tensor(den, den, inv[:], ALU.mult).then_inc(S["newton"], 1)
                    dve.wait_ge(S["newton"], n + 1)
                    dve.scalar_tensor_tensor(den, den, 2.0, inv[:], ALU.subtract, ALU.mult).then_inc(S["newton"], 1)
                    dve.wait_ge(S["newton"], n + 2)
                    dve.wait_ge(S["num_ready"], c0 + c + 1)
                    if c == 0:
                        dve.wait_ge(S["zn_ready"], c0 + 1)
                    dve.scalar_tensor_tensor(zT[:, c], num, -1.0, den, ALU.mult, ALU.mult).then_inc(S["z_parts"], 1)

                def head_norms(m):
                    uses.await_full(dve, f"su{m}")
                    n = 2 * (t * KT + m)
                    ins = dve.tensor_scalar(norms[:], uses.bank(f"su{m}")[:, 0:32].rearrange("p (b w h) -> p b w h", b=TB, w=2),
                                            HD * 1e-5, None, ALU.add)
                    ins.then_inc(S["sums_ready"], 1)
                    dve.wait_ge(S["sums_ready"], n + 1)
                    dve.reciprocal(norms[:], norms[:]).then_inc(S["sums_ready"], 1)
                    dve.wait_ge(S["sums_ready"], n + 2)
                    dve.tensor_scalar(scaled_q[:], norms[:, :, 0], float(HD), None, ALU.mult).then_inc(S["norms_ready"], 1)
                    if m == 0:
                        dve.wait_ge(S["v_ready"], t * TB + TB)
                    hs = slice(4 * m, 4 * m + 4)
                    dve.tensor_tensor(v[:, :, hs, 0:HD], v[:, :, hs, 0:HD],
                                      norms[:, :, 1].unsqueeze(3).broadcast_to([P, TB, 4, HD]), ALU.mult)
                    dve.tensor_copy(v[:, :, hs, HD], norms[:, :, 1]).then_inc(S["vs_ready"], 1)

                def masks(m):
                    for j in (0, 2):
                        dve.wait_ge(S["square_ready"], t * 16 + m * 4 + j + 1)
                        dve.tensor_tensor(weights[:, j].rearrange("p (b q) -> p b q", b=TB), weights[:, j].rearrange("p (b q) -> p b q", b=TB),
                                          causal[:].unsqueeze(1).broadcast_to([P, TB, P]), ALU.mult).then_inc(S["dve_mask"], 1)

                def normalize(m):
                    n = 3 * (t * KT + m)
                    dve.wait_ge(S["av_done"], t * KT + m + 1)
                    dve.wait_ge(S["norms_ready"], t * KT + m + 1)
                    heads_of = ps_o[:, :, 0:8 * (HD + 1)].rearrange("p a (g e) -> p a g e", e=HD + 1)
                    rq = scaled_q[:].rearrange("p (a b) h -> p a (b h)", a=2)
                    f = factor[:].rearrange("p (a g) -> p a g", a=2)
                    dve.tensor_tensor(f, heads_of[:, :, :, HD], rq, ALU.mult).then_inc(S["factor_ready"], 1)
                    dve.wait_ge(S["factor_ready"], n + 1)
                    dve.tensor_scalar(factor[:], factor[:], 1e-5, None, ALU.add).then_inc(S["factor_ready"], 1)
                    dve.wait_ge(S["factor_ready"], n + 2)
                    dve.reciprocal(factor[:], factor[:]).then_inc(S["factor_ready"], 1)
                    dve.wait_ge(S["factor_ready"], n + 3)
                    dve.tensor_tensor(f, f, rq, ALU.mult).then_inc(S["o_ready"], 1)
                    dve.wait_ge(S["o_ready"], 3 * (t * KT + m) + 1)
                    for a in range(2):
                        dve.tensor_tensor(o_nat[:, m % 2, 2 * a:2 * a + 2].rearrange("p b (h d) -> p b h d", h=4),
                                          heads_of[:, a, :, 0:HD].rearrange("p (b h) d -> p b h d", b=2),
                                          f[:, a].rearrange("p (b h) -> p b h", b=2).unsqueeze(3).broadcast_to([P, 2, 4, HD]),
                                          ALU.mult).then_inc(S["o_ready"], 1)

                def oT_lows(m):
                    dve.wait_ge(S["oT_high"], t * KT + m + 1)
                    ins = dve.tensor_tensor(oT_l[:, m], uses.bank(f"ot{m}")[:], oT_h[:, m].bitcast(F32), ALU.subtract)
                    ins.then_inc(S["oT_split"], 1)

                for s in range(6):
                    if recur:
                        if s >= 2:
                            divide(s - 2)
                        if s < 4:
                            start(s)
                        if 1 <= s <= 4:
                            scans(s - 1)
                    if attend and s < 4:
                        head_norms(s)
                        masks(s)
                        normalize(s)
                        if s:
                            oT_lows(s - 1)
                    if recur and 1 <= s <= 4:
                        fraction(s - 1)
                    if attend and s == 3:
                        if more:
                            for kt in range(KT):
                                dve.wait_ge(S["xT_high"], (t + 1) * KT + kt + 1)
                                ins = dve.tensor_tensor(xT_l[:, kt], uses.bank(f"xt{kt}")[:], xT_h[:, kt].bitcast(F32), ALU.subtract)
                                ins.then_inc(S["xT_split"], 1)
                        oT_lows(3)
                if attend:
                    dve.wait_ge(S["res_loaded"], t * 16 + 16)
                    for i in range(TB):
                        dve.wait_ge(S["out_done"], t * TB + i + 1)
                        dve.tensor_tensor(res[:, i], res[:, i], ps_s[i][:], ALU.add).then_inc(S["added"], 1)
                    dve.wait_ge(S["added"], t * TB + 2 * TB)
                    ln3.statistics(dve, lambda i: res[:, i], t)
                    dve.wait_ge(ln3.rstd_ready, t + 1)
                    for i in range(TB):
                        ln3.apply(dve, x3[:, i], res[:, i], i).then_inc(S["x3_ready"], 1)
                if recur:
                    dve.wait_ge(S["zn_ready"], t * TB + 1)
                    ln4.statistics(dve, lambda i: x4[:, i], t - 1)
                    dve.wait_ge(ln4.rstd_ready, t)
                    for i in range(TB):
                        ln4.apply(dve, x4[:, i], x4[:, i], i).then_inc(S["x4_ready"], 1)
            rounds(dve, body)

        @block.tensor
        def _(pe):
            pe.wait_ge(S["ident_ready"], 2)
            pe.wait_ge(S["const_ready"], 13)
            pe.wait_ge(S["xs_loaded"], 16)
            for kt in range(KT):
                if kt >= 2:
                    pe.wait_ge(S["xT_split"], kt - 1)
                for i in range(TB):
                    last = nc.tensor.transpose(ring[kt % 2][:, i * P:(i + 1) * P], xs[:, i, kt * P:(kt + 1) * P], ident[:])
                last.then_inc(ring_full[kt % 2], 1)

            def body(t, attend, recur, more, uses):
                c0 = (t - 1) * KT

                def values(i):
                    uses.claim(pe, f"v{i}")
                    for kt in range(KT):
                        if i == 0 and kt == 0:
                            pe.wait_ge(S["xT_split"], t * KT + KT)
                        part = slice(i * P, (i + 1) * P)
                        last = split3(nc, uses.bank(f"v{i}")[:], xT_h[:, kt, part], xT_l[:, kt, part], w_h[:, V, kt], w_l[:, V, kt], kt == 0, kt == KT - 1)
                    uses.filled(last, f"v{i}")

                def columns(name, c, m):
                    uses.claim(pe, f"{name}{m}")
                    for kt in range(KT):
                        part = slice(m * P, (m + 1) * P)
                        last = split3(nc, uses.bank(f"{name}{m}")[:], w_h[:, c, kt, part], w_l[:, c, kt, part], xT_h[:, kt], xT_l[:, kt], kt == 0, kt == KT - 1)
                    uses.filled(last, f"{name}{m}")

                def keys_transposed(c):
                    if c == 0:
                        pe.wait_ge(S["x3_ready"], (t - 1) * TB + TB)
                    uses.claim(pe, f"kx{c}")
                    for i in range(TB):
                        last = nc.tensor.transpose(uses.bank(f"kx{c}")[:, i * P:(i + 1) * P], x3[:, i, c * P:(c + 1) * P], ident[:])
                    uses.filled(last, f"kx{c}")

                def scores(m):
                    pe.wait_ge(S["q_ready"], t * KT + m + 1)
                    pe.wait_ge(S["k_ready"], t * KT + m + 1)
                    if m:
                        pe.wait_ge(S["square_ready"], (t * KT + m) * 4)
                    else:
                        pe.wait_ge(S["added"], t * TB + TB)
                    for b in range(TB):
                        for j in range(4):
                            rows, part = slice(j * HD, (j + 1) * HD), slice(b * P, (b + 1) * P)
                            last = nc.tensor.matmul(ps_s[j][:, part], kT[rows, 0, part], qT[rows, m % 2, part], start=True, stop=True)
                    last.then_inc(S["s_done"], 1)

                def sums(m):
                    uses.claim(pe, f"su{m}")
                    for i in range(TB):
                        for which in range(2):
                            at = i * 8 + which * 4
                            last = nc.tensor.matmul(uses.bank(f"su{m}")[:, at:at + 4], squares[:, m % 2, which, i * P:(i + 1) * P],
                                                    heads[:], start=True, stop=True)
                    uses.filled(last, f"su{m}")

                def weighted(m):
                    pe.wait_ge(S["vs_ready"], t * KT + m + 1)
                    if not (isinstance(t, int) and t == 0 and m == 0):
                        pe.wait_ge(S["o_ready"], 3 * (t * KT + m))
                    pe.wait_ge(S["dve_mask"], 2 * (t * KT + m) + 2)
                    pe.wait_ge(S["gps_mask"], 2 * (t * KT + m) + 2)
                    for b in range(TB):
                        for j in range(4):
                            at = ((b % 2) * 4 + j) * (HD + 1)
                            last = nc.tensor.matmul(ps_o[:, b // 2, at:at + HD + 1], weights[:, j, b * P:(b + 1) * P],
                                                    v[:, b, 4 * m + j], start=True, stop=True)
                    last.then_inc(S["av_done"], 1)

                def o_transposes(m):
                    pe.wait_ge(S["o_ready"], 3 * (t * KT + m) + 3)
                    uses.claim(pe, f"ot{m}")
                    for i in range(TB):
                        last = nc.tensor.transpose(uses.bank(f"ot{m}")[:, i * P:(i + 1) * P], o_nat[:, m % 2, i], ident[:])
                    uses.filled(last, f"ot{m}")

                def out_proj(m):
                    pe.wait_ge(S["oT_split"], t * KT + m + 1)
                    if m == 0:
                        pe.wait_ge(S["square_ready"], (t + 1) * 16)
                    for i in range(TB):
                        part = slice(i * P, (i + 1) * P)
                        last = split3(nc, ps_s[i][:], oT_h[:, m, part], oT_l[:, m, part], w_h[:, O, m], w_l[:, O, m], m == 0, m == KT - 1)
                        if m == KT - 1:
                            last.then_inc(S["out_done"], 1)

                if attend:
                    pe.wait_ge(S["w_split"], 4 * KT)
                    for i in range(TB):
                        values(i)
                    columns("q", Q, 0)
                    columns("k", K, 0)
                if recur:
                    for c in range(KT):
                        keys_transposed(c)
                if attend:
                    for m in range(4):
                        if m < 3:
                            columns("q", Q, m + 1)
                        scores(m)
                        if m < 3:
                            columns("k", K, m + 1)
                        sums(m)
                        weighted(m)
                        if m:
                            o_transposes(m - 1)
                    if more:
                        pe.wait_ge(S["xs_loaded"], t * 16 + 32)
                        for kt in range(KT):
                            uses.claim(pe, f"xt{kt}")
                            for i in range(TB):
                                last = nc.tensor.transpose(uses.bank(f"xt{kt}")[:, i * P:(i + 1) * P], xs[:, i, kt * P:(kt + 1) * P], ident[:])
                            uses.filled(last, f"xt{kt}")
                    out_proj(0)
                    out_proj(1)
                    o_transposes(3)
                    out_proj(2)
                    out_proj(3)
                if recur:
                    for i in range(TB):
                        if i == 0:
                            pe.wait_ge(S["z_ready"], c0 + KT + 1)
                        uses.claim(pe, f"zn{i}")
                        for c in range(KT):
                            last = nc.tensor.transpose(uses.bank(f"zn{i}")[:, c * P:(c + 1) * P], zT[:, c, i], ident[:])
                        uses.filled(last, f"zn{i}")
            rounds(pe, body)


ROUND = 12582912.0


def groups(eng, body):
    body(0, True, False)
    with eng.Fori(1, TG - 1) as t:
        body(t, False, False)
    body(TG - 1, False, True)


def ternary_ffn(nc, w_dram, x4_dram, out_dram):
    with ExitStack() as ctx:
        sb, sem, clear_semaphores = stage_memory(nc, ctx)
        NCH, RAW = 12, 4
        w_raw = sb("f_w_raw", [P, RAW, 4, D])
        gate_up = sb("f_gate_up", [P, 4, 2, KT, D], BF16)
        down = sb("f_down", [P, 4, 4, D], F32R)
        xs, res, magnitude = sb("f_xs", [P, TB, D]), sb("f_res", [P, TB, D]), sb("f_magnitude", [P, TB, D])
        xqT = sb("f_xqT", [P, 2, KT, TOK], BF16)
        scale_row = sb("f_scale_row", [P, 2, TOK])
        g_scaled, silu, prod = sb("f_g_scaled", [P, 2, TOK]), sb("f_silu", [P, 2, TOK]), sb("f_prod", [P, 2, TOK])
        prod_h, prod_l = sb("f_prod_h", [P, 4, TOK], F32R), sb("f_prod_l", [P, 4, TOK], F32R)
        top, scale, scale_inv, y_scale = sb("f_top", [P, TB]), sb("f_scale", [P, TB]), sb("f_scale_inv", [P, TB]), sb("f_y_scale", [P, TB])
        scale_cols = sb("f_scale_cols", [P, TB, P])
        ident, ones, unround = sb("f_ident", [P, P]), sb("f_ones", [P, P]), sb("f_unround", [P, 1])
        ln_in, ln_out = LayerNorm(nc, sb, sem, "f_ln_in", 1e-8), LayerNorm(nc, sb, sem, "f_ln_out", 1e-5)
        ps_y = [ctx.enter_context(nc.psum_tensor(f"f_ps_y{i}", [P, D], F32)) for i in range(TB)]
        ps_g = ctx.enter_context(nc.psum_tensor("f_ps_g", [P, TOK], F32))
        ps_u = [ctx.enter_context(nc.psum_tensor(f"f_ps_u{i}", [P, TOK], F32)) for i in range(2)]
        ps_t = ctx.enter_context(nc.psum_tensor("f_ps_t", [P, TOK], F32))
        w_loaded = [sem(f"f_w_loaded{i}") for i in range(RAW)]
        xs_loaded, res_loaded, out_stored = sem("f_xs_loaded"), sem("f_res_loaded"), sem("f_out_stored")
        ident_ready, const_ready, w_signs = sem("f_ident_ready"), sem("f_const_ready"), sem("f_w_signs")
        xn_ready, magnitude_ready, quant, xq_ready = sem("f_xn_ready"), sem("f_magnitude_ready"), sem("f_quant"), sem("f_xq_ready")
        turned, evacuated = sem("f_turned"), sem("f_evacuated")
        g_done, u_done, y_done = sem("f_g_done"), sem("f_u_done"), sem("f_y_done")
        g_ready, silu_ready, prod_ready, prod_high, prod_split = (
            sem("f_g_ready"), sem("f_silu_ready"), sem("f_prod_ready"), sem("f_prod_high"), sem("f_prod_split"))
        added, y_scale_ready, out_ready = sem("f_added"), sem("f_y_scale_ready"), sem("f_out_ready")
        QUANT = 4 + TB
        TURNS = KT + 1
        TURN_AT = 11
        out_view = out_dram.rearrange("(t b) p d -> t p b d", b=TB)
        parity = lambda t: t % 2 if isinstance(t, int) else t & 1
        ctx.callback(clear_semaphores)
        block = ctx.enter_context(nc.Block())

        @block.sync
        def _(sp):
            sp.dma_start(xs[:], x4_dram[0]).then_inc(xs_loaded, 16)
            for n in range(NCH):
                if n >= RAW:
                    sp.wait_ge(w_signs, n - RAW + 1)
                sp.dma_start(w_raw[:, n % RAW], w_dram[n]).then_inc(w_loaded[n % RAW], 16)

            def body(t, first, last):
                if not last:
                    sp.wait_ge(turned, t * TURNS + KT)
                    sp.dma_start(xs[:], x4_dram[t + 1]).then_inc(xs_loaded, 16)
                if not first:
                    sp.wait_ge(out_ready, t * TB)
                    sp.dma_start(out_view[t - 1], res[:]).then_inc(out_stored, 16)
                    sp.wait_ge(out_stored, t * 16)
                sp.dma_start(res[:], x4_dram[t]).then_inc(res_loaded, 16)
            groups(sp, body)
            sp.wait_ge(out_ready, TG * TB)
            sp.dma_start(out_view[TG - 1], res[:]).then_inc(out_stored, 16)
            sp.wait_ge(out_stored, TG * 16)

        @block.gpsimd
        def _(gps):
            ln_in.constants(gps)
            ln_out.constants(gps)
            gps.memset(ones[:], 1.0).then_inc(const_ready, 1)
            gps.memset(unround[:], -ROUND).then_inc(const_ready, 1)
            make_identity(nc, gps, ident, ident_ready)
            ln_in.power_step(gps, 0)

            def low(n, i):
                gps.wait_ge(prod_high, n + 1)
                gps.tensor_tensor(prod_l[:, i % 4], prod[:, i % 2], prod_h[:, i % 4].bitcast(F32), ALU.subtract).then_inc(prod_split, 1)

            def body(t, first, last):
                for i in range(NB):
                    if not (first and i == 0):
                        low(t * NB + i - 1, i - 1)
                    if not first and i == 4:
                        ln_out.power_step(gps, t - 1)
                    if not last and i == 6:
                        ln_in.power_step(gps, t + 1)
            groups(gps, body)
            low(TG * NB - 1, NB - 1)
            ln_out.power_step(gps, TG - 1)

        @block.scalar
        def _(act):
            def signs(n):
                act.wait_ge(w_loaded[n % RAW], (n // RAW + 1) * 16)
                out = down[:, n // 3] if n % 3 == 2 else gate_up[:, n // 3, n % 3]
                act.activation(out, w_raw[:, n % RAW], ACT.Sign).then_inc(w_signs, 1)

            def magnitudes(t):
                act.wait_ge(xn_ready, (t + 1) * TB)
                act.activation(magnitude[:], xs[:], ACT.Abs).then_inc(magnitude_ready, 1)

            def evacuate(t, k):
                act.wait_ge(turned, t * TURNS + k + 1)
                if k < KT:
                    ins = act.activation(xqT[:, parity(t), k], ps_t[:], ACT.Identity, bias=unround[:, 0:1])
                else:
                    ins = act.activation(scale_row[:, parity(t)], ps_t[:], ACT.Copy)
                ins.then_inc(evacuated, 1)

            def high(n, i, full):
                act.wait_ge(prod_ready, n + 1)
                if full:
                    act.wait_ge(y_done, (n - 3) * TB)
                act.activation(prod_h[:, i % 4], prod[:, i % 2], ACT.Copy).then_inc(prod_high, 1)

            act.wait_ge(const_ready, 2)
            magnitudes(0)
            for n in range(3):
                signs(n)
            for k in range(TURNS):
                evacuate(0, k)

            def body(t, first, last):
                for i in range(NB):
                    n = t * NB + i
                    act.wait_ge(g_ready, n + 1)
                    if not first or i >= 2:
                        act.wait_ge(prod_ready, n - 1)
                    act.activation(silu[:, i % 2], g_scaled[:, i % 2], ACT.Silu).then_inc(silu_ready, 1)
                    if not (first and i == 0):
                        high(n - 1, i - 1, not first or i >= 5)
                    if first and i < 12 and i % 4 < 3:
                        signs(3 + 3 * (i // 4) + i % 4)
                    if not last:
                        if i == 9:
                            magnitudes(t + 1)
                        if i >= TURN_AT:
                            evacuate(t + 1, i - TURN_AT)
            groups(act, body)
            high(TG * NB - 1, NB - 1, True)

        @block.vector
        def _(dve):
            def normalise(t):
                dve.wait_ge(ln_in.rstd_ready, t + 1)
                for i in range(TB):
                    ln_in.apply(dve, xs[:, i], xs[:, i], i).then_inc(xn_ready, 1)

            def scales(t):
                n = t * QUANT
                dve.wait_ge(magnitude_ready, t + 1)
                dve.tensor_reduce(top[:], magnitude[:], AX, ALU.max).then_inc(quant, 1)
                dve.wait_ge(quant, n + 1)
                dve.reciprocal(scale[:], top[:]).then_inc(quant, 1)
                dve.wait_ge(quant, n + 2)
                dve.tensor_scalar(scale[:], scale[:], 127.0, None, ALU.mult).then_inc(quant, 1)
                dve.tensor_scalar(scale_inv[:], top[:], 1.0 / 127.0, None, ALU.mult).then_inc(quant, 1)
                dve.wait_ge(quant, n + 4)
                for i in range(TB):
                    if i == 0 and not (isinstance(t, int) and t == 0):
                        dve.wait_ge(turned, t * TURNS)
                    dve.tensor_scalar(scale_cols[:, i], ones[:], scale_inv[:, i:i + 1], None, ALU.mult).then_inc(quant, 1)

            def quantise(t):
                for i in range(TB):
                    dve.tensor_scalar(xs[:, i], xs[:, i], scale[:, i:i + 1], ROUND, ALU.mult, ALU.add).then_inc(xq_ready, 1)
                dve.wait_ge(xq_ready, t * 2 * TB + TB)
                for i in range(TB):
                    dve.tensor_scalar(xs[:, i], xs[:, i], ROUND + 127.0, ROUND - 128.0, ALU.min, ALU.max).then_inc(xq_ready, 1)

            def product(n, i):
                dve.wait_ge(u_done, n + 1)
                dve.wait_ge(silu_ready, n + 1)
                if not isinstance(n, int) or n >= 2:
                    dve.wait_ge(prod_split, n - 1)
                dve.tensor_tensor(prod[:, i % 2], silu[:, i % 2], ps_u[i % 2][:], ALU.mult).then_inc(prod_ready, 1)

            def residual(t):
                dve.wait_ge(res_loaded, t * 16 + 16)
                dve.wait_ge(y_scale_ready, t + 1)
                for i in range(TB):
                    dve.wait_ge(y_done, (t * NB + NB - 1) * TB + i + 1)
                    dve.scalar_tensor_tensor(res[:, i], ps_y[i][:], y_scale[:, i:i + 1], res[:, i], ALU.mult, ALU.add).then_inc(added, 1)

            def out_statistics(t):
                dve.wait_ge(added, t * TB + TB)
                ln_out.statistics(dve, lambda i: res[:, i], t)

            def out_apply(t):
                dve.wait_ge(ln_out.rstd_ready, t + 1)
                for i in range(TB):
                    ln_out.apply(dve, res[:, i], res[:, i], i).then_inc(out_ready, 1)

            dve.wait_ge(xs_loaded, 16)
            ln_in.statistics(dve, lambda i: xs[:, i], 0)
            normalise(0)
            dve.wait_ge(const_ready, 2)
            scales(0)
            quantise(0)

            def body(t, first, last):
                for i in range(NB):
                    n = t * NB + i
                    if not first and i == 2:
                        residual(t - 1)
                    if i == 0:
                        dve.wait_ge(evacuated, t * TURNS + TURNS)
                    dve.wait_ge(g_done, n + 1)
                    if not first or i >= 2:
                        dve.wait_ge(silu_ready, n - 1)
                    dve.tensor_tensor(g_scaled[:, i % 2], ps_g[:], scale_row[:, parity(t)], ALU.mult).then_inc(g_ready, 1)
                    if not (first and i == 0):
                        product(n - 1, i - 1)
                    if i == 3:
                        if not first:
                            dve.wait_ge(added, t * TB)
                        dve.tensor_copy(y_scale[:], scale_inv[:]).then_inc(y_scale_ready, 1)
                        if not first:
                            out_statistics(t - 1)
                    if not first and i == 5:
                        out_apply(t - 1)
                    if not last:
                        if i == 6:
                            dve.wait_ge(xs_loaded, t * 16 + 32)
                            ln_in.statistics(dve, lambda i: xs[:, i], t + 1)
                        if i == 8:
                            normalise(t + 1)
                        if i == 10:
                            dve.wait_ge(y_scale_ready, t + 1)
                            scales(t + 1)
                            quantise(t + 1)
            groups(dve, body)
            product(TG * NB - 1, NB - 1)
            residual(TG - 1)
            out_statistics(TG - 1)
            out_apply(TG - 1)

        @block.tensor
        def _(pe):
            def turn(t, k):
                if k == 0:
                    pe.wait_ge(xq_ready, (t + 1) * 2 * TB)
                if not (isinstance(t, int) and t == 0 and k == 0):
                    pe.wait_ge(evacuated, t * TURNS + k)
                if k == KT:
                    pe.wait_ge(quant, (t + 1) * QUANT)
                for i in range(TB):
                    source = xs[:, i, k * P:(k + 1) * P] if k < KT else scale_cols[:, i]
                    done = nc.tensor.transpose(ps_t[:, i * P:(i + 1) * P], source, ident[:])
                done.then_inc(turned, 1)

            def hidden(t, i):
                n = t * NB + i
                part = slice((i % 4) * P, (i % 4 + 1) * P)
                if not isinstance(t, int) or n >= 1:
                    pe.wait_ge(g_ready, n)
                for kt in range(KT):
                    if i == 0 and kt == 0:
                        pe.wait_ge(evacuated, t * TURNS + KT)
                    if kt == 0:
                        pe.wait_ge(w_signs, 3 * (i // 4) + 1)
                    done = nc.tensor.matmul(ps_g[:], gate_up[:, i // 4, 0, kt, part], xqT[:, parity(t), kt], start=kt == 0, stop=kt == KT - 1)
                done.then_inc(g_done, 1)
                if not isinstance(t, int) or n >= 2:
                    pe.wait_ge(prod_ready, n - 1)
                for kt in range(KT):
                    if kt == 0:
                        pe.wait_ge(w_signs, 3 * (i // 4) + 2)
                    done = nc.tensor.matmul(ps_u[i % 2][:], gate_up[:, i // 4, 1, kt, part], xqT[:, parity(t), kt], start=kt == 0, stop=kt == KT - 1)
                done.then_inc(u_done, 1)

            def back(t, i, first):
                pe.wait_ge(prod_split, t * NB + i + 1)
                pe.wait_ge(w_signs, 3 * (i // 4) + 3)
                for b in range(TB):
                    if i == 0 and not first:
                        pe.wait_ge(added, (t - 1) * TB + b + 1)
                    part = slice(b * P, (b + 1) * P)
                    nc.tensor.matmul(ps_y[b][:], prod_h[:, i % 4, part], down[:, i // 4, i % 4], start=i == 0, stop=False)
                    nc.tensor.matmul(ps_y[b][:], prod_l[:, i % 4, part], down[:, i // 4, i % 4], start=False, stop=i == NB - 1).then_inc(y_done, 1)

            pe.wait_ge(ident_ready, 2)
            for k in range(TURNS):
                turn(0, k)

            def body(t, first, last):
                for i in range(NB):
                    hidden(t, i)
                    if not last and i >= TURN_AT:
                        turn(t + 1, i - TURN_AT)
                    if i >= 2:
                        back(t, i - 2, first)
                    elif not first:
                        back(t - 1, NB - 2 + i, False)
            groups(pe, body)
            back(TG - 1, NB - 2, False)
            back(TG - 1, NB - 1, False)


def decoder(nc, x_dram, xT_dram, w_attn_dram, ctxT_dram, w_cross_dram, bg_dram, w_ffn_dram, wr_dram, br_dram,
            w_powered_dram, gamma_dram, beta_dram, wu_dram, w_ternary_dram, out_dram):
    x1_dram, x2_dram, x4_dram = (nc.dram_tensor(name, (TG, P, TB, D), F32, kind="Internal").ap()
                                 for name in ("x1_dram", "x2_dram", "x4_dram"))
    with nc.sbuf_tensor("acc", [P, TG * TB, D], F32) as acc:
        self_attention(nc, x_dram, xT_dram, w_attn_dram, acc)
        linear_cross_attention(nc, ctxT_dram, w_cross_dram, bg_dram, acc, x1_dram)
    blockwise_ffn(nc, w_ffn_dram, wr_dram, br_dram, x1_dram, x2_dram)
    powered_attention_and_wkv(nc, x2_dram, ctxT_dram, w_powered_dram, gamma_dram, beta_dram, wu_dram, x4_dram)
    ternary_ffn(nc, w_ternary_dram, x4_dram, out_dram)


def kernel(**inputs):
    import numpy as np
    import concourse.bacc as bacc
    from concourse.bass_utils import run_bass_kernel_spmd

    a = {name: np.asarray(value) for name, value in inputs.items()}

    def rows_by_input(w):
        return w.reshape(-1, 4, 128).transpose(2, 1, 0)

    def columns_of(x):
        return x.reshape(4, 512, 4, 128).transpose(0, 3, 2, 1)

    def hidden_rows(w):
        return w.reshape(4, 512, 4, 128).transpose(0, 3, 2, 1)

    def hidden_columns(w):
        return w.reshape(512, 4, 4, 128).transpose(1, 3, 2, 0)

    qkv = a["L0_attn_w_qkv"].reshape(3, 4, 512, 4, 128)[[2, 0, 1]].transpose(1, 0, 4, 3, 2).reshape(4, 3, 128, 2048)
    w_out = hidden_columns(a["L0_attn_w_out"]).reshape(4, 1, 128, 2048)
    wk, wv = a["L0_xattn_Wkv"][:512], a["L0_xattn_Wkv"][512:]
    arrays = {
        "x": a["x"].transpose(1, 0, 2),
        "xT": columns_of(a["x"]),
        "w_attn": np.concatenate([qkv, w_out], 1),
        "ctxT": columns_of(a["ctx_2048"]),
        "w_cross": np.stack([rows_by_input(w) for w in (wk, wv, a["L0_xattn_Wq"], a["L0_xattn_Wg"], a["L0_xattn_Wo"])]),
        "bg": a["L0_xattn_bg"].reshape(4, 128).T,
        "w_ffn": np.stack([hidden_rows(a["L0_ffn_W1"]), hidden_columns(a["L0_ffn_W2"])], 1).reshape(8, 128, 4, 512),
        "wr": rows_by_input(a["L0_ffn_Wr"]),
        "br": a["L0_ffn_br"].reshape(16, 1),
        "w_powered": np.stack([rows_by_input(a["L1_attn_W" + c]) for c in "qkvo"]),
        "gamma": a["L1_attn_gamma"],
        "beta": a["L1_attn_beta"],
        "wu": np.stack([a["L1_xattn_w"], a["L1_xattn_u"]]).reshape(2, 4, 128).transpose(2, 0, 1),
        "w_ternary": np.stack([hidden_rows(a["L1_ffn_W_g"]), hidden_rows(a["L1_ffn_W_u"]), hidden_columns(a["L1_ffn_W_d"])],
                              1).reshape(12, 128, 4, 512),
    }
    nc = bacc.Bacc("TRN2", target_bir_lowering=False, num_devices=1)
    feed, args = {}, []
    for name, value in arrays.items():
        value = np.ascontiguousarray(value)
        feed[f"in_{name}_dram"] = value
        args.append(nc.dram_tensor(f"in_{name}_dram", value.shape, mybir.dt.from_np(value.dtype), kind="ExternalInput").ap())
    args.append(nc.dram_tensor("out_0_dram", (16, 128, 512), F32, kind="ExternalOutput").ap())
    decoder(nc, *args)
    result = run_bass_kernel_spmd(nc, [feed], core_ids=[0])
    return result.results[0]["out_0_dram"]
```

```python
from contextlib import ExitStack
import concourse.bass as bass
from concourse import mybir
P = 128
F32 = mybir.dt.float32
F32R = mybir.dt.float32r
BF16 = mybir.dt.bfloat16
ALU = mybir.AluOpType
ACT = mybir.ActivationFunctionType
AX = mybir.AxisListType.X
D = 512
KT = D // P
HG = 4
GROUPS = 4
TB = 4
TG = 4
TOK = TB * P


def stage_memory(nc, ctx):
    used = []

    def clear():
        with nc.Block() as block:
            @block.gpsimd
            def _(gps):
                for semaphore in used:
                    gps.sem_clear(semaphore)

    def sb(name, shape, dt=F32):
        return ctx.enter_context(nc.sbuf_tensor(name, shape, dt))

    def sem(name):
        used.append(ctx.enter_context(nc.semaphore(name)))
        return used[-1]

    return sb, sem, clear


def split3(nc, out, st_h, st_l, mv_h, mv_l, first, last):
    nc.tensor.matmul(out, st_h, mv_h, start=first, stop=False)
    nc.tensor.matmul(out, st_h, mv_l, start=False, stop=False)
    return nc.tensor.matmul(out, st_l, mv_h, start=False, stop=last)


def make_identity(nc, gps, ident, ready):
    gps.memset(ident[:], 0.0).then_inc(ready, 1)
    gps.wait_ge(ready, 1)
    gps.affine_select(out=ident[:], in_=ident[:], compare_op=ALU.not_equal, fill=1.0, base=0,
                      pattern=[[-1, P]], channel_multiplier=1).then_inc(ready, 1)


def self_attention(nc, x_dram, xT_dram, w_dram, acc):
    with ExitStack() as ctx:
        sb, sem, clear_semaphores = stage_memory(nc, ctx)
        w_raw = sb("a_w_raw", [P, 4, KT * D])
        w_h = sb("a_w_h", [P, 4, KT, D], F32R)
        w_l = sb("a_w_l", [P, 4, KT, D], F32R)
        xT_raw = sb("a_xT_raw", [P, KT, TOK])
        xT_h = sb("a_xT_h", [P, KT, TOK], F32R)
        xT_l = sb("a_xT_l", [P, KT, TOK], F32R)
        qT = sb("a_qT", [P, 2, TOK])
        kT = sb("a_kT", [P, 2, TOK])
        v = sb("a_v", [P, TB, D])
        probs = sb("a_probs", [P, 2, TB, P])
        probsT = sb("a_probsT", [P, TOK])
        oT_h = sb("a_oT_h", [P, HG, TOK], F32R)
        oT_l = sb("a_oT_l", [P, HG, TOK], F32R)
        ident = sb("a_ident", [P, P])
        rowmax = sb("a_rowmax", [P, 2, TB])
        negmax = sb("a_negmax", [P, 2, TB])
        rowsum = sb("a_rowsum", [P, 2, TB])
        rowinv = sb("a_rowinv", [P, 2, TB])
        ring = [ctx.enter_context(nc.psum_tensor(f"a_ring{i}", [P, D], F32)) for i in range(4)]
        ps_s = [ctx.enter_context(nc.psum_tensor(f"a_ps_s{i}", [P, TOK], F32)) for i in range(2)]
        ps_t = ctx.enter_context(nc.psum_tensor("a_ps_t", [P, TOK], F32))
        ps_o = ctx.enter_context(nc.psum_tensor("a_ps_o", [P, TOK], F32))
        x_loaded, w_loaded, xT_loaded = sem("a_x_loaded"), [sem(f"a_w_loaded{c}") for c in range(4)], sem("a_xT_loaded")
        ident_ready = sem("a_ident_ready")
        w_high, w_split, sp_waited = sem("a_w_high"), sem("a_w_split"), sem("a_sp_waited")
        xT_high, xT_split = sem("a_xT_high"), sem("a_xT_split")
        v_done, q_done, k_done, s_done = sem("a_v_done"), sem("a_q_done"), sem("a_k_done"), sem("a_s_done")
        t_done, o_done, out_done = sem("a_t_done"), sem("a_o_done"), sem("a_out_done")
        v_ready, q_ready, k_ready = sem("a_v_ready"), sem("a_q_ready"), sem("a_k_ready")
        max_ready, negmax_ready, exp_ready, inv_ready, probs_ready = (
            sem("a_max_ready"), sem("a_negmax_ready"), sem("a_exp_ready"), sem("a_inv_ready"), sem("a_probs_ready"))
        probsT_ready, o_high, o_split, added = sem("a_probsT_ready"), sem("a_o_high"), sem("a_o_split"), sem("a_added")
        V, Q, K, O = range(4)
        SCALE = float(P) ** -0.5
        ctx.callback(clear_semaphores)
        block = ctx.enter_context(nc.Block())

        @block.sync
        def _(sp):
            sp.dma_start(xT_raw[:], xT_dram[0]).then_inc(xT_loaded, 16)
            for c in range(4):
                sp.dma_start(w_raw[:, c], w_dram[0, c]).then_inc(w_loaded[c], 16)
            sp.dma_start(acc[:], x_dram).then_inc(x_loaded, 16)
            with sp.Fori(0, GROUPS) as g:
                with sp.Fori(0, TG) as t:
                    sp.wait_ge(xT_split, (g * TG + t) * KT + KT)
                    sp.sem_inc(sp_waited, 1)
                    sp.dma_start(xT_raw[:], xT_dram[(t + 1) % TG if isinstance(t, int) else (t + 1) & 3]).then_inc(xT_loaded, 16)
                for c in range(4):
                    sp.wait_ge(w_split, g * 4 * KT + (c + 1) * KT)
                    sp.sem_inc(sp_waited, 1)
                    sp.dma_start(w_raw[:, c], w_dram[(g + 1) & 3, c]).then_inc(w_loaded[c], 16)
            for c in range(4):
                sp.wait_ge(w_loaded[c], (GROUPS + 1) * 16)

        @block.gpsimd
        def _(gps):
            make_identity(nc, gps, ident, ident_ready)
            with gps.Fori(0, GROUPS) as g:
                for c in range(4):
                    for kt in range(KT):
                        gps.wait_ge(w_high, g * 4 * KT + c * KT + kt + 1)
                        gps.tensor_tensor(w_l[:, c, kt], w_raw[:, c, kt * D:(kt + 1) * D],
                                          w_h[:, c, kt].bitcast(F32), ALU.subtract).then_inc(w_split, 1)

        @block.scalar
        def _(act):
            act.wait_ge(xT_loaded, 16)
            for kt in range(KT):
                act.activation(xT_h[:, kt], xT_raw[:, kt], ACT.Copy).then_inc(xT_high, 1)
            with act.Fori(0, GROUPS) as g:
                for c, (freed, per) in enumerate(((v_done, 16), (q_done, 16), (k_done, 16), (out_done, 16))):
                    act.wait_ge(w_loaded[c], g * 16 + 16)
                    act.wait_ge(freed, g * per + 1)
                    for kt in range(KT):
                        act.activation(w_h[:, c, kt], w_raw[:, c, kt * D:(kt + 1) * D], ACT.Copy).then_inc(w_high, 1)
                with act.Fori(0, TG) as t:
                    s = g * TG + t

                    def q_evac(j):
                        act.wait_ge(q_done, s * HG + j + 2)
                        act.activation(qT[:, j % 2], ring[2 * (j % 2)][:], ACT.Copy).then_inc(q_ready, 1)

                    def exps(j):
                        act.wait_ge(negmax_ready, s * HG + j + 1)
                        for b in range(TB):
                            last = act.activation(probs[:, j % 2, b], ps_s[j % 2][:, b * P:(b + 1) * P], ACT.Exp,
                                                  bias=negmax[:, j % 2, b:b + 1], scale=SCALE,
                                                  accum_out=rowsum[:, j % 2, b:b + 1])
                        last.then_inc(exp_ready, 1)

                    def probsT_evac(j):
                        act.wait_ge(t_done, s * HG + j + 1)
                        act.activation(probsT[:], ps_t[:], ACT.Copy).then_inc(probsT_ready, 1)

                    def o_evac(j):
                        act.wait_ge(o_done, s * HG + j + 1)
                        act.activation(oT_h[:, j], ps_o[:], ACT.Copy).then_inc(o_high, 1)

                    for i in range(TB):
                        act.wait_ge(v_done, s * TB + i + 2)
                        act.activation(v[:, i], ring[i][:], ACT.Copy).then_inc(v_ready, 1)
                    q_evac(0)
                    exps(0)
                    for j in range(1, HG):
                        q_evac(j)
                        probsT_evac(j - 1)
                        o_evac(j - 1)
                        exps(j)
                    act.wait_ge(xT_loaded, s * 16 + 32)
                    act.wait_ge(k_done, s * HG + HG + 1)
                    for kt in range(KT):
                        act.activation(xT_h[:, kt], xT_raw[:, kt], ACT.Copy).then_inc(xT_high, 1)
                    probsT_evac(HG - 1)
                    o_evac(HG - 1)

        @block.vector
        def _(dve):
            def low_parts(s):
                for kt in range(KT):
                    dve.wait_ge(xT_high, s * KT + kt + 1)
                    dve.tensor_tensor(xT_l[:, kt], xT_raw[:, kt], xT_h[:, kt].bitcast(F32), ALU.subtract).then_inc(xT_split, 1)
            dve.sem_inc(added, TB)
            low_parts(0)
            dve.wait_ge(x_loaded, 16)
            with dve.Fori(0, GROUPS) as g:
                with dve.Fori(0, TG) as t:
                    s = g * TG + t

                    def k_evac(j):
                        dve.wait_ge(k_done, s * HG + j + 2)
                        dve.tensor_copy(kT[:, j % 2], ring[2 * (j % 2) + 1][:]).then_inc(k_ready, 1)

                    def softmax(j):
                        n = s * HG + j + 1
                        dve.wait_ge(s_done, n)
                        dve.tensor_reduce(rowmax[:, j % 2], ps_s[j % 2][:].rearrange("p (b k) -> p b k", b=TB), AX, ALU.max).then_inc(max_ready, 1)
                        dve.wait_ge(max_ready, n)
                        dve.tensor_scalar(negmax[:, j % 2], rowmax[:, j % 2], -SCALE, None, ALU.mult).then_inc(negmax_ready, 1)
                        dve.wait_ge(exp_ready, n)
                        dve.reciprocal(rowinv[:, j % 2], rowsum[:, j % 2]).then_inc(inv_ready, 1)
                        dve.wait_ge(inv_ready, n)
                        dve.tensor_tensor(probs[:, j % 2], probs[:, j % 2],
                                          rowinv[:, j % 2].unsqueeze(2).broadcast_to([P, TB, P]), ALU.mult).then_inc(probs_ready, 1)

                    def o_low(j):
                        dve.wait_ge(o_high, s * HG + j + 1)
                        dve.tensor_tensor(oT_l[:, j], ps_o[:], oT_h[:, j].bitcast(F32), ALU.subtract).then_inc(o_split, 1)

                    k_evac(0)
                    softmax(0)
                    for j in range(1, HG):
                        k_evac(j)
                        o_low(j - 1)
                        softmax(j)
                    low_parts(s + 1)
                    o_low(HG - 1)
                    for i in range(TB):
                        dve.wait_ge(out_done, s * TB + i + 2)
                        dve.tensor_tensor(acc[:, t * TB + i], acc[:, t * TB + i], ring[i][:], ALU.add).then_inc(added, 1)

        @block.tensor
        def _(pe):
            for freed in (v_done, q_done, k_done, out_done):
                pe.sem_inc(freed, 1)
            pe.wait_ge(ident_ready, 2)
            with pe.Fori(0, GROUPS) as g:
                with pe.Fori(0, TG) as t:
                    s = g * TG + t

                    def project(c, j, ks, bank, done):
                        for kt in ks:
                            cols = slice(j * P, (j + 1) * P)
                            last = split3(nc, bank[:], w_h[:, c, kt, cols], w_l[:, c, kt, cols],
                                          xT_h[:, kt], xT_l[:, kt], kt == 0, kt == KT - 1)
                        if ks[-1] == KT - 1:
                            last.then_inc(done, 1)

                    def scores(j):
                        pe.wait_ge(q_ready, s * HG + j + 1)
                        pe.wait_ge(k_ready, s * HG + j + 1)
                        for b in range(TB):
                            c = slice(b * P, (b + 1) * P)
                            last = nc.tensor.matmul(ps_s[j % 2][:, c], qT[:, j % 2, c], kT[:, j % 2, c], start=True, stop=True)
                        last.then_inc(s_done, 1)

                    def transposes(j):
                        pe.wait_ge(probs_ready, s * HG + j + 1)
                        for b in range(TB):
                            last = nc.tensor.transpose(ps_t[:, b * P:(b + 1) * P], probs[:, j % 2, b], ident[:])
                        last.then_inc(t_done, 1)

                    def weighted(j):
                        pe.wait_ge(probsT_ready, s * HG + j + 1)
                        if j:
                            pe.wait_ge(o_split, s * HG + j)
                        for b in range(TB):
                            c = slice(b * P, (b + 1) * P)
                            last = nc.tensor.matmul(ps_o[:, c], v[:, b, j * P:(j + 1) * P], probsT[:, c], start=True, stop=True)
                        last.then_inc(o_done, 1)

                    def out_proj(j, tiles):
                        pe.wait_ge(o_split, s * HG + j + 1)
                        if j == 0:
                            pe.wait_ge(w_split, g * 4 * KT + 4 * KT)
                        for i in tiles:
                            if j == 0:
                                pe.wait_ge((q_ready, k_ready)[i % 2], s * HG + 3 + i // 2)
                            c = slice(i * P, (i + 1) * P)
                            last = split3(nc, ring[i][:], oT_h[:, j, c], oT_l[:, j, c],
                                          w_h[:, O, j], w_l[:, O, j], j == 0, j == HG - 1)
                            if j == HG - 1:
                                last.then_inc(out_done, 1)

                    for i in range(TB):
                        for kt in range(KT):
                            if i == 0:
                                pe.wait_ge(xT_split, s * KT + kt + 1)
                                pe.wait_ge(w_split, g * 4 * KT + kt + 1)
                            if kt == 0:
                                pe.wait_ge(added, s * TB + i + 1)
                            c = slice(i * P, (i + 1) * P)
                            last = split3(nc, ring[i][:], xT_h[:, kt, c], xT_l[:, kt, c],
                                          w_h[:, V, kt], w_l[:, V, kt], kt == 0, kt == KT - 1)
                        last.then_inc(v_done, 1)
                    for j in range(HG):
                        if j == 0:
                            pe.wait_ge(w_split, g * 4 * KT + 2 * KT)
                        if j < 2:
                            pe.wait_ge(v_ready, s * TB + 2 * j + 1)
                        else:
                            pe.wait_ge(q_ready, s * HG + j - 1)
                        project(Q, j, range(KT), ring[2 * (j % 2)], q_done)
                        if j == 0:
                            pe.wait_ge(w_split, g * 4 * KT + 3 * KT)
                        if j < 2:
                            pe.wait_ge(v_ready, s * TB + 2 * j + 2)
                        else:
                            pe.wait_ge(k_ready, s * HG + j - 1)
                        project(K, j, range(KT // 2), ring[2 * (j % 2) + 1], k_done)
                        if j:
                            transposes(j - 1)
                        project(K, j, range(KT // 2, KT), ring[2 * (j % 2) + 1], k_done)
                        if j:
                            weighted(j - 1)
                        scores(j)
                    out_proj(0, range(TB))
                    out_proj(1, range(TB))
                    transposes(HG - 1)
                    out_proj(2, range(TB // 2))
                    weighted(HG - 1)
                    out_proj(2, range(TB // 2, TB))
                    out_proj(3, range(TB))


class LayerNorm:

    def __init__(self, nc, sb, sem, name, eps, count=TB):
        self.nc, self.eps, self.count = nc, eps, count
        self.stats, self.moments = sb(f"{name}_stats", [P, count, 6]), sb(f"{name}_moments", [P, count, 2])
        self.var_eps, self.rstd, self.power = sb(f"{name}_var_eps", [P, count]), sb(f"{name}_rstd", [P, count]), sb(f"{name}_power", [P, count])
        self.stats_ready, self.moments_ready = sem(f"{name}_stats_ready"), sem(f"{name}_moments_ready")
        self.var_ready, self.rstd_ready = sem(f"{name}_var_ready"), sem(f"{name}_rstd_ready")
        self.power_ready, self.waited = sem(f"{name}_power_ready"), sem(f"{name}_waited")

    def constants(self, gps):
        gps.memset(self.power[:], -0.5).then_inc(self.power_ready, 1)
        gps.wait_ge(self.power_ready, 1)

    def statistics(self, dve, rows, n):
        for i in range(self.count):
            dve.bn_stats(self.stats[:, i], rows(i)).then_inc(self.stats_ready, 1)
        dve.wait_ge(self.stats_ready, n * self.count + self.count)
        dve.sem_inc(self.waited, 1)
        for i in range(self.count):
            dve.bn_aggr(self.moments[:, i], self.stats[:, i]).then_inc(self.moments_ready, 1)
        dve.wait_ge(self.moments_ready, n * self.count + self.count)
        dve.tensor_scalar(self.var_eps[:], self.moments[:, :, 1], self.eps, None, ALU.add).then_inc(self.var_ready, 1)

    def power_step(self, gps, n):
        gps.wait_ge(self.var_ready, n + 1)
        gps.tensor_tensor(self.rstd[:], self.var_eps[:], self.power[:], ALU.pow).then_inc(self.rstd_ready, 1)

    def apply(self, dve, out, row, i):
        return dve.tensor_scalar(out, row, self.moments[:, i, 0:1], self.rstd[:, i:i + 1], ALU.subtract, ALU.mult)


def linear_cross_attention(nc, ctxT_dram, w_dram, bg_dram, acc, x1_dram):
    with ExitStack() as ctx:
        sb, sem, clear_semaphores = stage_memory(nc, ctx)
        K, V, Q, G, O = range(5)
        w_h, w_l = sb("b_w_h", [P, 5, KT, D], F32R), sb("b_w_l", [P, 5, KT, D], F32R)
        c_raw = sb("b_c_raw", [P, KT, TOK])
        xs = c_raw
        c_h, c_l = sb("b_c_h", [P, KT, TOK], F32R), sb("b_c_l", [P, KT, TOK], F32R)
        xT_h, xT_l = sb("b_xT_h", [P, KT, TOK], F32R), sb("b_xT_l", [P, KT, TOK], F32R)
        kf, vs = sb("b_kf", [P, 2, D]), sb("b_v", [P, 2, D])
        low = sb("b_low", [P, 2, D])
        kv_blocks, ks_blocks = sb("b_kv_blocks", [P, TB, KT, P]), sb("b_ks_blocks", [P, TB, KT, P])
        qf_gate = sb("b_qf_gate", [P, 4, TOK])
        qf, gate = qf_gate[:, 0:2], qf_gate[:, 2:4]
        a_h, a_l = sb("b_a_h", [P, KT, TOK], F32R), sb("b_a_l", [P, KT, TOK], F32R)
        w_raw = [kv_blocks[:].rearrange("p b m e -> p b (m e)"), ks_blocks[:].rearrange("p b m e -> p b (m e)"),
                 qf_gate, qf_gate, qf_gate]
        bg, nbg = sb("b_bg", [P, KT]), sb("b_nbg", [P, KT])
        ident, blocks, ones = sb("b_ident", [P, P]), sb("b_blocks", [P, P]), sb("b_ones", [P, 1])
        ln_in, ln_out = LayerNorm(nc, sb, sem, "b_ln_in", 1e-5), LayerNorm(nc, sb, sem, "b_ln_out", 1e-5)
        bank = [ctx.enter_context(nc.psum_tensor(f"b_bank{i}", [P, D], F32)) for i in range(8)]
        w_loaded = [sem(f"b_w_loaded{c}") for c in range(5)]
        bg_loaded, c_loaded, x1_stored = sem("b_bg_loaded"), sem("b_c_loaded"), sem("b_x1_stored")
        ident_ready, blocks_ready, nbg_ready = sem("b_ident_ready"), sem("b_blocks_ready"), sem("b_nbg_ready")
        w_high, w_split, c_high, c_split = sem("b_w_high"), sem("b_w_split"), sem("b_c_high"), sem("b_c_split")
        xs_ready, x_kept, xT_done, xT_high, xT_split = (
            sem("b_xs_ready"), sem("b_x_kept"), sem("b_xT_done"), sem("b_xT_high"), sem("b_xT_split"))
        k_done, v_done, kv_done, q_done, g_done, nd_done, out_done = (
            sem("b_k_done"), sem("b_v_done"), sem("b_kv_done"), sem("b_q_done"), sem("b_g_done"), sem("b_nd_done"), sem("b_out_done"))
        k_min, k_exp, k_ready, v_ready, kv_ready = sem("b_k_min"), sem("b_k_exp"), sem("b_k_ready"), sem("b_v_ready"), sem("b_kv_ready")
        q_min, q_exp, q_ready, g_exp, g_ready = sem("b_q_min"), sem("b_q_exp"), sem("b_q_ready"), sem("b_g_exp"), sem("b_g_ready")
        den_ready, inv_ready, a_ready, a_high, a_split = (
            sem("b_den_ready"), sem("b_inv_ready"), sem("b_a_ready"), sem("b_a_high"), sem("b_a_split"))
        added, x1_ready = sem("b_added"), sem("b_x1_ready")
        waited, sp_waited = sem("b_waited"), sem("b_sp_waited")
        EPS = 1e-6
        ctx.callback(clear_semaphores)
        block = ctx.enter_context(nc.Block())

        def steps(eng, body):
            body(0, True, True)
            with eng.Fori(1, TG - 1) as t:
                body(t, False, True)
            body(TG - 1, False, False)

        @block.sync
        def _(sp):
            sp.dma_start(c_raw[:], ctxT_dram[0]).then_inc(c_loaded, 16)
            sp.dma_start(bg[:], bg_dram).then_inc(bg_loaded, 16)
            for c in range(5):
                if c > Q:
                    sp.wait_ge(w_split, c * KT)
                sp.dma_start(w_raw[c][:], w_dram[c]).then_inc(w_loaded[c], 16)

            def body(t, first, more):
                if more:
                    sp.wait_ge(xT_done, t * KT + KT)
                    sp.sem_inc(sp_waited, 1)
                    sp.wait_ge(x_kept, t + 1)
                    sp.sem_inc(sp_waited, 1)
                    sp.dma_start(c_raw[:], ctxT_dram[t + 1]).then_inc(c_loaded, 16)
                sp.wait_ge(x1_ready, t * TB + TB)
                sp.sem_inc(sp_waited, 1)
                sp.dma_start(x1_dram[t], acc[:, bass.ds(t * TB, TB)] if not isinstance(t, int) else acc[:, t * TB:t * TB + TB]).then_inc(x1_stored, 16)
            steps(sp, body)
            sp.wait_ge(x1_stored, TG * 16)

        @block.gpsimd
        def _(gps):
            ln_in.constants(gps)
            ln_out.constants(gps)
            make_identity(nc, gps, ident, ident_ready)
            gps.memset(ones[:], 1.0).then_inc(blocks_ready, 1)
            gps.memset(blocks[:], 0.0).then_inc(blocks_ready, 1)
            gps.wait_ge(blocks_ready, 2)
            for h in range(4):
                gps.memset(blocks[32 * h:32 * h + 32, 32 * h:32 * h + 32], 1.0).then_inc(blocks_ready, 1)
            gps.wait_ge(blocks_ready, 6)

            def context_low(t):
                for kt in range(KT):
                    gps.wait_ge(c_high, t * KT + kt + 1)
                    gps.tensor_tensor(c_l[:, kt], c_raw[:, kt], c_h[:, kt].bitcast(F32), ALU.subtract).then_inc(c_split, 1)

            ln_in.power_step(gps, 0)
            context_low(0)

            def body(t, first, more):
                if more:
                    ln_in.power_step(gps, t + 1)
                    context_low(t + 1)
                for m in range(KT):
                    gps.wait_ge(a_high, t * KT + m + 1)
                    gps.tensor_tensor(a_l[:, m], gate[:, m % 2], a_h[:, m].bitcast(F32), ALU.subtract).then_inc(a_split, 1)
                ln_out.power_step(gps, t)
            steps(gps, body)

        @block.scalar
        def _(act):
            def w_chunk(c):
                act.wait_ge(w_loaded[c], 16)
                for kt in range(KT):
                    act.activation(w_h[:, c, kt], w_raw[c][:, kt], ACT.Copy).then_inc(w_high, 1)

            def context_high(t):
                act.wait_ge(c_loaded, t * 16 + 16)
                for kt in range(KT):
                    act.activation(c_h[:, kt], c_raw[:, kt], ACT.Copy).then_inc(c_high, 1)

            def keep_x(t):
                act.wait_ge(xs_ready, t * TB + TB)
                act.activation(acc[:, bass.ds(t * TB, TB)], xs[:], ACT.Copy).then_inc(x_kept, 1)

            def xT_highs(t, kts):
                for kt in kts:
                    act.wait_ge(xT_done, t * KT + kt + 1)
                    act.activation(xT_h[:, kt], bank[4 + kt % 2][:], ACT.Copy).then_inc(xT_high, 1)

            context_high(0)
            w_chunk(K)
            w_chunk(V)

            def body(t, first, more):
                def a_highs(m):
                    act.wait_ge(a_ready, t * KT + m + 1)
                    act.activation(a_h[:, m], gate[:, m % 2], ACT.Copy).then_inc(a_high, 1)

                for i in range(TB):
                    act.wait_ge(k_min, t * TB + i + 1)
                    act.activation(low[:, i % 2], low[:, i % 2], ACT.Exp).then_inc(k_exp, 1)
                    if first and i == 0:
                        xT_highs(0, (0, 1))
                    act.wait_ge(v_done, t * TB + i + 1)
                    act.activation(vs[:, i % 2], bank[2 + i % 2][:], ACT.Copy).then_inc(v_ready, 1)
                    if first and i == 0:
                        xT_highs(0, (2, 3))
                        keep_x(0)
                    if first and i < 3:
                        w_chunk((Q, G, O)[i])
                if more:
                    context_high(t + 1)
                for m in range(KT):
                    act.wait_ge(q_min, t * KT + m + 1)
                    act.activation(low[:, m % 2], low[:, m % 2], ACT.Exp).then_inc(q_exp, 1)
                    act.wait_ge(g_done, t * KT + m + 1)
                    if m == 0:
                        act.wait_ge(nbg_ready, 1)
                    if m >= 2:
                        act.wait_ge(a_split, t * KT + m - 1)
                    act.activation(gate[:, m % 2], bank[2 + m % 2][:], ACT.Exp, bias=nbg[:, m:m + 1], scale=-1.0).then_inc(g_exp, 1)
                    if m:
                        a_highs(m - 1)
                if more:
                    xT_highs(t + 1, range(KT))
                    keep_x(t + 1)
                a_highs(KT - 1)
            steps(act, body)

        @block.vector
        def _(dve):
            dve.wait_ge(bg_loaded, 16)
            dve.tensor_scalar(nbg[:], bg[:], -1.0, None, ALU.mult).then_inc(nbg_ready, 1)

            def norm_in(t):
                dve.wait_ge(ln_in.rstd_ready, t + 1)
                dve.wait_ge(c_split, t * KT + KT)
                for i in range(TB):
                    ln_in.apply(dve, xs[:, i], acc[:, t * TB + i], i).then_inc(xs_ready, 1)

            def w_lows(c):
                for kt in range(KT):
                    dve.wait_ge(w_high, c * KT + kt + 1)
                    dve.tensor_tensor(w_l[:, c, kt], w_raw[c][:, kt], w_h[:, c, kt].bitcast(F32), ALU.subtract).then_inc(w_split, 1)

            def xT_lows(t, kts):
                for kt in kts:
                    dve.wait_ge(xT_high, t * KT + kt + 1)
                    dve.tensor_tensor(xT_l[:, kt], bank[4 + kt % 2][:], xT_h[:, kt].bitcast(F32), ALU.subtract).then_inc(xT_split, 1)

            ln_in.statistics(dve, lambda i: acc[:, i], 0)
            w_lows(K)
            norm_in(0)
            w_lows(V)
            dve.sem_inc(added, TB)

            def body(t, first, more):
                def feature_min(i, done, mins):
                    dve.wait_ge(done, t * TB + i + 1)
                    dve.tensor_scalar(low[:, i % 2], bank[i % 2][:], 0.0, None, ALU.min).then_inc(mins, 1)

                def feature(i, exps, out, ready):
                    dve.wait_ge(exps, t * TB + i + 1)
                    dve.scalar_tensor_tensor(out, bank[i % 2][:], 0.0, low[:, i % 2], ALU.max, ALU.add).then_inc(ready, 1)

                def kv_masks(i):
                    dve.wait_ge(kv_done, t * TB + i + 1)
                    if i == 0:
                        dve.wait_ge(blocks_ready, 6)
                    each = blocks[:].unsqueeze(1).broadcast_to([P, KT, P])
                    dve.tensor_tensor(kv_blocks[:, i], bank[4][:].rearrange("p (m e) -> p m e", m=KT), each, ALU.mult)
                    dve.tensor_tensor(ks_blocks[:, i], bank[5][:, 0:KT].unsqueeze(2).broadcast_to([P, KT, P]), each,
                                      ALU.mult).then_inc(kv_ready, 1)

                def quotient(m):
                    n = t * KT + m + 1
                    dve.wait_ge(g_exp, n)
                    dve.tensor_scalar(gate[:, m % 2], gate[:, m % 2], 1.0, None, ALU.add).then_inc(g_ready, 1)
                    dve.wait_ge(g_ready, n)
                    dve.wait_ge(nd_done, n)
                    dve.scalar_tensor_tensor(gate[:, m % 2], bank[7][:], EPS, gate[:, m % 2], ALU.add, ALU.mult).then_inc(den_ready, 1)
                    dve.wait_ge(den_ready, n)
                    dve.reciprocal(gate[:, m % 2], gate[:, m % 2]).then_inc(inv_ready, 1)
                    dve.wait_ge(inv_ready, n)
                    dve.tensor_tensor(gate[:, m % 2], bank[6][:], gate[:, m % 2], ALU.mult).then_inc(a_ready, 1)

                for i in range(TB):
                    feature_min(i, k_done, k_min)
                    if i:
                        kv_masks(i - 1)
                    feature(i, k_exp, kf[:, i % 2], k_ready)
                    if first and i == 0:
                        xT_lows(0, range(KT))
                    if first and i < 3:
                        w_lows((Q, G, O)[i])
                    if more and i == 2:
                        ln_in.statistics(dve, lambda i: acc[:, (t + 1) * TB + i], t + 1)
                kv_masks(TB - 1)
                for m in range(KT):
                    feature_min(m, q_done, q_min)
                    feature(m, q_exp, qf[:, m % 2], q_ready)
                    if m:
                        quotient(m - 1)
                    if more and m == 2:
                        norm_in(t + 1)
                if more:
                    xT_lows(t + 1, (0, 1))
                quotient(KT - 1)
                if more:
                    xT_lows(t + 1, (2, 3))
                dve.wait_ge(x_kept, t + 1)
                for i in range(TB):
                    dve.wait_ge(out_done, t * TB + i + 1)
                    dve.tensor_tensor(acc[:, t * TB + i], acc[:, t * TB + i], bank[i][:], ALU.add).then_inc(added, 1)
                dve.wait_ge(added, t * TB + 2 * TB)
                dve.sem_inc(waited, 1)
                ln_out.statistics(dve, lambda i: acc[:, t * TB + i], t)
                dve.wait_ge(ln_out.rstd_ready, t + 1)
                for i in range(TB):
                    ln_out.apply(dve, acc[:, t * TB + i], acc[:, t * TB + i], i).then_inc(x1_ready, 1)
            steps(dve, body)

        @block.tensor
        def _(pe):
            def xT_transposes(t, kts):
                for kt in kts:
                    if kt == 0:
                        pe.wait_ge(xs_ready, t * TB + TB)
                    if kt >= 2:
                        pe.wait_ge(xT_split, t * KT + kt - 1)
                    for i in range(TB):
                        last = nc.tensor.transpose(bank[4 + kt % 2][:, i * P:(i + 1) * P], xs[:, i, kt * P:(kt + 1) * P], ident[:])
                    last.then_inc(xT_done, 1)

            pe.wait_ge(ident_ready, 2)
            pe.wait_ge(blocks_ready, 6)

            def body(t, first, more):
                def rows(c, i, out, done, first):
                    for kt in range(KT):
                        if first:
                            pe.wait_ge(c_split, t * KT + kt + 1)
                        part = slice(i * P, (i + 1) * P)
                        last = split3(nc, out[:], c_h[:, kt, part], c_l[:, kt, part], w_h[:, c, kt], w_l[:, c, kt], kt == 0, kt == KT - 1)
                    last.then_inc(done, 1)

                def columns(c, m, out, done):
                    for kt in range(KT):
                        if m == 0 and c == Q:
                            pe.wait_ge(xT_split, t * KT + kt + 1)
                        part = slice(m * P, (m + 1) * P)
                        last = split3(nc, out[:], w_h[:, c, kt, part], w_l[:, c, kt, part], xT_h[:, kt], xT_l[:, kt], kt == 0, kt == KT - 1)
                    last.then_inc(done, 1)

                def summary(i):
                    pe.wait_ge(k_ready, t * TB + i + 1)
                    pe.wait_ge(v_ready, t * TB + i + 1)
                    if i:
                        pe.wait_ge(kv_ready, t * TB + i)
                    for m in range(KT):
                        part = slice(m * P, (m + 1) * P)
                        nc.tensor.matmul(bank[5][:, m:m + 1], kf[:, i % 2, part], ones[:], start=True, stop=True)
                    for m in range(KT):
                        part = slice(m * P, (m + 1) * P)
                        last = nc.tensor.matmul(bank[4][:, part], kf[:, i % 2, part], vs[:, i % 2, part], start=True, stop=True)
                    last.then_inc(kv_done, 1)

                def apply_summary(m):
                    pe.wait_ge(q_ready, t * KT + m + 1)
                    if m:
                        pe.wait_ge(a_ready, t * KT + m)
                    else:
                        pe.wait_ge(kv_ready, t * TB + TB)
                    for b in range(TB):
                        part = slice(b * P, (b + 1) * P)
                        nc.tensor.matmul(bank[7][:, part], ks_blocks[:, b, m], qf[:, m % 2, part], start=True, stop=True)
                    for b in range(TB):
                        part = slice(b * P, (b + 1) * P)
                        last = nc.tensor.matmul(bank[6][:, part], kv_blocks[:, b, m], qf[:, m % 2, part], start=True, stop=True)
                    last.then_inc(nd_done, 1)

                for i in range(TB):
                    if i < 2:
                        pe.wait_ge(added, t * TB + TB)
                    else:
                        pe.wait_ge(k_ready, t * TB + i - 1)
                        pe.wait_ge(v_ready, t * TB + i - 1)
                    if i == 0:
                        pe.wait_ge(w_split, (K + 1) * KT)
                    rows(K, i, bank[i % 2], k_done, i == 0)
                    if first and i == 0:
                        xT_transposes(0, (0, 1))
                    if i == 0:
                        pe.wait_ge(w_split, (V + 1) * KT)
                    rows(V, i, bank[2 + i % 2], v_done, False)
                    if first and i == 0:
                        xT_transposes(0, (2, 3))
                    if first and i == 1:
                        pe.wait_ge(xT_split, KT)
                    if i:
                        summary(i - 1)
                pe.wait_ge(w_split, (Q + 1) * KT)
                for m in range(KT):
                    if m < 2:
                        pe.wait_ge(k_ready, t * TB + 3 + m)
                    else:
                        pe.wait_ge(q_ready, t * KT + m - 1)
                    columns(Q, m, bank[m % 2], q_done)
                    if m == 0:
                        pe.wait_ge(w_split, (G + 1) * KT)
                        summary(TB - 1)
                    if m < 2:
                        pe.wait_ge(v_ready, t * TB + 3 + m)
                    else:
                        pe.wait_ge(g_exp, t * KT + m - 1)
                    columns(G, m, bank[2 + m % 2], g_done)
                    if m:
                        apply_summary(m - 1)
                if more:
                    pe.wait_ge(kv_ready, t * TB + TB)
                    xT_transposes(t + 1, (0, 1))

                def out_proj(m):
                    pe.wait_ge(a_split, t * KT + m + 1)
                    for i in range(TB):
                        if m == 0:
                            pe.wait_ge((q_ready, g_exp)[i // 2], t * KT + 3 + i % 2)
                        part = slice(i * P, (i + 1) * P)
                        last = split3(nc, bank[i][:], a_h[:, m, part], a_l[:, m, part], w_h[:, O, m], w_l[:, O, m], m == 0, m == KT - 1)
                        if m == KT - 1:
                            last.then_inc(out_done, 1)

                pe.wait_ge(w_split, (O + 1) * KT)
                out_proj(0)
                out_proj(1)
                apply_summary(KT - 1)
                if more:
                    xT_transposes(t + 1, (2, 3))
                out_proj(2)
                out_proj(3)
            steps(pe, body)


NB = 16
TOP = 4


def groups(eng, body):
    body(0, True, True)
    with eng.Fori(1, TG - 1) as t:
        body(t, False, True)
    body(TG - 1, False, False)


def blockwise_ffn(nc, w_dram, wr_dram, br_dram, x1_dram, x2_dram):
    with ExitStack() as ctx:
        sb, sem, clear_semaphores = stage_memory(nc, ctx)
        NC = 2 * NB // 4
        w_h, w_l = sb("c_w_h", [P, NC, 4, D], F32R), sb("c_w_l", [P, NC, 4, D], F32R)
        xT_h, xT_l = sb("c_xT_h", [P, 2, KT, TOK], F32R), sb("c_xT_l", [P, 2, KT, TOK], F32R)
        xs, res = sb("c_xs", [P, TB, D]), sb("c_res", [P, TB, D])
        w_raw = res
        act_f, act_m = sb("c_act_f", [P, 2, TOK]), sb("c_act_m", [P, 2, TOK])
        act_h, act_l = sb("c_act_h", [P, 2, TOK], F32R), sb("c_act_l", [P, 2, TOK], F32R)
        wr_raw = sb("c_wr_raw", [P, KT, NB])
        wr_h, wr_l = sb("c_wr_h", [P, KT, NB], F32R), sb("c_wr_l", [P, KT, NB], F32R)
        br = sb("c_br", [NB, 1])
        logitT = sb("c_logitT", [NB, TOK])
        ident, identb = sb("c_ident", [P, P]), sb("c_identb", [P, P], BF16)
        pick = sb("c_pick", [NB, NB, P], BF16)
        shifted, prob = sb("c_shifted", [P, TB, NB]), sb("c_prob", [P, TB, NB])
        rmax, rsum, rinv = sb("c_rmax", [P, TB]), sb("c_rsum", [P, TB]), sb("c_rinv", [P, TB])
        top8, above, n_above = sb("c_top8", [P, TB, 8]), sb("c_above", [P, TB, NB]), sb("c_n_above", [P, TB])
        equal, rank, ones = sb("c_equal", [P, TB, NB]), sb("c_rank", [P, TB, NB]), sb("c_ones", [P, NB])
        mask, maskT = sb("c_mask", [P, TB, NB], BF16), sb("c_maskT", [NB, 2, TOK], BF16)
        ln = LayerNorm(nc, sb, sem, "c_ln", 1e-5)
        bank = [ctx.enter_context(nc.psum_tensor(f"c_bank{i}", [P, D], F32)) for i in range(7)]
        small = ctx.enter_context(nc.psum_tensor("c_small", [P, D], F32))
        smallb = small[:].bitcast(BF16)
        w_loaded = [sem(f"c_w_loaded{i}") for i in range(4)]
        small_loaded, xs_loaded, res_loaded, x2_stored = sem("c_small_loaded"), sem("c_xs_loaded"), sem("c_res_loaded"), sem("c_x2_stored")
        ident_ready, identb_ready, pick_ready = sem("c_ident_ready"), sem("c_identb_ready"), sem("c_pick_ready")
        w_high, w_split, wr_high, wr_split = sem("c_w_high"), sem("c_w_split"), sem("c_wr_high"), sem("c_wr_split")
        xT_done, xT_high, xT_split = sem("c_xT_done"), sem("c_xT_high"), sem("c_xT_split")
        logits_done, logits_ready, back_done, shift_ready, exp_ready = (
            sem("c_logits_done"), sem("c_logits_ready"), sem("c_back_done"), sem("c_shift_ready"), sem("c_exp_ready"))
        chain = sem("c_chain")
        maskT_done, maskT_ready = sem("c_maskT_done"), sem("c_maskT_ready")
        h_done, b_done, y_done = sem("c_h_done"), sem("c_b_done"), sem("c_y_done")
        gelu_ready, masked_ready, act_high, act_split = (
            sem("c_gelu_ready"), sem("c_masked_ready"), sem("c_act_high"), sem("c_act_split"))
        added, x2_ready = sem("c_added"), sem("c_x2_ready")
        waited, pe_waited = sem("c_waited"), sem("c_pe_waited")
        CHAIN = 4 + 7 * TB
        ctx.callback(clear_semaphores)
        block = ctx.enter_context(nc.Block())

        @block.sync
        def _(sp):
            sp.dma_start(xs[:], x1_dram[0]).then_inc(xs_loaded, 16)
            sp.dma_start(wr_raw[:], wr_dram).then_inc(small_loaded, 16)
            sp.dma_start(br[:], br_dram).then_inc(small_loaded, 16)
            for n in range(NC * 4):
                if n == 8:
                    sp.wait_ge(xT_done, KT)
                    sp.dma_start(xs[:], x1_dram[1]).then_inc(xs_loaded, 16)
                if n >= 4:
                    sp.wait_ge(w_split, n - 3)
                sp.dma_start(w_raw[:, n % 4], w_dram[n // 4, :, n % 4]).then_inc(w_loaded[n % 4], 16)

            def store(t):
                sp.wait_ge(x2_ready, t * TB + TB)
                sp.dma_start(x2_dram[t], res[:]).then_inc(x2_stored, 16)

            def body(t, first, more):
                if more and not first:
                    sp.wait_ge(xT_done, t * KT + KT)
                    sp.dma_start(xs[:], x1_dram[t + 1]).then_inc(xs_loaded, 16)
                if not first:
                    store(t - 1)
                    sp.wait_ge(x2_stored, t * 16)
                if first:
                    sp.wait_ge(w_split, NC * 4)
                sp.dma_start(res[:], x1_dram[t]).then_inc(res_loaded, 16)
            groups(sp, body)
            store(TG - 1)
            sp.wait_ge(x2_stored, TG * 16)

        @block.gpsimd
        def _(gps):
            make_identity(nc, gps, ident, ident_ready)
            ln.constants(gps)
            gps.memset(pick[:], 0.0).then_inc(pick_ready, 1)
            gps.memset(ones[:], 1.0).then_inc(pick_ready, 1)
            gps.wait_ge(pick_ready, 2)
            gps.affine_select(out=pick[:], in_=pick[:], compare_op=ALU.not_equal, fill=1.0, base=0,
                              pattern=[[-1, NB], [0, P]], channel_multiplier=1).then_inc(pick_ready, 1)
            gps.wait_ge(pick_ready, 3)

            def body(t, first, more):
                for i in range(NB):
                    gps.wait_ge(act_high, t * NB + i + 1)
                    gps.tensor_tensor(act_l[:, i % 2], act_m[:, i % 2], act_h[:, i % 2].bitcast(F32), ALU.subtract).then_inc(act_split, 1)
                    if not first and i == 0:
                        ln.power_step(gps, t - 1)
            groups(gps, body)
            ln.power_step(gps, TG - 1)

        FIRST_PIECES = 8
        pieces_at = lambda i: range(FIRST_PIECES + 2 * i, min(FIRST_PIECES + 2 * i + 2, NC * 4))

        XT_AT, LOGITS_AT, BACK_AT, MASK_AT = (1, 3, 5, 7), 9, 10, 13

        @block.scalar
        def _(act):
            def xT_high_part(t, kt):
                act.wait_ge(xT_done, t * KT + kt + 1)
                act.activation(xT_h[:, t % 2 if isinstance(t, int) else t & 1, kt], small[:], ACT.Copy).then_inc(xT_high, 1)

            def logit_bias(t):
                act.wait_ge(logits_done, t + 1)
                act.activation(logitT[:], small[0:NB, :], ACT.Identity, bias=br[:, 0:1]).then_inc(logits_ready, 1)

            def exps(t):
                act.wait_ge(shift_ready, t + 1)
                act.activation(prob[:], shifted[:], ACT.Exp).then_inc(exp_ready, 1)

            act.wait_ge(small_loaded, 32)
            act.activation(wr_h[:], wr_raw[:], ACT.Copy).then_inc(wr_high, 1)
            for kt in range(KT):
                xT_high_part(0, kt)

            def w_highs(ns):
                for n in ns:
                    act.wait_ge(w_loaded[n % 4], (n // 4 + 1) * 16)
                    act.activation(w_h[:, n // 4, n % 4], w_raw[:, n % 4], ACT.Copy).then_inc(w_high, 1)

            w_highs(range(4))
            logit_bias(0)
            exps(0)
            w_highs(range(4, FIRST_PIECES))

            def body(t, first, more):
                for i in range(NB):
                    act.wait_ge(h_done, t * NB + i + 1)
                    act.activation(act_f[:, i % 2], bank[4 + i % 2][:], ACT.Gelu).then_inc(gelu_ready, 1)
                    act.wait_ge(masked_ready, t * NB + i + 1)
                    act.activation(act_h[:, i % 2], act_m[:, i % 2], ACT.Copy).then_inc(act_high, 1)
                    if first:
                        w_highs(pieces_at(i))
                    if more:
                        if i in XT_AT:
                            xT_high_part(t + 1, XT_AT.index(i))
                        if i == LOGITS_AT:
                            logit_bias(t + 1)
                        if i == BACK_AT:
                            exps(t + 1)
            groups(act, body)

        @block.vector
        def _(dve):
            def xT_low_part(t, kt):
                dve.wait_ge(xT_high, t * KT + kt + 1)
                par = t % 2 if isinstance(t, int) else t & 1
                dve.tensor_tensor(xT_l[:, par, kt], small[:], xT_h[:, par, kt].bitcast(F32), ALU.subtract).then_inc(xT_split, 1)

            def shift(t):
                dve.wait_ge(back_done, t + 1)
                logits = small[:, 0:TB * NB].rearrange("p (b e) -> p b e", b=TB)
                dve.tensor_reduce(rmax[:], logits, AX, ALU.max).then_inc(chain, 1)
                dve.wait_ge(chain, t * CHAIN + 1)
                dve.tensor_tensor(shifted[:], logits, rmax[:].unsqueeze(2).broadcast_to([P, TB, NB]), ALU.subtract).then_inc(shift_ready, 1)

            def choose(t):
                at = [1]

                def link(instruction):
                    at[0] += 1
                    instruction.then_inc(chain, 1)
                    dve.wait_ge(chain, t * CHAIN + at[0])

                dve.wait_ge(exp_ready, t + 1)
                link(dve.tensor_reduce(rsum[:], prob[:], AX, ALU.add))
                link(dve.reciprocal(rinv[:], rsum[:]))
                link(dve.tensor_tensor(prob[:], prob[:], rinv[:].unsqueeze(2).broadcast_to([P, TB, NB]), ALU.mult))
                for b in range(TB):
                    dve.sem_inc(waited, 1)
                    least = top8[:, b, TOP - 1:TOP]
                    link(dve.max(top8[:, b], prob[:, b]))
                    link(dve.tensor_scalar(above[:, b], prob[:, b], least, None, ALU.is_gt, ALU.add, accum_out=n_above[:, b:b + 1]))
                    link(dve.tensor_scalar(equal[:, b], prob[:, b], least, None, ALU.is_equal))
                    link(dve.tensor_tensor_scan(rank[:, b], ones[:], equal[:, b], 0.0, ALU.mult, ALU.add))
                    link(dve.tensor_scalar(rank[:, b], rank[:, b], n_above[:, b:b + 1], float(TOP), ALU.add, ALU.is_le))
                    link(dve.tensor_tensor(rank[:, b], rank[:, b], equal[:, b], ALU.mult))
                    link(dve.tensor_tensor(mask[:, b], rank[:, b], above[:, b], ALU.add))
                assert at[0] == CHAIN

            def mask_columns(t):
                dve.wait_ge(maskT_done, t + 1)
                par = t % 2 if isinstance(t, int) else t & 1
                dve.tensor_copy(maskT[:, par], smallb[0:NB, 0:TOK]).then_inc(maskT_ready, 1)

            dve.wait_ge(ident_ready, 2)
            dve.tensor_copy(identb[:], ident[:]).then_inc(identb_ready, 1)
            dve.wait_ge(wr_high, 1)
            dve.tensor_tensor(wr_l[:], wr_raw[:], wr_h[:].bitcast(F32), ALU.subtract).then_inc(wr_split, 1)
            dve.wait_ge(pick_ready, 3)
            for kt in range(KT):
                xT_low_part(0, kt)

            def w_lows(ns):
                for n in ns:
                    dve.wait_ge(w_high, n + 1)
                    dve.tensor_tensor(w_l[:, n // 4, n % 4], w_raw[:, n % 4], w_h[:, n // 4, n % 4].bitcast(F32), ALU.subtract).then_inc(w_split, 1)

            w_lows(range(4))
            shift(0)
            choose(0)
            mask_columns(0)
            w_lows(range(4, FIRST_PIECES))

            def finish(t):
                dve.wait_ge(res_loaded, t * 16 + 16)
                for i in range(TB):
                    dve.wait_ge(y_done, t * TB + i + 1)
                    dve.tensor_tensor(res[:, i], res[:, i], bank[i][:], ALU.add).then_inc(added, 1)
                dve.wait_ge(added, t * TB + 2 * TB)
                ln.statistics(dve, lambda i: res[:, i], t)

            def finish_rows(t):
                dve.wait_ge(ln.rstd_ready, t + 1)
                for i in range(TB):
                    ln.apply(dve, res[:, i], res[:, i], i).then_inc(x2_ready, 1)

            dve.sem_inc(added, TB)

            def body(t, first, more):
                for i in range(NB):
                    dve.wait_ge(gelu_ready, t * NB + i + 1)
                    dve.wait_ge(b_done, t * NB + i + 1)
                    if not first or i >= 2:
                        dve.wait_ge(act_split, t * NB + i - 1)
                    dve.tensor_tensor(act_m[:, i % 2], act_f[:, i % 2], bank[6][:], ALU.mult).then_inc(masked_ready, 1)
                    if first:
                        w_lows(pieces_at(i))
                    if not first and i == 0:
                        finish(t - 1)
                    if not first and i == 1:
                        finish_rows(t - 1)
                    if more:
                        if i in XT_AT:
                            xT_low_part(t + 1, XT_AT.index(i))
                        if i == BACK_AT:
                            shift(t + 1)
                            choose(t + 1)
                        if i == MASK_AT:
                            mask_columns(t + 1)
            groups(dve, body)
            finish(TG - 1)
            finish_rows(TG - 1)

        @block.tensor
        def _(pe):
            def xT_transposes(t, kt):
                if kt == 0:
                    pe.wait_ge(xs_loaded, t * 16 + 16)
                else:
                    pe.wait_ge(xT_split, t * KT + kt)
                for i in range(TB):
                    last = nc.tensor.transpose(small[:, i * P:(i + 1) * P], xs[:, i, kt * P:(kt + 1) * P], ident[:])
                last.then_inc(xT_done, 1)

            def logits(t):
                par = t % 2 if isinstance(t, int) else t & 1
                pe.wait_ge(xT_split, t * KT + KT)
                for kt in range(KT):
                    last = split3(nc, small[0:NB, :], wr_h[:, kt], wr_l[:, kt], xT_h[:, par, kt], xT_l[:, par, kt], kt == 0, kt == KT - 1)
                last.then_inc(logits_done, 1)

            def logits_back(t):
                pe.wait_ge(logits_ready, t + 1)
                pe.sem_inc(pe_waited, 1)
                for b in range(TB):
                    last = nc.tensor.transpose(small[:, b * NB:(b + 1) * NB], logitT[:, b * P:(b + 1) * P], ident[0:NB, 0:NB])
                last.then_inc(back_done, 1)

            def mask_transposes(t):
                pe.wait_ge(chain, t * CHAIN + CHAIN)
                for b in range(TB):
                    last = nc.tensor.transpose(smallb[0:NB, b * P:(b + 1) * P], mask[:, b], identb[:])
                last.then_inc(maskT_done, 1)

            pe.wait_ge(ident_ready, 2)
            pe.wait_ge(pick_ready, 3)
            pe.wait_ge(identb_ready, 1)
            pe.wait_ge(wr_split, 1)
            for kt in range(KT):
                xT_transposes(0, kt)
            logits(0)
            logits_back(0)

            def back(t, i):
                pe.wait_ge(act_split, t * NB + i + 1)
                pe.wait_ge(w_split, 8 * (i // 4) + 4 + i % 4 + 1)
                for b in range(TB):
                    if i == 0:
                        pe.wait_ge(added, t * TB + b + 1)
                    part = slice(b * P, (b + 1) * P)
                    last = split3(nc, bank[b][:], act_h[:, i % 2, part], act_l[:, i % 2, part],
                                  w_h[:, 2 * (i // 4) + 1, i % 4], w_l[:, 2 * (i // 4) + 1, i % 4], i == 0, i == NB - 1)
                    if i == NB - 1:
                        last.then_inc(y_done, 1)

            def body(t, first, more):
                par = t % 2 if isinstance(t, int) else t & 1

                def hidden(i):
                    if not first or i >= 2:
                        pe.wait_ge(gelu_ready, t * NB + i - 1)
                    for kt in range(KT):
                        pe.wait_ge(w_split, 8 * (i // 4) + kt + 1)
                        part = slice((i % 4) * P, (i % 4 + 1) * P)
                        last = split3(nc, bank[4 + i % 2][:], w_h[:, 2 * (i // 4), kt, part], w_l[:, 2 * (i // 4), kt, part],
                                      xT_h[:, par, kt], xT_l[:, par, kt], kt == 0, kt == KT - 1)
                    last.then_inc(h_done, 1)
                    if first and i == 0:
                        mask_transposes(0)
                    if i == 0:
                        pe.wait_ge(maskT_ready, t + 1)
                    if not first or i:
                        pe.wait_ge(masked_ready, t * NB + i)
                    pe.sem_inc(pe_waited, 1)
                    nc.tensor.matmul(bank[6][:], pick[:, i], maskT[:, par], start=True, stop=True).then_inc(b_done, 1)

                for i in range(NB):
                    hidden(i)
                    if more:
                        if i in XT_AT:
                            xT_transposes(t + 1, XT_AT.index(i))
                        if i == LOGITS_AT:
                            logits(t + 1)
                        if i == BACK_AT:
                            logits_back(t + 1)
                        if i == MASK_AT:
                            mask_transposes(t + 1)
                    if i:
                        back(t, i - 1)
                    elif not first:
                        back(t - 1, NB - 1)
            groups(pe, body)
            back(TG - 1, NB - 1)


HD = 32
NH = D // HD
NEG = -1e38
EXT = P + 1


def powered_attention_and_wkv(nc, x2_dram, ctxT_dram, w_dram, gamma_dram, beta_dram, wu_dram, x4_dram):
    with ExitStack() as ctx:
        sb, sem, clear_semaphores = stage_memory(nc, ctx)
        Q, K, V, O = range(4)
        w_h, w_l = sb("d_w_h", [P, 4, KT, D], F32R), sb("d_w_l", [P, 4, KT, D], F32R)
        xs, res = sb("d_xs", [P, TB, D]), sb("d_res", [P, TB, D])
        x3 = res
        x4 = xs
        zT = sb("d_zT", [P, KT, TB, P])
        w_raw = [res[:], zT[:].rearrange("p c b e -> p c (b e)")]
        w_mean = sb("d_w_mean", [P, KT * NH])
        xT_h, xT_l = sb("d_xT_h", [P, KT, TOK], F32R), sb("d_xT_l", [P, KT, TOK], F32R)
        gamma, beta_row, beta_mean = sb("d_gamma", [P, HD]), sb("d_beta_row", [P, HD]), sb("d_beta_mean", [P, 1])
        beta = sb("d_beta", [P, 1])
        qT, kT = sb("d_qT", [P, 2, TOK]), sb("d_kT", [P, 1, TOK])
        squares = sb("d_squares", [P, 2, 2, TOK])
        v = sb("d_v", [P, TB, NH, HD + 1])
        norms, factor = sb("d_norms", [P, TB, 2, 4]), sb("d_factor", [P, TB * 4])
        scaled_q = sb("d_scaled_q", [P, 2, TB, 4])
        weights = sb("d_weights", [P, 4, TOK])
        o_nat = sb("d_o_nat", [P, 2, TB, P])
        oT_h, oT_l = sb("d_oT_h", [P, KT, TOK], F32R), sb("d_oT_l", [P, KT, TOK], F32R)
        ident, causal, heads = sb("d_ident", [P, P]), sb("d_causal", [P, P]), sb("d_heads", [P, 4])
        ln3, ln4 = LayerNorm(nc, sb, sem, "d_ln3", 1e-5), LayerNorm(nc, sb, sem, "d_ln4", 1e-5)
        ext = lambda name, n=2: sb(name, [P, n, TB, EXT])
        k_ext = sb("d_k_ext", [P, KT, TB, P])
        wu = sb("d_wu", [P, 2, KT])
        vT = sb("d_vT", [P, KT, TB, P])
        o_ext, decay, entry, entry_v = ext("d_o_ext", 1), ext("d_decay"), ext("d_entry"), ext("d_entry_v", 1)
        p_ext, q_ext = ext("d_p_ext"), ext("d_q_ext")
        old, new = sb("d_old", [P, 2, TB, P]), sb("d_new", [P, 2, TB, P])
        part = sb("d_part", [P, 2, TB, P])
        num, den = (lambda c: p_ext[:, c % 2, :, 0:P]), (lambda c: q_ext[:, c % 2, :, 0:P])
        inv = lambda c: part[:, c % 2]
        ps_s = [ctx.enter_context(nc.psum_tensor(f"d_ps_s{i}", [P, TOK], F32)) for i in range(4)]
        ps_o = ctx.enter_context(nc.psum_tensor("d_ps_o", [P, 2, TOK], F32))
        ring = [ctx.enter_context(nc.psum_tensor(f"d_ring{i}", [P, TOK], F32)) for i in range(2)]
        names = """sp_waited small_loaded xs_loaded res_loaded v_loaded x4_stored ident_ready const_ready beta_ready
            w_fold w_high w_split xT_high xT_split
            v_ready q_ready k_ready sums_ready norms_ready vs_ready
            s_done square_ready masked av_done factor_ready o_ready oT_high oT_split out_done added x3_ready
            kx_ready o_scan a_ready d_ready e_ready decay_ready entry_ready old_ready new_ready ev_ready
            p_ready num_ready q_scan pool_parts den_ready ln_ready inv_ready newton z_parts z_ready zn_ready x4_ready""".split()
        S = {n: sem("d_" + n) for n in names}
        w_loaded = [sem("d_w_loaded0"), sem("d_w_loaded1")]
        ring_full = [sem("d_full0"), sem("d_full1")]
        FL = NH * HD
        ctx.callback(clear_semaphores)
        block = ctx.enter_context(nc.Block())

        def ring_order(attend, recur, more):
            names = []
            if recur:
                names += [f"kx{c}" for c in range(4)]
            if attend:
                for m in range(4):
                    if m < 3:
                        names += [f"q{m + 1}", f"k{m + 1}", f"su{m + 1}"]
                    if m == 3 and more:
                        names += ["xt0", "xt1"]
                    if m:
                        names += [f"ot{m - 1}"]
                    if m == 3 and more:
                        names += ["xt2", "xt3"]
                names += ["ot3"]
                if more:
                    names += ["q0", "k0", "v0", "v1", "v2", "v3", "su0"]
            if recur:
                names += [f"zn{i}" for i in range(4)]
            return names

        class Ring:

            def __init__(self, t, attend, recur, more):
                self.t, self.order = t, ring_order(attend, recur, more)
                self.before = (11, 35, 67, 99, 120)[t] if isinstance(t, int) else 35
                self.repeated = 0 if isinstance(t, int) else (t - 1) * 16

            def place(self, name):
                return self.before + self.order.index(name)

            def bank(self, name):
                return ring[self.place(name) % 2]

            def claim(self, pe, name):
                n, t = self.order.index(name), self.t
                if n < 2:
                    if not (isinstance(t, int) and t == TG):
                        pe.wait_ge(*((S["v_ready"], t * TB + TB), (S["sums_ready"], 2 * t * KT + 1))[n])
                    if not (isinstance(t, int) and t == 0):
                        pe.wait_ge(S["zn_ready"], (t - 1) * TB + 1)
                    return
                kind, k = self.order[n - 2][:-1], int(self.order[n - 2][-1])
                ahead = 1 if k == 0 else 0
                pe.wait_ge(*{
                    "v": (S["v_ready"], (t + 1) * TB + k + 1), "q": (S["q_ready"], (t + ahead) * KT + k + 1),
                    "k": (S["k_ready"], (t + ahead) * KT + k + 1), "kx": (S["kx_ready"], (t - 1) * KT + k + 1),
                    "su": (S["sums_ready"], ((t + ahead) * KT + k) * 2 + 1), "ot": (S["oT_split"], t * KT + k + 1),
                    "xt": (S["xT_split"], (t + 1) * KT + k + 1), "zn": (S["zn_ready"], (t - 1) * TB + k + 2),
                }[kind])

            def filled(self, instruction, name):
                instruction.then_inc(ring_full[self.place(name) % 2], 1)

            def await_full(self, eng, name):
                place = self.place(name)
                eng.wait_ge(ring_full[place % 2], place // 2 + 1 + self.repeated)

        class FirstUses:

            order = ["q0", "k0", "v0", "v1", "v2", "v3", "su0"]

            def bank(self, name):
                return ring[self.order.index(name) % 2]

            def claim(self, pe, name):
                n = self.order.index(name)
                pe.wait_ge(*((S["xT_split"], n + 3), (S["xT_split"], n + 3), (S["q_ready"], 1), (S["k_ready"], 1),
                             (S["v_ready"], n - 3), (S["v_ready"], n - 3), (S["v_ready"], n - 3))[n])

            def filled(self, instruction, name):
                instruction.then_inc(ring_full[self.order.index(name) % 2], 1)

            def await_full(self, eng, name):
                n = self.order.index(name)
                eng.wait_ge(ring_full[n % 2], 2 + n // 2 + 1)

        def rounds(eng, body):
            body(0, True, False, True, Ring(0, True, False, True))
            with eng.Fori(1, TG - 1) as t:
                body(t, True, True, True, Ring(t, True, True, True))
            body(TG - 1, True, True, False, Ring(TG - 1, True, True, False))
            body(TG, False, True, False, Ring(TG, False, True, False))


        @block.sync
        def _(sp):
            sp.sem_inc(S["x4_stored"], 16)
            sp.dma_start(xs[:], x2_dram[0]).then_inc(S["xs_loaded"], 16)
            sp.dma_start(w_raw[0], w_dram[Q]).then_inc(w_loaded[0], 16)
            sp.dma_start(gamma[:], gamma_dram.rearrange("(a n) -> a n", a=1).broadcast_to([P, HD])).then_inc(S["small_loaded"], 16)
            sp.dma_start(beta_row[:], beta_dram.rearrange("(a n) -> a n", a=1).broadcast_to([P, HD])).then_inc(S["small_loaded"], 16)
            for j in range(4):
                sp.dma_start(beta[j * HD:(j + 1) * HD], beta_dram.rearrange("(n a) -> n a", a=1)).then_inc(S["small_loaded"], 16)
            sp.dma_start(wu[:], wu_dram).then_inc(S["small_loaded"], 16)
            sp.dma_start(w_raw[1], w_dram[K]).then_inc(w_loaded[1], 16)
            for c in (V, O):
                sp.wait_ge(S["w_split"], (c - 1) * KT)
                sp.dma_start(w_raw[c % 2], w_dram[c]).then_inc(w_loaded[c % 2], 16)
            sp.wait_ge(S["w_split"], 4 * KT)
            sp.dma_start(res[:], x2_dram[0]).then_inc(S["res_loaded"], 16)
            sp.dma_start(vT[:], ctxT_dram[0]).then_inc(S["v_loaded"], 16)

            def body(t, attend, recur, more, ring_uses):
                if attend and more:
                    sp.wait_ge(S["xT_high"], (t + 1) * KT)
                    sp.sem_inc(S["sp_waited"], 1)
                    if recur:
                        sp.wait_ge(S["x4_stored"], t * 16)
                    sp.dma_start(xs[:], x2_dram[t + 1]).then_inc(S["xs_loaded"], 16)
                if attend and recur:
                    sp.wait_ge(S["kx_ready"], t * KT)
                    sp.dma_start(res[:], x2_dram[t]).then_inc(S["res_loaded"], 16)
                    sp.wait_ge(S["pool_parts"], t * KT * 3 + 1)
                    sp.dma_start(vT[:], ctxT_dram[t]).then_inc(S["v_loaded"], 16)
                if recur:
                    sp.wait_ge(S["x4_ready"], (t - 1) * TB + TB)
                    sp.dma_start(x4_dram[t - 1], x4[:]).then_inc(S["x4_stored"], 16)
            rounds(sp, body)
            sp.wait_ge(S["x4_stored"], TG * 16 + 16)

        @block.gpsimd
        def _(gps):
            for counted in ("pool_parts", "e_ready", "z_ready"):
                gps.sem_inc(S[counted], 1)
            ln3.constants(gps)
            ln4.constants(gps)
            make_identity(nc, gps, ident, S["ident_ready"])
            const = S["const_ready"]
            gps.memset(causal[:], 1.0).then_inc(const, 1)
            gps.memset(heads[:], 0.0).then_inc(const, 1)
            gps.memset(o_ext[:], NEG).then_inc(const, 1)
            for buffer in (decay, entry, entry_v):
                gps.memset(buffer[:], 0.0).then_inc(const, 1)
            gps.wait_ge(const, 6)
            gps.affine_select(out=causal[:], in_=causal[:], compare_op=ALU.is_ge, fill=0.0, base=0,
                              pattern=[[1, P]], channel_multiplier=-1).then_inc(const, 1)
            gps.wait_ge(const, 7)
            for j in range(4):
                gps.memset(heads[j * HD:(j + 1) * HD, j:j + 1], 1.0).then_inc(const, 1)
            gps.wait_ge(const, 11)

            def body(t, attend, recur, more, uses):
                c0 = (t - 1) * KT

                def restart_part(c):
                    gps.wait_ge(S["o_scan"], (c0 + c + 1) * TB)
                    gps.tensor_tensor(entry[:, c % 2, :, 1:], k_ext[:, c], o_ext[:, 0, :, 1:], ALU.subtract).then_inc(S["e_ready"], 1)

                def entry_values(c):
                    gps.wait_ge(S["entry_ready"], c0 + c + 1)
                    if c == 0:
                        gps.wait_ge(S["v_loaded"], (t - 1) * 16 + 16)
                    gps.tensor_tensor(entry_v[:, 0, :, 1:], entry[:, c % 2, :, 1:], vT[:, c], ALU.mult).then_inc(S["ev_ready"], 1)

                def parts(c):
                    gps.wait_ge(S["q_scan"], c0 + c + 1)
                    gps.wait_ge(S["new_ready"], c0 + c + 1)
                    gps.tensor_tensor(num(c), old[:, c % 2], num(c), ALU.mult).then_inc(S["pool_parts"], 1)
                    gps.tensor_tensor(den(c), old[:, c % 2], den(c), ALU.mult).then_inc(S["pool_parts"], 1)
                    gps.tensor_tensor(part[:, c % 2], new[:, c % 2], vT[:, c], ALU.mult).then_inc(S["pool_parts"], 1)

                def add_keys(c):
                    gps.wait_ge(S["z_parts"], c0 + c + 1)
                    gps.tensor_tensor(zT[:, c], zT[:, c], k_ext[:, c], ALU.add).then_inc(S["z_ready"], 1)

                for s in range(7):
                    if recur:
                        if s < 4:
                            restart_part(s)
                        if 1 <= s <= 4:
                            parts(s - 1)
                        if s < 4:
                            entry_values(s)
                        if s >= 3:
                            add_keys(s - 3)
                if attend:
                    ln3.power_step(gps, t)
                if recur:
                    ln4.power_step(gps, t - 1)
            rounds(gps, body)

        @block.scalar
        def _(act):
            act.sem_inc(S["zn_ready"], 1)
            for kt in range(KT):
                act.wait_ge(ring_full[kt % 2], kt // 2 + 1)
                act.activation(xT_h[:, kt], ring[kt % 2][:], ACT.Copy).then_inc(S["xT_high"], 1)
            def w_highs(c):
                if c < V:
                    act.wait_ge(S["w_fold"], 2 + 4 * (c + 1))
                else:
                    act.wait_ge(w_loaded[c % 2], 32)
                for kt in range(KT):
                    act.activation(w_h[:, c, kt], w_raw[c % 2][:, kt], ACT.Copy).then_inc(S["w_high"], 1)

            for c in (Q, K, V):
                w_highs(c)

            def v_evac(t, uses, i):
                uses.await_full(act, f"v{i}")
                if i == 0 and not (isinstance(t, int) and t == 0):
                    act.wait_ge(S["av_done"], t * KT)
                ins = act.activation(v[:, i, :, 0:HD], uses.bank(f"v{i}")[:].rearrange("p (h d) -> p h d", h=NH), ACT.Copy)
                ins.then_inc(S["v_ready"], 1)

            def qk_evac(t, uses, name, m, out, which, ready):
                uses.await_full(act, f"{name}{m}")
                if m == 0:
                    act.wait_ge(S["beta_ready"], 1)
                bank = uses.bank(f"{name}{m}")
                act.activation(out, bank[:], ACT.Identity, bias=beta[:, 0:1])
                ins = act.activation(squares[:, m % 2, which], bank[:], ACT.Square, bias=beta[:, 0:1])
                ins.then_inc(ready, 1)

            def first_evacs(t, uses):
                qk_evac(t, uses, "q", 0, qT[:, 0], 0, S["q_ready"])
                qk_evac(t, uses, "k", 0, kT[:, 0], 1, S["k_ready"])
                for i in range(TB):
                    v_evac(t, uses, i)

            first_evacs(0, FirstUses())
            w_highs(O)

            def body(t, attend, recur, more, uses):
                c0 = (t - 1) * KT

                def score_squares(m):
                    for j in range(4):
                        if j == 0:
                            act.wait_ge(S["s_done"], t * KT + m + 1)
                        act.activation(weights[:, j], ps_s[j][:], ACT.Square).then_inc(S["square_ready"], 1)

                def kx_evac(c):
                    uses.await_full(act, f"kx{c}")
                    act.wait_ge(S["z_ready"], c0 + 1)
                    if isinstance(t, int) and t == 1 and c == 0:
                        act.wait_ge(S["const_ready"], 11)
                    ins = act.activation(k_ext[:, c], uses.bank(f"kx{c}")[:].rearrange("p (b q) -> p b q", b=TB), ACT.Copy)
                    ins.then_inc(S["kx_ready"], 1)

                def exponentials(c):
                    act.wait_ge(S["a_ready"], c0 + c + 1)
                    act.activation(decay[:, c % 2, :, 1:], decay[:, c % 2, :, 1:], ACT.Exp).then_inc(S["decay_ready"], 1)
                    act.wait_ge(S["e_ready"], c0 + c + 2)
                    act.activation(entry[:, c % 2, :, 1:], entry[:, c % 2, :, 1:], ACT.Exp).then_inc(S["entry_ready"], 1)
                    act.wait_ge(S["d_ready"], c0 + c + 1)
                    act.activation(old[:, c % 2], new[:, c % 2], ACT.Relu).then_inc(S["old_ready"], 1)
                    act.activation(new[:, c % 2], new[:, c % 2], ACT.Relu, scale=-1.0).then_inc(S["old_ready"], 1)
                    act.wait_ge(S["old_ready"], (c0 + c) * 2 + 2)
                    act.activation(old[:, c % 2], old[:, c % 2], ACT.Exp, scale=-1.0)
                    act.activation(new[:, c % 2], new[:, c % 2], ACT.Exp, scale=-1.0).then_inc(S["new_ready"], 1)

                def inverse_start(c):
                    act.wait_ge(S["den_ready"], c0 + c + 1)
                    act.activation(inv(c), den(c), ACT.Ln).then_inc(S["ln_ready"], 1)
                    act.wait_ge(S["ln_ready"], c0 + c + 1)
                    act.activation(inv(c), inv(c), ACT.Exp, scale=-1.0).then_inc(S["inv_ready"], 1)

                def oT_highs(m):
                    uses.await_full(act, f"ot{m}")
                    act.activation(oT_h[:, m], uses.bank(f"ot{m}")[:], ACT.Copy).then_inc(S["oT_high"], 1)

                if recur:
                    for c in range(4):
                        kx_evac(c)
                def next_highs(kts):
                    for kt in kts:
                        uses.await_full(act, f"xt{kt}")
                        act.activation(xT_h[:, kt], uses.bank(f"xt{kt}")[:], ACT.Copy).then_inc(S["xT_high"], 1)

                for s in range(4):
                    if attend:
                        score_squares(s)
                        if more and s == 3:
                            next_highs((0, 1))
                        if s == 3:
                            oT_highs(2)
                        if s < 3:
                            qk_evac(t, uses, "q", s + 1, qT[:, (s + 1) % 2], 0, S["q_ready"])
                            qk_evac(t, uses, "k", s + 1, kT[:, 0], 1, S["k_ready"])
                    if recur:
                        exponentials(s)
                        if s >= 2:
                            inverse_start(s - 2)
                    if attend and 1 <= s < 3:
                        oT_highs(s - 1)
                if recur:
                    inverse_start(2)
                if more:
                    next_highs((2, 3))
                if attend:
                    oT_highs(3)
                if recur:
                    inverse_start(3)
                if more:
                    first_evacs(t + 1, uses)
                if recur:
                    act.wait_ge(S["x4_stored"], t * 16)
                    for i in range(TB):
                        uses.await_full(act, f"zn{i}")
                        ins = act.activation(x4[:, i], uses.bank(f"zn{i}")[:], ACT.Copy)
                        ins.then_inc(S["zn_ready"], 1)
            rounds(act, body)

        @block.vector
        def _(dve):
            dve.wait_ge(S["small_loaded"], 7 * 16)
            dve.tensor_reduce(beta_mean[:], beta_row[:], AX, ALU.add).then_inc(S["w_fold"], 1)
            dve.wait_ge(S["w_fold"], 1)
            dve.tensor_scalar(beta_mean[:], beta_mean[:], -1.0 / HD, None, ALU.mult).then_inc(S["w_fold"], 1)
            dve.wait_ge(S["w_fold"], 2)
            dve.tensor_tensor(beta[:], beta[:], beta_mean[:], ALU.add).then_inc(S["beta_ready"], 1)
            for c in (Q, K):
                wv = w_raw[c].rearrange("p k (h d) -> p (k h) d", d=HD)
                dve.wait_ge(w_loaded[c], 16)
                base = 2 + 4 * c
                dve.tensor_tensor(wv, wv, gamma[:].unsqueeze(1).broadcast_to([P, KT * NH, HD]), ALU.mult).then_inc(S["w_fold"], 1)
                dve.wait_ge(S["w_fold"], base + 1)
                dve.tensor_reduce(w_mean[:], wv, AX, ALU.add).then_inc(S["w_fold"], 1)
                dve.wait_ge(S["w_fold"], base + 2)
                dve.tensor_scalar(w_mean[:], w_mean[:], 1.0 / HD, None, ALU.mult).then_inc(S["w_fold"], 1)
                dve.wait_ge(S["w_fold"], base + 3)
                dve.tensor_tensor(wv, wv, w_mean[:].unsqueeze(2).broadcast_to([P, KT * NH, HD]), ALU.subtract).then_inc(S["w_fold"], 1)

            def w_lows(c):
                for kt in range(KT):
                    dve.wait_ge(S["w_high"], c * KT + kt + 1)
                    dve.tensor_tensor(w_l[:, c, kt], w_raw[c % 2][:, kt], w_h[:, c, kt].bitcast(F32), ALU.subtract).then_inc(S["w_split"], 1)

            for kt in range(KT):
                dve.wait_ge(S["xT_high"], kt + 1)
                ins = dve.tensor_tensor(xT_l[:, kt], ring[kt % 2][:], xT_h[:, kt].bitcast(F32), ALU.subtract)
                ins.then_inc(S["xT_split"], 1)
            for c in range(4):
                w_lows(c)
            dve.wait_ge(S["const_ready"], 11)
            dve.sem_inc(S["added"], TB)

            def head_norms(t, uses, m):
                uses.await_full(dve, f"su{m}")
                n = 2 * (t * KT + m)
                ins = dve.tensor_scalar(norms[:], uses.bank(f"su{m}")[:, 0:32].rearrange("p (b w h) -> p b w h", b=TB, w=2),
                                        HD * 1e-5, None, ALU.add)
                ins.then_inc(S["sums_ready"], 1)
                dve.wait_ge(S["sums_ready"], n + 1)
                dve.reciprocal(norms[:], norms[:]).then_inc(S["sums_ready"], 1)
                dve.wait_ge(S["sums_ready"], n + 2)
                dve.tensor_scalar(scaled_q[:, m % 2], norms[:, :, 0], float(HD), None, ALU.mult).then_inc(S["norms_ready"], 1)
                if m == 0:
                    dve.wait_ge(S["v_ready"], t * TB + TB)
                hs = slice(4 * m, 4 * m + 4)
                dve.tensor_tensor(v[:, :, hs, 0:HD], v[:, :, hs, 0:HD],
                                  norms[:, :, 1].unsqueeze(3).broadcast_to([P, TB, 4, HD]), ALU.mult)
                dve.tensor_copy(v[:, :, hs, HD], norms[:, :, 1]).then_inc(S["vs_ready"], 1)

            head_norms(0, FirstUses(), 0)

            def body(t, attend, recur, more, uses):
                c0 = (t - 1) * KT
                flat = lambda x: x.rearrange("p b e -> p (b e)")

                def start(c):
                    dve.wait_ge(S["kx_ready"], c0 + c + 1)
                    dve.wait_ge(S["e_ready"], c0 + c + 1)
                    if c or not (isinstance(t, int) and t == 1):
                        dve.wait_ge(S["d_ready"], c0 + c)
                        dve.wait_ge(S["a_ready"], c0 + c)
                    for b in range(TB):
                        dve.tensor_tensor_scan(o_ext[:, 0, b, 1:], wu[:, 0, c:c + 1].broadcast_to([P, P]), k_ext[:, c, b], NEG,
                                               ALU.add, ALU.max).then_inc(S["o_scan"], 1)
                    dve.wait_ge(S["o_scan"], (c0 + c + 1) * TB)
                    before, after = o_ext[:, 0, :, 0:P], o_ext[:, 0, :, 1:]
                    dve.scalar_tensor_tensor(decay[:, c % 2, :, 1:], before, wu[:, 0, c:c + 1], after, ALU.add, ALU.subtract).then_inc(S["a_ready"], 1)
                    dve.scalar_tensor_tensor(new[:, c % 2], k_ext[:, c], wu[:, 1, c:c + 1], before, ALU.add, ALU.subtract).then_inc(S["d_ready"], 1)

                def scans(c):
                    dve.wait_ge(S["ev_ready"], c0 + c + 1)
                    dve.wait_ge(S["decay_ready"], c0 + c + 1)
                    if c >= 2:
                        dve.wait_ge(S["z_parts"], c0 + c - 1)
                    dve.tensor_tensor_scan(flat(p_ext[:, c % 2]), flat(decay[:, c % 2]), flat(entry_v[:, 0]), 0.0, ALU.mult, ALU.add).then_inc(S["p_ready"], 1)
                    dve.tensor_tensor_scan(flat(q_ext[:, c % 2]), flat(decay[:, c % 2]), flat(entry[:, c % 2]), 0.0, ALU.mult, ALU.add).then_inc(S["q_scan"], 1)

                def fraction(c):
                    dve.wait_ge(S["pool_parts"], (c0 + c) * 3 + 4)
                    dve.tensor_tensor(num(c), num(c), part[:, c % 2], ALU.add).then_inc(S["num_ready"], 1)
                    dve.tensor_tensor(den(c), den(c), new[:, c % 2], ALU.add).then_inc(S["den_ready"], 1)

                def divide(c):
                    n = 2 * (c0 + c)
                    dve.wait_ge(S["inv_ready"], c0 + c + 1)
                    dve.tensor_tensor(den(c), den(c), inv(c), ALU.mult).then_inc(S["newton"], 1)
                    dve.wait_ge(S["newton"], n + 1)
                    dve.scalar_tensor_tensor(den(c), den(c), 2.0, inv(c), ALU.subtract, ALU.mult).then_inc(S["newton"], 1)
                    dve.wait_ge(S["newton"], n + 2)
                    dve.wait_ge(S["num_ready"], c0 + c + 1)
                    if c == 0:
                        dve.wait_ge(S["zn_ready"], c0 + 1)
                    dve.scalar_tensor_tensor(zT[:, c], num(c), -1.0, den(c), ALU.mult, ALU.mult).then_inc(S["z_parts"], 1)

                def masks(m):
                    for j in range(4):
                        dve.wait_ge(S["square_ready"], t * 16 + m * 4 + j + 1)
                        dve.tensor_tensor(weights[:, j].rearrange("p (b q) -> p b q", b=TB), weights[:, j].rearrange("p (b q) -> p b q", b=TB),
                                          causal[:].unsqueeze(1).broadcast_to([P, TB, P]), ALU.mult).then_inc(S["masked"], 1)

                def normalize(m):
                    n = 3 * (t * KT + m)
                    dve.wait_ge(S["av_done"], t * KT + m + 1)
                    dve.wait_ge(S["norms_ready"], t * KT + m + 1)
                    heads_of = ps_o[:, :, 0:8 * (HD + 1)].rearrange("p a (g e) -> p a g e", e=HD + 1)
                    rq = scaled_q[:, m % 2].rearrange("p (a b) h -> p a (b h)", a=2)
                    f = factor[:].rearrange("p (a g) -> p a g", a=2)
                    dve.tensor_tensor(f, heads_of[:, :, :, HD], rq, ALU.mult).then_inc(S["factor_ready"], 1)
                    dve.wait_ge(S["factor_ready"], n + 1)
                    dve.tensor_scalar(factor[:], factor[:], 1e-5, None, ALU.add).then_inc(S["factor_ready"], 1)
                    dve.wait_ge(S["factor_ready"], n + 2)
                    dve.reciprocal(factor[:], factor[:]).then_inc(S["factor_ready"], 1)
                    dve.wait_ge(S["factor_ready"], n + 3)
                    dve.tensor_tensor(f, f, rq, ALU.mult).then_inc(S["o_ready"], 1)
                    dve.wait_ge(S["o_ready"], 3 * (t * KT + m) + 1)
                    for a in range(2):
                        dve.tensor_tensor(o_nat[:, m % 2, 2 * a:2 * a + 2].rearrange("p b (h d) -> p b h d", h=4),
                                          heads_of[:, a, :, 0:HD].rearrange("p (b h) d -> p b h d", b=2),
                                          f[:, a].rearrange("p (b h) -> p b h", b=2).unsqueeze(3).broadcast_to([P, 2, 4, HD]),
                                          ALU.mult).then_inc(S["o_ready"], 1)

                def oT_lows(m):
                    dve.wait_ge(S["oT_high"], t * KT + m + 1)
                    ins = dve.tensor_tensor(oT_l[:, m], uses.bank(f"ot{m}")[:], oT_h[:, m].bitcast(F32), ALU.subtract)
                    ins.then_inc(S["oT_split"], 1)

                def next_lows(kts):
                    for kt in kts:
                        dve.wait_ge(S["xT_high"], (t + 1) * KT + kt + 1)
                        ins = dve.tensor_tensor(xT_l[:, kt], uses.bank(f"xt{kt}")[:], xT_h[:, kt].bitcast(F32), ALU.subtract)
                        ins.then_inc(S["xT_split"], 1)

                for s in range(4):
                    if recur:
                        if s >= 2:
                            fraction(s - 2)
                        start(s)
                        if s == 3:
                            divide(0)
                        if s:
                            scans(s - 1)
                    if attend:
                        masks(s)
                        if more and s == 3:
                            next_lows((0, 1))
                        if s == 3:
                            oT_lows(2)
                    if recur and s == 3:
                        fraction(2)
                    if attend:
                        normalize(s)
                        if s < 3:
                            head_norms(t, uses, s + 1)
                        if 1 <= s < 3:
                            oT_lows(s - 1)
                if more:
                    next_lows((2, 3))
                if recur:
                    divide(1)
                    scans(3)
                if attend:
                    oT_lows(3)
                if recur:
                    fraction(3)
                    divide(2)
                    divide(3)
                if attend:
                    dve.wait_ge(S["res_loaded"], t * 16 + 16)
                    for i in range(TB):
                        dve.wait_ge(S["out_done"], t * TB + i + 1)
                        dve.tensor_tensor(res[:, i], res[:, i], ps_s[i][:], ALU.add).then_inc(S["added"], 1)
                    dve.wait_ge(S["added"], t * TB + 2 * TB)
                    ln3.statistics(dve, lambda i: res[:, i], t)
                    dve.wait_ge(ln3.rstd_ready, t + 1)
                    for i in range(TB):
                        ln3.apply(dve, x3[:, i], res[:, i], i).then_inc(S["x3_ready"], 1)
                if more:
                    head_norms(t + 1, uses, 0)
                if recur:
                    dve.wait_ge(S["zn_ready"], t * TB + 1)
                    ln4.statistics(dve, lambda i: x4[:, i], t - 1)
                    dve.wait_ge(ln4.rstd_ready, t)
                    for i in range(TB):
                        ln4.apply(dve, x4[:, i], x4[:, i], i).then_inc(S["x4_ready"], 1)
            rounds(dve, body)

        @block.tensor
        def _(pe):
            pe.wait_ge(S["ident_ready"], 2)
            pe.wait_ge(S["const_ready"], 11)
            pe.wait_ge(S["xs_loaded"], 16)
            for kt in range(KT):
                if kt >= 2:
                    pe.wait_ge(S["xT_split"], kt - 1)
                for i in range(TB):
                    last = nc.tensor.transpose(ring[kt % 2][:, i * P:(i + 1) * P], xs[:, i, kt * P:(kt + 1) * P], ident[:])
                last.then_inc(ring_full[kt % 2], 1)

            def values(t, uses, i):
                uses.claim(pe, f"v{i}")
                for kt in range(KT):
                    part = slice(i * P, (i + 1) * P)
                    last = split3(nc, uses.bank(f"v{i}")[:], xT_h[:, kt, part], xT_l[:, kt, part], w_h[:, V, kt], w_l[:, V, kt], kt == 0, kt == KT - 1)
                uses.filled(last, f"v{i}")

            def columns(uses, name, c, m):
                uses.claim(pe, f"{name}{m}")
                for kt in range(KT):
                    part = slice(m * P, (m + 1) * P)
                    last = split3(nc, uses.bank(f"{name}{m}")[:], w_h[:, c, kt, part], w_l[:, c, kt, part], xT_h[:, kt], xT_l[:, kt], kt == 0, kt == KT - 1)
                uses.filled(last, f"{name}{m}")

            def sums(t, uses, m):
                pe.wait_ge(S["q_ready"], t * KT + m + 1)
                pe.wait_ge(S["k_ready"], t * KT + m + 1)
                uses.claim(pe, f"su{m}")
                for i in range(TB):
                    for which in range(2):
                        at = i * 8 + which * 4
                        last = nc.tensor.matmul(uses.bank(f"su{m}")[:, at:at + 4], squares[:, m % 2, which, i * P:(i + 1) * P],
                                                heads[:], start=True, stop=True)
                uses.filled(last, f"su{m}")

            def first_products(t, uses):
                pe.wait_ge(S["xT_split"], t * KT + KT)
                pe.wait_ge(S["w_split"], (Q + 1) * KT)
                columns(uses, "q", Q, 0)
                pe.wait_ge(S["w_split"], (K + 1) * KT)
                columns(uses, "k", K, 0)
                pe.wait_ge(S["w_split"], (V + 1) * KT)
                for i in range(TB):
                    values(t, uses, i)
                sums(t, uses, 0)

            first_products(0, FirstUses())

            def body(t, attend, recur, more, uses):
                c0 = (t - 1) * KT

                def keys_transposed(c):
                    if c == 0:
                        pe.wait_ge(S["x3_ready"], (t - 1) * TB + TB)
                    uses.claim(pe, f"kx{c}")
                    for i in range(TB):
                        last = nc.tensor.transpose(uses.bank(f"kx{c}")[:, i * P:(i + 1) * P], x3[:, i, c * P:(c + 1) * P], ident[:])
                    uses.filled(last, f"kx{c}")

                def scores(m):
                    pe.wait_ge(S["q_ready"], t * KT + m + 1)
                    pe.wait_ge(S["k_ready"], t * KT + m + 1)
                    if m:
                        pe.wait_ge(S["square_ready"], (t * KT + m) * 4)
                    else:
                        pe.wait_ge(S["added"], t * TB + TB)
                    for b in range(TB):
                        for j in range(4):
                            rows, part = slice(j * HD, (j + 1) * HD), slice(b * P, (b + 1) * P)
                            last = nc.tensor.matmul(ps_s[j][:, part], kT[rows, 0, part], qT[rows, m % 2, part], start=True, stop=True)
                    last.then_inc(S["s_done"], 1)

                def next_transposes(uses, kts):
                    for kt in kts:
                        uses.claim(pe, f"xt{kt}")
                        for i in range(TB):
                            last = nc.tensor.transpose(uses.bank(f"xt{kt}")[:, i * P:(i + 1) * P], xs[:, i, kt * P:(kt + 1) * P], ident[:])
                        uses.filled(last, f"xt{kt}")

                def weighted(m):
                    pe.wait_ge(S["vs_ready"], t * KT + m + 1)
                    if not (isinstance(t, int) and t == 0 and m == 0):
                        pe.wait_ge(S["o_ready"], 3 * (t * KT + m))
                    pe.wait_ge(S["masked"], 4 * (t * KT + m) + 4)
                    for b in range(TB):
                        for j in range(4):
                            at = ((b % 2) * 4 + j) * (HD + 1)
                            last = nc.tensor.matmul(ps_o[:, b // 2, at:at + HD + 1], weights[:, j, b * P:(b + 1) * P],
                                                    v[:, b, 4 * m + j], start=True, stop=True)
                    last.then_inc(S["av_done"], 1)

                def o_transposes(m):
                    pe.wait_ge(S["o_ready"], 3 * (t * KT + m) + 3)
                    uses.claim(pe, f"ot{m}")
                    for i in range(TB):
                        last = nc.tensor.transpose(uses.bank(f"ot{m}")[:, i * P:(i + 1) * P], o_nat[:, m % 2, i], ident[:])
                    uses.filled(last, f"ot{m}")

                def out_proj(m):
                    pe.wait_ge(S["oT_split"], t * KT + m + 1)
                    if m == 0:
                        pe.wait_ge(S["w_split"], (O + 1) * KT)
                        pe.wait_ge(S["square_ready"], (t + 1) * 16)
                    for i in range(TB):
                        part = slice(i * P, (i + 1) * P)
                        last = split3(nc, ps_s[i][:], oT_h[:, m, part], oT_l[:, m, part], w_h[:, O, m], w_l[:, O, m], m == 0, m == KT - 1)
                        if m == KT - 1:
                            last.then_inc(S["out_done"], 1)

                if recur:
                    for c in range(KT):
                        keys_transposed(c)
                if attend:
                    for m in range(4):
                        scores(m)
                        if m < 3:
                            columns(uses, "q", Q, m + 1)
                            columns(uses, "k", K, m + 1)
                        if m == 3:
                            if more:
                                pe.wait_ge(S["xs_loaded"], t * 16 + 32)
                                next_transposes(uses, (0, 1))
                            out_proj(0)
                            o_transposes(2)
                        weighted(m)
                        if m < 3:
                            sums(t, uses, m + 1)
                        if 1 <= m < 3:
                            o_transposes(m - 1)
                    if more:
                        next_transposes(uses, (2, 3))
                    out_proj(1)
                    out_proj(2)
                    o_transposes(3)
                    out_proj(3)
                    if more:
                        first_products(t + 1, uses)
                if recur:
                    for i in range(TB):
                        if i == 0:
                            pe.wait_ge(S["z_ready"], c0 + KT + 1)
                        uses.claim(pe, f"zn{i}")
                        for c in range(KT):
                            last = nc.tensor.transpose(uses.bank(f"zn{i}")[:, c * P:(c + 1) * P], zT[:, c, i], ident[:])
                        uses.filled(last, f"zn{i}")
            rounds(pe, body)


ROUND = 12582912.0


def ternary_ffn(nc, w_dram, x4_dram, out_dram):
    with ExitStack() as ctx:
        sb, sem, clear_semaphores = stage_memory(nc, ctx)
        NCH, RAW = 12, 4
        w_raw = sb("f_w_raw", [P, RAW, 4, D])
        gate_up = sb("f_gate_up", [P, 4, 2, KT, D], BF16)
        down = sb("f_down", [P, 4, 4, D], F32R)
        xs, res, magnitude = sb("f_xs", [P, TB, D]), sb("f_res", [P, TB, D]), sb("f_magnitude", [P, TB, D])
        xqT = sb("f_xqT", [P, 2, KT, TOK], BF16)
        scale_row = sb("f_scale_row", [P, 2, TOK])
        g_scaled, silu, prod = sb("f_g_scaled", [P, 2, TOK]), sb("f_silu", [P, 2, TOK]), sb("f_prod", [P, 2, TOK])
        prod_h, prod_l = sb("f_prod_h", [P, 4, TOK], F32R), sb("f_prod_l", [P, 4, TOK], F32R)
        top, scale, scale_inv, y_scale = sb("f_top", [P, TB]), sb("f_scale", [P, TB]), sb("f_scale_inv", [P, TB]), sb("f_y_scale", [P, TB])
        scale_cols = sb("f_scale_cols", [P, TB, P])
        ident, ones, unround = sb("f_ident", [P, P]), sb("f_ones", [P, P]), sb("f_unround", [P, 1])
        ln_in, ln_out = LayerNorm(nc, sb, sem, "f_ln_in", 1e-8), LayerNorm(nc, sb, sem, "f_ln_out", 1e-5)
        ps_y = [ctx.enter_context(nc.psum_tensor(f"f_ps_y{i}", [P, D], F32)) for i in range(TB)]
        ps_g = ctx.enter_context(nc.psum_tensor("f_ps_g", [P, TOK], F32))
        ps_u = [ctx.enter_context(nc.psum_tensor(f"f_ps_u{i}", [P, TOK], F32)) for i in range(2)]
        ps_t = ctx.enter_context(nc.psum_tensor("f_ps_t", [P, TOK], F32))
        w_loaded = [sem(f"f_w_loaded{i}") for i in range(RAW)]
        xs_loaded, res_loaded, out_stored = sem("f_xs_loaded"), sem("f_res_loaded"), sem("f_out_stored")
        ident_ready, const_ready, w_signs = sem("f_ident_ready"), sem("f_const_ready"), sem("f_w_signs")
        xn_ready, magnitude_ready, quant, xq_ready = sem("f_xn_ready"), sem("f_magnitude_ready"), sem("f_quant"), sem("f_xq_ready")
        turned, evacuated = sem("f_turned"), sem("f_evacuated")
        g_done, u_done, y_done = sem("f_g_done"), sem("f_u_done"), sem("f_y_done")
        g_ready, silu_ready, prod_ready, prod_high, prod_split = (
            sem("f_g_ready"), sem("f_silu_ready"), sem("f_prod_ready"), sem("f_prod_high"), sem("f_prod_split"))
        added, y_scale_ready, out_ready = sem("f_added"), sem("f_y_scale_ready"), sem("f_out_ready")
        QUANT = 4 + TB
        TURNS = KT + 1
        TURN_AT = 11
        out_view = out_dram.rearrange("(t b) p d -> t p b d", b=TB)
        parity = lambda t: t % 2 if isinstance(t, int) else t & 1
        ctx.callback(clear_semaphores)
        block = ctx.enter_context(nc.Block())

        @block.sync
        def _(sp):
            sp.dma_start(xs[:], x4_dram[0]).then_inc(xs_loaded, 16)
            for n in range(NCH):
                if n == RAW:
                    sp.wait_ge(turned, KT)
                    sp.dma_start(xs[:], x4_dram[1]).then_inc(xs_loaded, 16)
                if n >= RAW:
                    sp.wait_ge(w_signs, n - RAW + 1)
                sp.dma_start(w_raw[:, n % RAW], w_dram[n]).then_inc(w_loaded[n % RAW], 16)

            def body(t, first, more):
                if more and not first:
                    sp.wait_ge(turned, t * TURNS + KT)
                    sp.dma_start(xs[:], x4_dram[t + 1]).then_inc(xs_loaded, 16)
                if not first:
                    sp.wait_ge(out_ready, t * TB)
                    sp.dma_start(out_view[t - 1], res[:]).then_inc(out_stored, 16)
                    sp.wait_ge(out_stored, t * 16)
                sp.dma_start(res[:], x4_dram[t]).then_inc(res_loaded, 16)
            groups(sp, body)
            sp.wait_ge(out_ready, TG * TB)
            sp.dma_start(out_view[TG - 1], res[:]).then_inc(out_stored, 16)
            sp.wait_ge(out_stored, TG * 16)

        @block.gpsimd
        def _(gps):
            ln_in.constants(gps)
            ln_out.constants(gps)
            gps.memset(ones[:], 1.0).then_inc(const_ready, 1)
            gps.memset(unround[:], -ROUND).then_inc(const_ready, 1)
            make_identity(nc, gps, ident, ident_ready)
            ln_in.power_step(gps, 0)

            def low(n, i):
                gps.wait_ge(prod_high, n + 1)
                gps.tensor_tensor(prod_l[:, i % 4], prod[:, i % 2], prod_h[:, i % 4].bitcast(F32), ALU.subtract).then_inc(prod_split, 1)

            def body(t, first, more):
                for i in range(NB):
                    if not (first and i == 0):
                        low(t * NB + i - 1, i - 1)
                    if not first and i == 4:
                        ln_out.power_step(gps, t - 1)
                    if more and i == 5:
                        ln_in.power_step(gps, t + 1)
            groups(gps, body)
            low(TG * NB - 1, NB - 1)
            ln_out.power_step(gps, TG - 1)

        @block.scalar
        def _(act):
            def signs(n):
                act.wait_ge(w_loaded[n % RAW], (n // RAW + 1) * 16)
                out = down[:, n // 3] if n % 3 == 2 else gate_up[:, n // 3, n % 3]
                act.activation(out, w_raw[:, n % RAW], ACT.Sign).then_inc(w_signs, 1)

            def magnitudes(t):
                act.wait_ge(xn_ready, (t + 1) * TB)
                act.activation(magnitude[:], xs[:], ACT.Abs).then_inc(magnitude_ready, 1)

            def evacuate(t, k):
                act.wait_ge(turned, t * TURNS + k + 1)
                if k < KT:
                    ins = act.activation(xqT[:, parity(t), k], ps_t[:], ACT.Identity, bias=unround[:, 0:1])
                else:
                    ins = act.activation(scale_row[:, parity(t)], ps_t[:], ACT.Copy)
                ins.then_inc(evacuated, 1)

            def high(n, i, full):
                act.wait_ge(prod_ready, n + 1)
                if full:
                    act.wait_ge(y_done, (n - 3) * TB)
                act.activation(prod_h[:, i % 4], prod[:, i % 2], ACT.Copy).then_inc(prod_high, 1)

            act.wait_ge(const_ready, 2)
            magnitudes(0)
            for n in range(3):
                signs(n)
            for k in range(TURNS):
                evacuate(0, k)

            def body(t, first, more):
                for i in range(NB):
                    n = t * NB + i
                    act.wait_ge(g_ready, n + 1)
                    if not first or i >= 2:
                        act.wait_ge(prod_ready, n - 1)
                    act.activation(silu[:, i % 2], g_scaled[:, i % 2], ACT.Silu).then_inc(silu_ready, 1)
                    if not (first and i == 0):
                        high(n - 1, i - 1, not first or i >= 5)
                    if first and i < 12 and i % 4 < 3:
                        signs(3 + 3 * (i // 4) + i % 4)
                    if more:
                        if i == 7:
                            magnitudes(t + 1)
                        if i >= TURN_AT:
                            evacuate(t + 1, i - TURN_AT)
            groups(act, body)
            high(TG * NB - 1, NB - 1, True)

        @block.vector
        def _(dve):
            def normalise(t):
                dve.wait_ge(ln_in.rstd_ready, t + 1)
                for i in range(TB):
                    ln_in.apply(dve, xs[:, i], xs[:, i], i).then_inc(xn_ready, 1)

            def scales(t):
                n = t * QUANT
                dve.wait_ge(magnitude_ready, t + 1)
                dve.tensor_reduce(top[:], magnitude[:], AX, ALU.max).then_inc(quant, 1)
                dve.wait_ge(quant, n + 1)
                dve.reciprocal(scale[:], top[:]).then_inc(quant, 1)
                dve.wait_ge(quant, n + 2)
                dve.tensor_scalar(scale[:], scale[:], 127.0, None, ALU.mult).then_inc(quant, 1)
                dve.tensor_scalar(scale_inv[:], top[:], 1.0 / 127.0, None, ALU.mult).then_inc(quant, 1)
                dve.wait_ge(quant, n + 4)
                for i in range(TB):
                    if i == 0 and not (isinstance(t, int) and t == 0):
                        dve.wait_ge(turned, t * TURNS)
                    dve.tensor_scalar(scale_cols[:, i], ones[:], scale_inv[:, i:i + 1], None, ALU.mult).then_inc(quant, 1)

            def quantise(t):
                for i in range(TB):
                    dve.tensor_scalar(xs[:, i], xs[:, i], scale[:, i:i + 1], ROUND, ALU.mult, ALU.add).then_inc(xq_ready, 1)

            def clip(t):
                dve.wait_ge(xq_ready, t * 2 * TB + TB)
                for i in range(TB):
                    dve.tensor_scalar(xs[:, i], xs[:, i], ROUND + 127.0, ROUND - 128.0, ALU.min, ALU.max).then_inc(xq_ready, 1)

            def product(n, i):
                dve.wait_ge(u_done, n + 1)
                dve.wait_ge(silu_ready, n + 1)
                if not isinstance(n, int) or n >= 2:
                    dve.wait_ge(prod_split, n - 1)
                dve.tensor_tensor(prod[:, i % 2], silu[:, i % 2], ps_u[i % 2][:], ALU.mult).then_inc(prod_ready, 1)

            def residual(t):
                dve.wait_ge(res_loaded, t * 16 + 16)
                dve.wait_ge(y_scale_ready, t + 1)
                for i in range(TB):
                    dve.wait_ge(y_done, (t * NB + NB - 1) * TB + i + 1)
                    dve.scalar_tensor_tensor(res[:, i], ps_y[i][:], y_scale[:, i:i + 1], res[:, i], ALU.mult, ALU.add).then_inc(added, 1)

            def out_statistics(t):
                dve.wait_ge(added, t * TB + TB)
                ln_out.statistics(dve, lambda i: res[:, i], t)

            def out_apply(t):
                dve.wait_ge(ln_out.rstd_ready, t + 1)
                for i in range(TB):
                    ln_out.apply(dve, res[:, i], res[:, i], i).then_inc(out_ready, 1)

            dve.wait_ge(xs_loaded, 16)
            ln_in.statistics(dve, lambda i: xs[:, i], 0)
            normalise(0)
            dve.wait_ge(const_ready, 2)
            scales(0)
            quantise(0)
            clip(0)

            def body(t, first, more):
                for i in range(NB):
                    n = t * NB + i
                    if not first and i == 2:
                        residual(t - 1)
                    if i == 0:
                        dve.wait_ge(evacuated, t * TURNS + TURNS)
                    dve.wait_ge(g_done, n + 1)
                    if not first or i >= 2:
                        dve.wait_ge(silu_ready, n - 1)
                    dve.tensor_tensor(g_scaled[:, i % 2], ps_g[:], scale_row[:, parity(t)], ALU.mult).then_inc(g_ready, 1)
                    if not (first and i == 0):
                        product(n - 1, i - 1)
                    if i == 3:
                        if not first:
                            dve.wait_ge(added, t * TB)
                        dve.tensor_copy(y_scale[:], scale_inv[:]).then_inc(y_scale_ready, 1)
                        if not first:
                            out_statistics(t - 1)
                    if not first and i == 5:
                        out_apply(t - 1)
                    if more:
                        if i == 4:
                            dve.wait_ge(xs_loaded, t * 16 + 32)
                            ln_in.statistics(dve, lambda i: xs[:, i], t + 1)
                        if i == 6:
                            normalise(t + 1)
                        if i == 8:
                            dve.wait_ge(y_scale_ready, t + 1)
                            scales(t + 1)
                        if i == 9:
                            quantise(t + 1)
                        if i == 10:
                            clip(t + 1)
            groups(dve, body)
            product(TG * NB - 1, NB - 1)
            residual(TG - 1)
            out_statistics(TG - 1)
            out_apply(TG - 1)

        @block.tensor
        def _(pe):
            def turn(t, k):
                if k == 0:
                    pe.wait_ge(xq_ready, (t + 1) * 2 * TB)
                if not (isinstance(t, int) and t == 0 and k == 0):
                    pe.wait_ge(evacuated, t * TURNS + k)
                if k == KT:
                    pe.wait_ge(quant, (t + 1) * QUANT)
                for i in range(TB):
                    source = xs[:, i, k * P:(k + 1) * P] if k < KT else scale_cols[:, i]
                    done = nc.tensor.transpose(ps_t[:, i * P:(i + 1) * P], source, ident[:])
                done.then_inc(turned, 1)

            def hidden(t, i):
                n = t * NB + i
                part = slice((i % 4) * P, (i % 4 + 1) * P)
                if not isinstance(t, int) or n >= 1:
                    pe.wait_ge(g_ready, n)
                for kt in range(KT):
                    if i == 0 and kt == 0:
                        pe.wait_ge(evacuated, t * TURNS + KT)
                    if kt == 0:
                        pe.wait_ge(w_signs, 3 * (i // 4) + 1)
                    done = nc.tensor.matmul(ps_g[:], gate_up[:, i // 4, 0, kt, part], xqT[:, parity(t), kt], start=kt == 0, stop=kt == KT - 1)
                done.then_inc(g_done, 1)
                if not isinstance(t, int) or n >= 2:
                    pe.wait_ge(prod_ready, n - 1)
                for kt in range(KT):
                    if kt == 0:
                        pe.wait_ge(w_signs, 3 * (i // 4) + 2)
                    done = nc.tensor.matmul(ps_u[i % 2][:], gate_up[:, i // 4, 1, kt, part], xqT[:, parity(t), kt], start=kt == 0, stop=kt == KT - 1)
                done.then_inc(u_done, 1)

            def back(t, i, first):
                pe.wait_ge(prod_split, t * NB + i + 1)
                pe.wait_ge(w_signs, 3 * (i // 4) + 3)
                for b in range(TB):
                    if i == 0 and not first:
                        pe.wait_ge(added, (t - 1) * TB + b + 1)
                    part = slice(b * P, (b + 1) * P)
                    nc.tensor.matmul(ps_y[b][:], prod_h[:, i % 4, part], down[:, i // 4, i % 4], start=i == 0, stop=False)
                    nc.tensor.matmul(ps_y[b][:], prod_l[:, i % 4, part], down[:, i // 4, i % 4], start=False, stop=i == NB - 1).then_inc(y_done, 1)

            pe.wait_ge(ident_ready, 2)
            for k in range(TURNS):
                turn(0, k)

            def body(t, first, more):
                for i in range(NB):
                    hidden(t, i)
                    if more and i >= TURN_AT:
                        turn(t + 1, i - TURN_AT)
                    if i >= 2:
                        back(t, i - 2, first)
                    elif not first:
                        back(t - 1, NB - 2 + i, False)
            groups(pe, body)
            back(TG - 1, NB - 2, False)
            back(TG - 1, NB - 1, False)


def decoder(nc, x_dram, xT_dram, w_attn_dram, ctxT_dram, w_cross_dram, bg_dram, w_ffn_dram, wr_dram, br_dram,
            w_powered_dram, gamma_dram, beta_dram, wu_dram, w_ternary_dram, out_dram):
    x1_dram, x2_dram, x4_dram = (nc.dram_tensor(name, (TG, P, TB, D), F32, kind="Internal").ap()
                                 for name in ("x1_dram", "x2_dram", "x4_dram"))
    with nc.sbuf_tensor("acc", [P, TG * TB, D], F32) as acc:
        self_attention(nc, x_dram, xT_dram, w_attn_dram, acc)
        linear_cross_attention(nc, ctxT_dram, w_cross_dram, bg_dram, acc, x1_dram)
    blockwise_ffn(nc, w_ffn_dram, wr_dram, br_dram, x1_dram, x2_dram)
    powered_attention_and_wkv(nc, x2_dram, ctxT_dram, w_powered_dram, gamma_dram, beta_dram, wu_dram, x4_dram)
    ternary_ffn(nc, w_ternary_dram, x4_dram, out_dram)


def kernel(**inputs):
    import numpy as np
    import concourse.bacc as bacc
    from concourse.bass_utils import run_bass_kernel_spmd

    a = {name: np.asarray(value) for name, value in inputs.items()}

    def rows_by_input(w):
        return w.reshape(-1, 4, 128).transpose(2, 1, 0)

    def columns_of(x):
        return x.reshape(4, 512, 4, 128).transpose(0, 3, 2, 1)

    def hidden_rows(w):
        return w.reshape(4, 512, 4, 128).transpose(0, 3, 2, 1)

    def hidden_columns(w):
        return w.reshape(512, 4, 4, 128).transpose(1, 3, 2, 0)

    qkv = a["L0_attn_w_qkv"].reshape(3, 4, 512, 4, 128)[[2, 0, 1]].transpose(1, 0, 4, 3, 2).reshape(4, 3, 128, 2048)
    w_out = hidden_columns(a["L0_attn_w_out"]).reshape(4, 1, 128, 2048)
    wk, wv = a["L0_xattn_Wkv"][:512], a["L0_xattn_Wkv"][512:]
    arrays = {
        "x": a["x"].transpose(1, 0, 2),
        "xT": columns_of(a["x"]),
        "w_attn": np.concatenate([qkv, w_out], 1),
        "ctxT": columns_of(a["ctx_2048"]),
        "w_cross": np.stack([rows_by_input(w) for w in (wk, wv, a["L0_xattn_Wq"], a["L0_xattn_Wg"], a["L0_xattn_Wo"])]),
        "bg": a["L0_xattn_bg"].reshape(4, 128).T,
        "w_ffn": np.stack([hidden_rows(a["L0_ffn_W1"]), hidden_columns(a["L0_ffn_W2"])], 1).reshape(8, 128, 4, 512),
        "wr": rows_by_input(a["L0_ffn_Wr"]),
        "br": a["L0_ffn_br"].reshape(16, 1),
        "w_powered": np.stack([rows_by_input(a["L1_attn_W" + c]) for c in "qkvo"]),
        "gamma": a["L1_attn_gamma"],
        "beta": a["L1_attn_beta"],
        "wu": np.stack([a["L1_xattn_w"], a["L1_xattn_u"]]).reshape(2, 4, 128).transpose(2, 0, 1),
        "w_ternary": np.stack([hidden_rows(a["L1_ffn_W_g"]), hidden_rows(a["L1_ffn_W_u"]), hidden_columns(a["L1_ffn_W_d"])],
                              1).reshape(12, 128, 4, 512),
    }
    nc = bacc.Bacc("TRN2", target_bir_lowering=False, num_devices=1)
    feed, args = {}, []
    for name, value in arrays.items():
        value = np.ascontiguousarray(value)
        feed[f"in_{name}_dram"] = value
        args.append(nc.dram_tensor(f"in_{name}_dram", value.shape, mybir.dt.from_np(value.dtype), kind="ExternalInput").ap())
    args.append(nc.dram_tensor("out_0_dram", (16, 128, 512), F32, kind="ExternalOutput").ap())
    decoder(nc, *args)
    result = run_bass_kernel_spmd(nc, [feed], core_ids=[0])
    return result.results[0]["out_0_dram"]
```
